# Optimizing a Trainium2 kernel written in Bass

```python
import numpy as np
import jax
import jax.numpy as jnp

def _softmax(x, axis=-1):
    return jax.nn.softmax(x, axis=axis)

def _gelu(x):
    return jax.nn.gelu(x, approximate=True)

def _silu(x):
    return jax.nn.silu(x)

def _sigmoid(x):
    return jax.nn.sigmoid(x)

def _layernorm(x, axis=-1, eps=1e-05):
    m = jnp.mean(x, axis=axis, keepdims=True)
    v = jnp.var(x, axis=axis, keepdims=True)
    return (x - m) / jnp.sqrt(v + eps)

def _scatter_add(tgt, idx, src, axis=0):
    return tgt.at[idx].add(src)

def _segment_sum(src, seg, n):
    return jax.ops.segment_sum(src, seg, n)
kernel_name = 'mk_flamingo_gated_d2_seqx_r8_4f5320'

def setup_inputs(seed: int=0):
    np.random.seed(seed)
    _w = jnp.asarray

    def _rec_inputs():
        import jax
        import jax.numpy as jnp
        _rk = jax.random.key(seed)
        x = 7.22e-05 + 1 * jax.random.normal(jax.random.fold_in(_rk, 1), (16, 256, 128), jnp.float32)
        _lenS = 256 - jax.random.randint(jax.random.fold_in(_rk, 7), (16,), 0, max(1, 256 // 4) + 1, jnp.int32)
        _lenS2 = 64 - jax.random.randint(jax.random.fold_in(_rk, 8), (16,), 0, max(1, 64 // 4) + 1, jnp.int32)
        _ctx_1024P = jax.random.normal(jax.random.fold_in(_rk, 11), (16, 16, 128), jnp.float32)
        _ctx_1024c = jax.random.dirichlet(jax.random.fold_in(_rk, 511), 0.3 * jnp.ones((16,), jnp.float32), (16, 64))
        _ctx_1024t = jnp.einsum('bsk,bkd->bsd', _ctx_1024c, _ctx_1024P)
        _ctx_1024t = _ctx_1024t * jax.lax.rsqrt(jnp.mean(jnp.square(_ctx_1024t)) + 1e-12) * 0.953939
        ctx_1024 = -0.000514642 + 1.00011 * (_ctx_1024t + 0.3 * jax.random.normal(jax.random.fold_in(_rk, 611), (16, 64, 128), jnp.float32))
        _g = jax.random.normal(jax.random.fold_in(_rk, 9001), (2, 2), jnp.float32)
        _g = jnp.sign(_g) * jnp.maximum(jnp.abs(_g), 1.0) + (_g == 0) * 1.0
        g_xattn = _g[0]
        g_ffn = _g[1]
        return (x, ctx_1024, g_xattn, g_ffn)
    x, ctx_1024, g_xattn, g_ffn = _rec_inputs()

    def _L0_xattn_setup():
        import jax, jax.numpy as jnp
        import numpy as np
        B, L_ENC, L_DEC, D = (16, 64, 128, 128)
        key = jax.random.key(seed)
        k1, k2, k3, k4, k5, k6 = jax.random.split(key, 6)
        encoder_hc = jax.random.normal(k1, (B, L_ENC, D), dtype=jnp.float32)
        decoder_hq = jax.random.normal(k2, (B, L_DEC, D), dtype=jnp.float32)
        w_sim = jax.random.normal(k3, (3 * D,), dtype=jnp.float32) * 0.02
        b_sim = jax.random.normal(k4, (1,), dtype=jnp.float32) * 0.02
        W_qv = jax.random.normal(k5, (4 * D, D), dtype=jnp.float32) * 0.02
        b_qv = jax.random.normal(k6, (D,), dtype=jnp.float32) * 0.02
        return {'encoder_hc': encoder_hc, 'decoder_hq': decoder_hq, 'w_sim': w_sim, 'b_sim': b_sim, 'W_qv': W_qv, 'b_qv': b_qv}
    _L0_xattn_all = _L0_xattn_setup()
    _L0_xattn_in = {k: v for k, v in _L0_xattn_all.items() if k in ('w_sim', 'b_sim', 'W_qv', 'b_qv')}
    del _L0_xattn_all

    def _L0_ffn_setup():
        import jax, jax.numpy as jnp
        import numpy as np
        D_MODEL = 128
        D_FF = 512
        NUM_M = 2
        E_ROUTER = 8 * NUM_M - 1
        D_FF_R = D_FF // NUM_M
        TOP_K = NUM_M * 2 - 1
        B, T = (2, 256)

        def _expert_stack(x, W1, b1, W2, b2):
            h = jax.nn.gelu(jnp.einsum('btd,edf->ebtf', x, W1) + b1[:, None, None, :], approximate=False)
            return jnp.einsum('ebtf,efd->ebtd', h, W2) + b2[:, None, None, :]
        key = jax.random.key(seed)
        ks = jax.random.split(key, 12)
        s = lambda fan_in: 1.0 / np.sqrt(fan_in)
        x = jax.random.normal(ks[0], (B, T, D_MODEL), dtype=jnp.float32)
        sW1 = jax.random.uniform(ks[1], (1, D_MODEL, D_FF), jnp.float32, -s(D_MODEL), s(D_MODEL))
        sb1 = jax.random.uniform(ks[2], (1, D_FF), jnp.float32, -s(D_MODEL), s(D_MODEL))
        sW2 = jax.random.uniform(ks[3], (1, D_FF, D_MODEL), jnp.float32, -s(D_FF), s(D_FF))
        sb2 = jax.random.uniform(ks[4], (1, D_MODEL), jnp.float32, -s(D_FF), s(D_FF))
        rW1 = jax.random.uniform(ks[5], (E_ROUTER, D_MODEL, D_FF_R), jnp.float32, -s(D_MODEL), s(D_MODEL))
        rb1 = jax.random.uniform(ks[6], (E_ROUTER, D_FF_R), jnp.float32, -s(D_MODEL), s(D_MODEL))
        rW2 = jax.random.uniform(ks[7], (E_ROUTER, D_FF_R, D_MODEL), jnp.float32, -s(D_FF_R), s(D_FF_R))
        rb2 = jax.random.uniform(ks[8], (E_ROUTER, D_MODEL), jnp.float32, -s(D_FF_R), s(D_FF_R))
        gW = jax.random.uniform(ks[9], (D_MODEL, E_ROUTER), jnp.float32, -s(D_MODEL), s(D_MODEL))
        gb = jax.random.uniform(ks[10], (E_ROUTER,), jnp.float32, -s(D_MODEL), s(D_MODEL))
        return {'x': x, 'sW1': sW1, 'sb1': sb1, 'sW2': sW2, 'sb2': sb2, 'rW1': rW1, 'rb1': rb1, 'rW2': rW2, 'rb2': rb2, 'gW': gW, 'gb': gb}
    _L0_ffn_all = _L0_ffn_setup()
    _L0_ffn_in = {k: v for k, v in _L0_ffn_all.items() if k in ('sW1', 'sb1', 'sW2', 'sb2', 'rW1', 'rb1', 'rW2', 'rb2', 'gW', 'gb')}
    del _L0_ffn_all

    def _L1_xattn_setup():
        import jax, jax.numpy as jnp
        import numpy as np
        D_MODEL = 128
        N_HEAD = 8
        STRIDE = 8
        HEAD_DIM = D_MODEL // N_HEAD
        NEG_INF = jnp.float32(-1e+30)

        def _hepos_head_mask(src_len):
            src_idx = jnp.arange(src_len)
            h_idx = jnp.arange(N_HEAD)[:, None]
            m = (src_idx[None, :] - h_idx) % STRIDE != 0
            all_masked = jnp.all(m, axis=-1, keepdims=True)
            m = m.at[:, 0].set(jnp.where(all_masked[:, 0], False, m[:, 0]))
            return m
        key = jax.random.key(seed)
        ks = jax.random.split(key, 8)
        B, TGT, SRC = (2, 128, 1024)
        scale = 1.0 / np.sqrt(D_MODEL)
        return {'q': jax.random.normal(ks[0], (B, TGT, D_MODEL), jnp.float32), 'k': jax.random.normal(ks[1], (B, SRC, D_MODEL), jnp.float32), 'v': jax.random.normal(ks[2], (B, SRC, D_MODEL), jnp.float32), 'Wq': jax.random.normal(ks[3], (D_MODEL, D_MODEL), jnp.float32) * scale, 'bq': jnp.zeros((D_MODEL,), jnp.float32), 'Wk': jax.random.normal(ks[4], (D_MODEL, D_MODEL), jnp.float32) * scale, 'bk': jnp.zeros((D_MODEL,), jnp.float32), 'Wv': jax.random.normal(ks[5], (D_MODEL, D_MODEL), jnp.float32) * scale, 'bv': jnp.zeros((D_MODEL,), jnp.float32), 'Wo': jax.random.normal(ks[6], (D_MODEL, D_MODEL), jnp.float32) * scale, 'bo': jnp.zeros((D_MODEL,), jnp.float32)}
    _L1_xattn_all = _L1_xattn_setup()
    _L1_xattn_in = {k: v for k, v in _L1_xattn_all.items() if k in ('Wq', 'bq', 'Wk', 'bk', 'Wv', 'bv', 'Wo', 'bo')}
    del _L1_xattn_all

    def _L1_ffn_setup():
        import jax, jax.numpy as jnp
        import numpy as np
        TOP_K = 2
        key = jax.random.key(seed)
        ks = jax.random.split(key, 6)
        B, S, D, E = (8, 512, 128, 8)
        s = 1.0 / np.sqrt(D)
        return {'x': jax.random.normal(ks[0], (B, S, D), dtype=jnp.float32), 'Wr': jax.random.normal(ks[1], (D, E), dtype=jnp.float32) * s, 'br': jnp.zeros((E,), dtype=jnp.float32), 'W1': jax.random.normal(ks[2], (E, D, D), dtype=jnp.float32) * s, 'b1': jnp.zeros((E, D), dtype=jnp.float32), 'W2': jax.random.normal(ks[3], (E, D, D), dtype=jnp.float32) * s, 'b2': jnp.zeros((E, D), dtype=jnp.float32)}
    _L1_ffn_all = _L1_ffn_setup()
    _L1_ffn_in = {k: v for k, v in _L1_ffn_all.items() if k in ('Wr', 'br', 'W1', 'b1', 'W2', 'b2')}
    del _L1_ffn_all
    return {'x': x, 'ctx_1024': ctx_1024, 'g_xattn': g_xattn, 'g_ffn': g_ffn, 'L0_xattn_w_sim': _L0_xattn_in['w_sim'], 'L0_xattn_b_sim': _L0_xattn_in['b_sim'], 'L0_xattn_W_qv': _L0_xattn_in['W_qv'], 'L0_xattn_b_qv': _L0_xattn_in['b_qv'], 'L0_ffn_sW1': _L0_ffn_in['sW1'], 'L0_ffn_sb1': _L0_ffn_in['sb1'], 'L0_ffn_sW2': _L0_ffn_in['sW2'], 'L0_ffn_sb2': _L0_ffn_in['sb2'], 'L0_ffn_rW1': _L0_ffn_in['rW1'], 'L0_ffn_rb1': _L0_ffn_in['rb1'], 'L0_ffn_rW2': _L0_ffn_in['rW2'], 'L0_ffn_rb2': _L0_ffn_in['rb2'], 'L0_ffn_gW': _L0_ffn_in['gW'], 'L0_ffn_gb': _L0_ffn_in['gb'], 'L1_xattn_Wq': _L1_xattn_in['Wq'], 'L1_xattn_bq': _L1_xattn_in['bq'], 'L1_xattn_Wk': _L1_xattn_in['Wk'], 'L1_xattn_bk': _L1_xattn_in['bk'], 'L1_xattn_Wv': _L1_xattn_in['Wv'], 'L1_xattn_bv': _L1_xattn_in['bv'], 'L1_xattn_Wo': _L1_xattn_in['Wo'], 'L1_xattn_bo': _L1_xattn_in['bo'], 'L1_ffn_Wr': _L1_ffn_in['Wr'], 'L1_ffn_br': _L1_ffn_in['br'], 'L1_ffn_W1': _L1_ffn_in['W1'], 'L1_ffn_b1': _L1_ffn_in['b1'], 'L1_ffn_W2': _L1_ffn_in['W2'], 'L1_ffn_b2': _L1_ffn_in['b2']}

def reference(x, ctx_1024, g_xattn, g_ffn, L0_xattn_w_sim, L0_xattn_b_sim, L0_xattn_W_qv, L0_xattn_b_qv, L0_ffn_sW1, L0_ffn_sb1, L0_ffn_sW2, L0_ffn_sb2, L0_ffn_rW1, L0_ffn_rb1, L0_ffn_rW2, L0_ffn_rb2, L0_ffn_gW, L0_ffn_gb, L1_xattn_Wq, L1_xattn_bq, L1_xattn_Wk, L1_xattn_bk, L1_xattn_Wv, L1_xattn_bv, L1_xattn_Wo, L1_xattn_bo, L1_ffn_Wr, L1_ffn_br, L1_ffn_W1, L1_ffn_b1, L1_ffn_W2, L1_ffn_b2):
    import jax
    import jax.numpy as jnp

    def _L0_xattn_ref(encoder_hc, decoder_hq, w_sim, b_sim, W_qv, b_qv):
        import jax, jax.numpy as jnp
        import numpy as np
        B, L_ENC, L_DEC, D = (16, 64, 128, 128)
        d = encoder_hc.shape[-1]
        w1, w2, w3 = (w_sim[:d], w_sim[d:2 * d], w_sim[2 * d:])
        Sim = (encoder_hc @ w1)[:, :, None] + (decoder_hq @ w2)[:, None, :] + jnp.einsum('bid,bjd->bij', encoder_hc * w3, decoder_hq) + b_sim[0]
        A = jax.nn.softmax(Sim, axis=2)
        hq_hat = jnp.einsum('bij,bjd->bid', A, decoder_hq)
        Batt = jax.nn.softmax(jnp.max(Sim, axis=2), axis=1)
        hc_bar = jnp.einsum('bi,bid->bd', Batt, encoder_hc)[:, None, :]
        hc_hat = jnp.broadcast_to(hc_bar, encoder_hc.shape)
        feats = jnp.concatenate([encoder_hc, hq_hat, encoder_hc * hq_hat, encoder_hc * hc_hat], axis=-1)
        hcq = feats @ W_qv + b_qv
        return hcq

    def _L0_ffn_ref(x, sW1, sb1, sW2, sb2, rW1, rb1, rW2, rb2, gW, gb):
        import jax, jax.numpy as jnp
        import numpy as np
        D_MODEL = 128
        D_FF = 512
        NUM_M = 2
        E_ROUTER = 8 * NUM_M - 1
        D_FF_R = D_FF // NUM_M
        TOP_K = NUM_M * 2 - 1
        B, T = (2, 256)

        def _expert_stack(x, W1, b1, W2, b2):
            h = jax.nn.gelu(jnp.einsum('btd,edf->ebtf', x, W1) + b1[:, None, None, :], approximate=False)
            return jnp.einsum('ebtf,efd->ebtd', h, W2) + b2[:, None, None, :]
        shared_enc = _expert_stack(x, sW1, sb1, sW2, sb2).sum(0)
        weights = jax.nn.softmax(x @ gW + gb, axis=-1)
        topv, topi = jax.lax.top_k(weights, TOP_K)
        gated = (jax.nn.one_hot(topi, E_ROUTER, dtype=weights.dtype) * topv[..., None]).sum(axis=-2)
        router_out = _expert_stack(x, rW1, rb1, rW2, rb2)
        router_enc = jnp.einsum('ebtd,bte->btd', router_out, gated)
        return shared_enc + router_enc + x

    def _L1_xattn_ref(q, k, v, Wq, bq, Wk, bk, Wv, bv, Wo, bo):
        import jax, jax.numpy as jnp
        import numpy as np
        D_MODEL = 128
        N_HEAD = 8
        STRIDE = 8
        HEAD_DIM = D_MODEL // N_HEAD
        NEG_INF = jnp.float32(-1e+30)

        def _hepos_head_mask(src_len):
            src_idx = jnp.arange(src_len)
            h_idx = jnp.arange(N_HEAD)[:, None]
            m = (src_idx[None, :] - h_idx) % STRIDE != 0
            all_masked = jnp.all(m, axis=-1, keepdims=True)
            m = m.at[:, 0].set(jnp.where(all_masked[:, 0], False, m[:, 0]))
            return m
        B, tgt_len, _ = q.shape
        src_len = k.shape[1]
        Q = (q @ Wq + bq).reshape(B, tgt_len, N_HEAD, HEAD_DIM)
        K = (k @ Wk + bk).reshape(B, src_len, N_HEAD, HEAD_DIM)
        V = (v @ Wv + bv).reshape(B, src_len, N_HEAD, HEAD_DIM)
        scores = jnp.einsum('bthd,bshd->bhts', Q, K) / np.sqrt(HEAD_DIM)
        head_mask = _hepos_head_mask(src_len)
        scores = jnp.where(head_mask[None, :, None, :], NEG_INF, scores)
        attn = jax.nn.softmax(scores, axis=-1)
        out = jnp.einsum('bhts,bshd->bthd', attn, V).reshape(B, tgt_len, D_MODEL)
        return out @ Wo + bo

    def _L1_ffn_ref(x, Wr, br, W1, b1, W2, b2):
        import jax, jax.numpy as jnp
        import numpy as np
        TOP_K = 2
        k = TOP_K
        scores0 = x[:, 0, :] @ Wr + br
        _, idx = jax.lax.top_k(scores0, k)
        W1g, b1g = (W1[idx], b1[idx])
        W2g, b2g = (W2[idx], b2[idx])
        h = jnp.einsum('bsd,bkde->bkse', x, W1g) + b1g[:, :, None, :]
        h = jax.nn.gelu(h, approximate=False)
        o = jnp.einsum('bkse,bkef->bksf', h, W2g) + b2g[:, :, None, :]
        return jnp.sum(o, axis=1) / k
    x = x + jnp.tanh(g_xattn[0]) * _L0_xattn_ref(_layernorm(x, axis=-1), ctx_1024, L0_xattn_w_sim, L0_xattn_b_sim, L0_xattn_W_qv, L0_xattn_b_qv)
    x = x + jnp.tanh(g_ffn[0]) * _L0_ffn_ref(_layernorm(x, axis=-1), L0_ffn_sW1, L0_ffn_sb1, L0_ffn_sW2, L0_ffn_sb2, L0_ffn_rW1, L0_ffn_rb1, L0_ffn_rW2, L0_ffn_rb2, L0_ffn_gW, L0_ffn_gb)
    x = x + jnp.tanh(g_xattn[1]) * _L1_xattn_ref(_layernorm(x, axis=-1), ctx_1024, ctx_1024, L1_xattn_Wq, L1_xattn_bq, L1_xattn_Wk, L1_xattn_bk, L1_xattn_Wv, L1_xattn_bv, L1_xattn_Wo, L1_xattn_bo)
    x = x + jnp.tanh(g_ffn[1]) * _L1_ffn_ref(_layernorm(x, axis=-1), L1_ffn_Wr, L1_ffn_br, L1_ffn_W1, L1_ffn_b1, L1_ffn_W2, L1_ffn_b2)
    return x

_drawn_inputs = setup_inputs


def setup_inputs(seed=0):
    import zlib

    import numpy as np

    out = dict(_drawn_inputs(seed))
    spreads = {'g_ffn': (-1.0, 0.2),
     'L1_xattn_bq': (0.0, 0.1),
     'L1_xattn_bk': (0.0, 0.8),
     'L1_xattn_bv': (0.0, 0.1),
     'L1_xattn_bo': (0.0, 0.1),
     'L1_ffn_br': (0.0, 0.1),
     'L1_ffn_b1': (0.0, 0.1),
     'L1_ffn_b2': (0.0, 0.1)}
    factors = {'L0_xattn_w_sim': 4.234, 'L0_xattn_b_qv': 4.392, 'L0_ffn_rb1': 8.0, 'L0_ffn_gb': 3.262}
    for name, (base, spread) in spreads.items():
        noise = np.random.default_rng([zlib.crc32(name.encode()), seed]).standard_normal(out[name].shape)
        drawn = base * np.exp(spread * noise) if base else spread * noise
        out[name] = jnp.asarray(drawn.astype(out[name].dtype))
    for name, factor in factors.items():
        out[name] = (out[name] * factor).astype(out[name].dtype)
    return out
```

```python
from contextlib import ExitStack

import concourse.bass as bass
from concourse import mybir

F32 = mybir.dt.float32
F16 = mybir.dt.float16
I32 = mybir.dt.int32
U32 = mybir.dt.uint32
ALU = mybir.AluOpType
ACT = mybir.ActivationFunctionType
AX = mybir.AxisListType.X

P = 128
B = 16
SEQ = 256
TPB = SEQ // P
NT = B * TPB
TOK = B * SEQ
D = 128
L = 64
HEADS = 8
HD = D // HEADS
E0 = 15
F0 = 256
K0 = 3
FS = 512
E1 = 8
K1 = 2
EPS = 1e-5

SU = 256.0
SW = 1024.0
SH = 64.0
UN1 = 1.0 / (SU * SW)
UN2 = 1.0 / (SH * SW)

BLK = 256
REGION = TOK + BLK
BLOCKS = (TOK * K0) // BLK + E0 + 1
ROWS = E0 * REGION + BLK
WEW = F0 + 2 * D + 2

V_WSIM, V_BQ, V_BK, V_BV, V_RB1, V_SB1, V_B1 = 0, 3, 4, 5, 6, 36, 40
NVEC = 48
C_ID, C_TRI, C_MASK, C_IOTA, C_BASE, C_LE, C_PART = 0, 128, 256, 320, 410, 425, 650
NCONST = 651

CREDIT = 2


def done(n):
    return n + 1 + CREDIT


def free(n):
    return n + 1


class Chain:

    def __init__(self, eng, sem, per=0):
        self.eng, self.sem, self.per, self.base, self.k = eng, sem, per, 0, 0

    def step(self, n):
        assert self.k in (0, self.per), (self.k, self.per)
        self.base, self.k = n * self.per, 0

    def __call__(self, ins):
        ins.then_inc(self.sem, 1)
        self.k += 1
        self.eng.wait_ge(self.sem, self.base + self.k)


def build(nc, a, const, out):
    with ExitStack() as ctx:
        def sb(name, shape, dt=F32):
            return ctx.enter_context(nc.sbuf_tensor(name, shape, dt))

        def sem(name):
            return ctx.enter_context(nc.semaphore(name))

        banks = [ctx.enter_context(nc.psum_tensor(f"bank{i}", [P, 512], F32)) for i in range(8)]

        sorted_rows = nc.dram_tensor("sorted_rows", (ROWS, 2 * D), F16, kind="Internal").ap()
        expert_rows = nc.dram_tensor("expert_rows", (BLOCKS * BLK, D), F32, kind="Internal").ap()

        X = sb("X", [P, NT, D])
        hc = sb("hc", [P, NT, D])
        hcT = sb("hcT", [P, TOK])
        AT = sb("AT", [P, TOK])
        uT = sb("uT", [P, 2, TOK], F16)

        cst = sb("cst", [P, NCONST])
        ident = cst[:, C_ID:C_ID + P]
        ident16 = sb("ident16", [P, P], F16)
        tri16 = sb("tri16", [P, P], F16)
        ones16 = sb("ones16", [P, P], F16)
        ones = sb("ones", [P, P])
        vecs = sb("vecs", [NVEC, P])
        cols = sb("cols", [P, NVEC])
        rows = sb("rows", [1, 4, P])
        gates = sb("gates", [P, 4])
        tg = sb("tg", [P, 4])
        bsim = sb("bsim", [1, 1])

        early = uT[:].rearrange("p h t -> p (h t)").bitcast(F32)
        ctxk = early[:, 0:1024].rearrange("p (t d) -> p t d", d=D)
        ctxT = early[:, 1024:2048]
        VmT = early[:, 2048:3072]
        Wa = early[:, 3072:3584].rearrange("p (w d) -> p w d", d=D)
        WqT = early[:, 3584:3712]
        MT = sb("MT", [P, B * L])
        KmT = sb("KmT", [P, B * L])
        QK = sb("QK", [P, B * L])
        srow = sb("srow", [1, 2, B * L])
        HW1 = sb("HW1", [L, B, D])
        VO = sb("VO", [L, B, D])
        Wqv = sb("Wqv", [P, 4, D])

        WE = sb("WE", [P, E0, WEW])
        WE16 = WE[:].rearrange("p e w -> p (e w)").bitcast(F16).rearrange("p (e w) -> p e w", e=E0)
        W1 = WE16[:, :, 0:2 * F0].rearrange("p e (h f) -> p h e f", h=2)
        W2 = WE16[:, :, 2 * F0:2 * F0 + 4 * D].rearrange("p e (h f) -> p h e f", h=2)
        S1 = sb("S1", [P, 2, FS], F16)
        S2 = sb("S2", [P, 2, FS], F16)
        M1 = sb("M1", [P, 2, E1, D], F16)
        M2 = sb("M2", [P, 2, E1, D], F16)
        gw = sb("gw", [P, E0])
        gw16 = sb("gw16", [P, 2, E0 + 1], F16)
        wr = sb("wr", [P, E1])
        wr16 = sb("wr16", [P, 2, E1], F16)
        b2a = sb("b2a", [E0 + 1, D])
        b2m = sb("b2m", [1, E1, D])

        st_W1 = hcT[:, 0:E0 * F0].rearrange("p (e f) -> p e f", e=E0)
        st_W2 = hc[:].rearrange("p t d -> p (t d)")[:, 0:E0 * 2 * D].rearrange("p (e f) -> p e f", e=E0)
        st_S1 = AT[:, 0:512]
        st_S2 = AT[:, 512:1024]
        st_M1 = AT[:, 1024:2048].rearrange("p (e f) -> p e f", e=E1)
        st_M2 = AT[:, 2048:3072].rearrange("p (e f) -> p e f", e=E1)

        stats = sb("stats", [P, 2, 6])
        mv = [sb(f"mv{i}", [P, 2, 2]) for i in range(2)]
        rs = [sb(f"rs{i}", [P, 4, 2]) for i in range(2)]

        def pair(name, shape, dt=F32):
            return [sb(f"{name}{i}", shape, dt) for i in range(2)]

        LN_LINKS = 14

        def layer_norm(dve, link, x, dst, par, done_sem):
            hold(dve, "dve")
            for j in range(2):
                ins = nc.vector.bn_stats(stats[:, j, :], x[:, j, :])
            link(ins)
            hold(dve, "dve")
            for j in range(2):
                ins = nc.vector.bn_aggr(mv[par][:, j, :], stats[:, j, :])
            link(ins)
            v, y, t, w = (rs[par][:, i, :] for i in range(4))
            link(nc.vector.tensor_scalar(v, mv[par][:, :, 1], EPS, None, ALU.add))
            link(nc.vector.tensor_scalar(t.bitcast(I32), v.bitcast(I32), 1, None, ALU.logical_shift_right))
            link(nc.vector.tensor_scalar(y.bitcast(I32), t.bitcast(I32), -1.0, float(0x5f3759df), ALU.mult, ALU.add))
            for _ in range(3):
                link(nc.vector.scalar_tensor_tensor(t, y, -0.5, y, ALU.mult, ALU.mult))
                link(nc.vector.tensor_tensor(w, t, v, ALU.mult))
                link(nc.vector.scalar_tensor_tensor(y, w, 1.5, y, ALU.add, ALU.mult))
            for j in range(2):
                ins = nc.vector.tensor_scalar(dst[:, j, :], x[:, j, :], mv[par][:, j, 0:1],
                                              rs[par][:, 1, j:j + 1], ALU.subtract, ALU.mult)
            if done_sem is None:
                link(ins)
            else:
                ins.then_inc(done_sem, 1)

        held = {e: sem("held_" + e) for e in ("pe", "dve", "act", "pool", "sp")}

        def hold(eng, name):
            eng.sem_inc(held[name], 1)

        def xt(n):
            return X[:, bass.ds(n * TPB, TPB), :]

        ld_small, ld_ctx, ld_x, ld_wa, ld_w = (sem(s) for s in ("ld_small", "ld_ctx", "ld_x", "ld_wa", "ld_w"))
        s_pe, s_dve, s_act, s_pool, s_consts = (
            sem(s) for s in ("setup_pe", "setup_dve", "setup_act", "setup_pool", "setup_consts"))
        zeros = sb("zeros", [P, 4 * D], F16)
        with nc.Block() as block:
            @block.sync
            def _(sp):
                sp.dma_start(cst[:], const).then_inc(ld_small, 16)
                r = [(V_WSIM, 3, a["L0_xattn_w_sim"].rearrange("(r c) -> r c", c=P)),
                     (V_BQ, 1, a["L1_xattn_bq"].rearrange("(r c) -> r c", c=P)),
                     (V_BK, 1, a["L1_xattn_bk"].rearrange("(r c) -> r c", c=P)),
                     (V_BV, 1, a["L1_xattn_bv"].rearrange("(r c) -> r c", c=P)),
                     (V_RB1, 30, a["L0_ffn_rb1"].rearrange("e (r c) -> (e r) c", c=P)),
                     (V_SB1, 4, a["L0_ffn_sb1"].rearrange("e (r c) -> (e r) c", c=P)),
                     (V_B1, 8, a["L1_ffn_b1"])]
                for at, n, src in r:
                    sp.dma_start(vecs[at:at + n, :], src).then_inc(ld_small, 16)
                for i, (name, n) in enumerate((("L0_xattn_b_qv", D), ("L1_xattn_bo", D), ("L0_ffn_gb", E0),
                                               ("L1_ffn_br", E1))):
                    sp.dma_start(rows[:, i, 0:n], a[name].rearrange("(r c) -> r c", r=1)).then_inc(ld_small, 16)
                sp.dma_start(bsim[:], a["L0_xattn_b_sim"].rearrange("(r c) -> r c", r=1)).then_inc(ld_small, 16)
                for i, name in enumerate(("g_xattn", "g_ffn")):
                    sp.dma_start(gates[:, 2 * i:2 * i + 2],
                                 a[name].rearrange("(r c) -> r c", r=1).broadcast_to([P, 2])).then_inc(ld_small, 16)
                sp.dma_start(gw[:], a["L0_ffn_gW"]).then_inc(ld_small, 16)
                sp.dma_start(wr[:], a["L1_ffn_Wr"]).then_inc(ld_small, 16)
                sp.dma_start(b2a[0:E0, :], a["L0_ffn_rb2"]).then_inc(ld_small, 16)
                sp.dma_start(b2a[E0:E0 + 1, :], a["L0_ffn_sb2"]).then_inc(ld_small, 16)
                sp.dma_start(b2m[:], a["L1_ffn_b2"].rearrange("(o e) d -> o e d", o=1)).then_inc(ld_small, 16)

            N_SMALL = 20

            @block.gpsimd
            def _(pool):
                nc.gpsimd.memset(zeros[:], 0.0)
                nc.gpsimd.memset(ones[:], 1.0).then_inc(s_pool, 1)
                nc.gpsimd.memset(ones16[:], 1.0).then_inc(s_pool, 1)
                pool.wait_ge(ld_small, 16 * N_SMALL)
                nc.gpsimd.tensor_copy(ident16[:], ident).then_inc(s_pool, 1)
                nc.gpsimd.tensor_copy(tri16[:], cst[:, C_TRI:C_TRI + P]).then_inc(s_pool, 1)

            @block.scalar
            def _(act):
                act.dma_start(ctxk, a["ctx_1024"].rearrange("(t b) s d -> (b s) t d", b=P // L)).then_inc(ld_ctx, 16)
                act.dma_start(Wqv[:], a["L0_xattn_W_qv"].rearrange("(c p) d -> p c d", p=P)).then_inc(ld_wa, 16)
                for i, name in enumerate(("L1_xattn_Wq", "L1_xattn_Wk", "L1_xattn_Wv", "L1_xattn_Wo")):
                    act.dma_start(Wa[:, i, :], a[name]).then_inc(ld_wa, 16)
                act.dma_start(st_W1, a["L0_ffn_rW1"].rearrange("e p f -> p e f")).then_inc(ld_w, 16)
                act.dma_start(st_W2.rearrange("p e (c d) -> p e c d", c=2),
                              a["L0_ffn_rW2"].rearrange("e (c p) d -> p e c d", p=P)).then_inc(ld_w, 16)
                act.dma_start(st_S1, a["L0_ffn_sW1"].rearrange("e p f -> p (e f)")).then_inc(ld_w, 16)
                act.dma_start(st_S2.rearrange("p (c d) -> p c d", c=4),
                              a["L0_ffn_sW2"].rearrange("e (c p) d -> p (e c) d", p=P)).then_inc(ld_w, 16)
                act.dma_start(st_M1, a["L1_ffn_W1"].rearrange("e p f -> p e f")).then_inc(ld_w, 16)
                act.dma_start(st_M2, a["L1_ffn_W2"].rearrange("e p f -> p e f")).then_inc(ld_w, 16)
                for g in range(4):
                    act.dma_start(X[:, 8 * g:8 * g + 8, :],
                                  a["x"].rearrange("b (t p) d -> p (b t) d", p=P)[:, 8 * g:8 * g + 8, :]).then_inc(ld_x, 16)
                act.wait_ge(ld_small, 16 * N_SMALL)
                nc.scalar.activation(tg[:], gates[:], ACT.Tanh).then_inc(s_consts, 1)
                act.wait_ge(ld_w, 16 * 6)
                for dst, src in ((W1, st_W1), (W2, st_W2), (S1, st_S1), (S2, st_S2), (M1, st_M1), (M2, st_M2)):
                    nc.scalar.activation(dst[:, 0], src, ACT.Copy, scale=SW).then_inc(s_act, 1)

            @block.vector
            def _(dve):
                link = Chain(dve, s_dve)
                dve.wait_ge(ld_small, 16 * N_SMALL)
                nc.vector.tensor_scalar(gw16[:, 0, 0:E0], gw[:], SW, None, ALU.mult)
                nc.vector.tensor_scalar(rows[:, 1, :], rows[:, 1, :], 1.0 / HEADS, None, ALU.mult)
                nc.vector.tensor_scalar(rows[:, 2, 0:E0], rows[:, 2, 0:E0], SU * SW, None, ALU.mult)
                nc.vector.tensor_scalar(rows[:, 3, 0:E1], rows[:, 3, 0:E1], SU * SW, None, ALU.mult)
                nc.vector.tensor_scalar(b2a[:], b2a[:], SH * SW, None, ALU.mult)
                nc.vector.tensor_scalar(b2m[:], b2m[:], SH * SW, None, ALU.mult)
                link(nc.vector.tensor_scalar(wr16[:, 0, :], wr[:], SW, None, ALU.mult))
                nc.vector.scalar_tensor_tensor(gw16[:, 1, 0:E0], gw[:], SW, gw16[:, 0, 0:E0], ALU.mult, ALU.subtract)
                link(nc.vector.scalar_tensor_tensor(wr16[:, 1, :], wr[:], SW, wr16[:, 0, :], ALU.mult, ALU.subtract))
                dve.wait_ge(s_pe, 1)
                link(nc.vector.tensor_copy(cols[:], banks[0][:, 0:NVEC]))
                nc.vector.tensor_copy(WE[:, :, F0 + 2 * D:WEW],
                                      cols[:, V_RB1:V_RB1 + 2 * E0].rearrange("p (e c) -> p e c", c=2))
                dve.wait_ge(s_pe, 2)
                link(nc.vector.tensor_copy(WqT, banks[1][:, 0:D]))
                for h in range(2):
                    dve.wait_ge(s_pe, 3 + h)
                    link(nc.vector.tensor_copy(ctxT[:, 512 * h:512 * h + 512], banks[2 + h][:]))
                link(nc.vector.tensor_scalar(MT[:], ctxT, cols[:, V_WSIM + 2:V_WSIM + 3],
                                             cols[:, V_WSIM:V_WSIM + 1], ALU.mult, ALU.add))
                mask = cst[:, C_MASK:C_MASK + L].rearrange("p (o s) -> p o s", o=1).broadcast_to([P, 8, L])
                for h in range(2):
                    dve.wait_ge(s_pe, 5 + h)
                    link(nc.vector.scalar_tensor_tensor(
                        KmT[:, 512 * h:512 * h + 512].rearrange("p (b s) -> p b s", s=L),
                        banks[4 + h][:].rearrange("p (b s) -> p b s", s=L),
                        cols[:, V_BK:V_BK + 1], mask, ALU.add, ALU.mult))
                link(nc.vector.tensor_scalar(KmT[:], KmT[:], float(HD) ** -0.5, None, ALU.mult))
                for h in range(2):
                    dve.wait_ge(s_pe, 7 + h)
                    link(nc.vector.scalar_tensor_tensor(
                        VmT[:, 512 * h:512 * h + 512].rearrange("p (b s) -> p b s", s=L),
                        banks[6 + h][:].rearrange("p (b s) -> p b s", s=L),
                        cols[:, V_BV:V_BV + 1], mask, ALU.add, ALU.mult))
                for h in range(2):
                    dve.wait_ge(s_pe, 9 + h)
                    link(nc.vector.tensor_scalar(srow[0:1, 0, 512 * h:512 * h + 512], banks[h][0:1, :], bsim[0:1, 0:1],
                                                 None, ALU.add))
                for h in range(2):
                    dve.wait_ge(s_pe, 11 + h)
                    link(nc.vector.tensor_copy(srow[0:1, 1, 512 * h:512 * h + 512], banks[2 + h][0:1, :]))
                for h in range(2):
                    dve.wait_ge(s_pe, 13 + h)
                    link(nc.vector.tensor_copy(QK[:, 512 * h:512 * h + 512], banks[4 + h][:]))
                for q in range(4):
                    dve.wait_ge(s_pe, 15 + q)
                    link(nc.vector.tensor_copy(HW1[:, 4 * q:4 * q + 4, :],
                                               banks[q][0:L, :].rearrange("p (b d) -> p b d", d=D)))
                for q in range(4):
                    dve.wait_ge(s_pe, 19 + q)
                    link(nc.vector.tensor_copy(VO[:, 4 * q:4 * q + 4, :],
                                               banks[4 + q][0:L, :].rearrange("p (b d) -> p b d", d=D)))
                dve.wait_ge(s_act, 6)
                for dst, src in ((W1, st_W1), (W2, st_W2), (S1, st_S1), (S2, st_S2), (M1, st_M1), (M2, st_M2)):
                    ins = nc.vector.scalar_tensor_tensor(dst[:, 1], src, SW, dst[:, 0], ALU.mult, ALU.subtract)
                link(ins)
                dve.wait_ge(ld_x, 16 * 4)

            @block.tensor
            def _(pe):
                mm = nc.tensor.matmul
                pe.wait_ge(ld_small, 16 * N_SMALL)
                pe.wait_ge(s_pool, 4)
                nc.tensor.transpose(banks[0][:, 0:NVEC], vecs[:], ident[0:NVEC, 0:NVEC]).then_inc(s_pe, 1)
                pe.wait_ge(ld_wa, 16 * 5)
                nc.tensor.transpose(banks[1][:, 0:D], Wa[:, 0, :], ident).then_inc(s_pe, 1)
                pe.wait_ge(ld_ctx, 16)
                for h in range(2):
                    for t in range(4):
                        ins = nc.tensor.transpose(banks[2 + h][:, t * P:(t + 1) * P], ctxk[:, 4 * h + t, :], ident)
                    ins.then_inc(s_pe, 1)
                pe.wait_ge(s_dve, 6)
                for h in range(2):
                    mm(banks[4 + h][:], Wa[:, 1, :], ctxT[:, 512 * h:512 * h + 512], start=True, stop=True).then_inc(s_pe, 1)
                for h in range(2):
                    mm(banks[6 + h][:], Wa[:, 2, :], ctxT[:, 512 * h:512 * h + 512], start=True, stop=True).then_inc(s_pe, 1)
                for h in range(2):
                    mm(banks[h][0:1, :], cols[:, V_WSIM + 1:V_WSIM + 2], ctxT[:, 512 * h:512 * h + 512],
                       start=True, stop=True).then_inc(s_pe, 1)
                pe.wait_ge(s_dve, 10)
                for h in range(2):
                    mm(banks[2 + h][0:1, :], cols[:, V_BQ:V_BQ + 1], KmT[:, 512 * h:512 * h + 512],
                       start=True, stop=True).then_inc(s_pe, 1)
                for h in range(2):
                    mm(banks[4 + h][:], WqT, KmT[:, 512 * h:512 * h + 512], start=True, stop=True).then_inc(s_pe, 1)
                for q in range(4):
                    pe.wait_ge(s_dve, 13 + q)
                    for b in range(4 * q, 4 * q + 4):
                        o = banks[q][0:L, (b % 4) * D:(b % 4 + 1) * D]
                        mm(o, ctxT[:, b * L:(b + 1) * L], Wqv[:, 1, :], start=True, stop=False)
                        ins = mm(o, ones[0:1, 0:L], rows[0:1, 0, :], start=False, stop=True)
                    ins.then_inc(s_pe, 1)
                for q in range(4):
                    pe.wait_ge(s_dve, 18)
                    for b in range(4 * q, 4 * q + 4):
                        o = banks[4 + q][0:L, (b % 4) * D:(b % 4 + 1) * D]
                        mm(o, VmT[:, b * L:(b + 1) * L], Wa[:, 3, :], start=True, stop=False)
                        ins = mm(o, ones[0:1, 0:L], rows[0:1, 1, :], start=False, stop=True)
                    ins.then_inc(s_pe, 1)

        ln_out, xT_s, diff, prob = pair("ln_out", [P, 2, D]), pair("xT_s", [P, 2 * P]), \
            pair("diff", [P, 2, L]), pair("prob", [P, 2, L])
        m_all = sb("m_all", [P, NT])
        den = pair("den", [P, 2])

        with nc.Block() as block:
            (hc_ready, hc_saved, hcT_psum, hcT_ready, hcT_saved, sim_psum, diff_ready, exp_ready, prob_ready,
             AT_psum, AT_saved, a0_dve) = (sem("a0_" + s) for s in (
                "hc_ready", "hc_saved", "hcT_psum", "hcT_ready", "hcT_saved", "sim_psum", "diff_ready", "exp_ready",
                "prob_ready", "AT_psum", "AT_saved", "chain"))
            T, S, A = banks[0:2], banks[2:4], banks[4:6]

            @block.gpsimd
            def _(pool):
                pool.sem_inc(hc_saved, CREDIT)
                with pool.Fori(0, B // 2) as i:
                    for par in range(2):
                        n = i * 2 + par
                        pool.wait_ge(hc_ready, done(n))
                        nc.gpsimd.tensor_copy(hc[:, bass.ds(n * TPB, TPB), :], ln_out[par][:]).then_inc(hc_saved, 1)

            @block.vector
            def _(dve):
                for s in (hc_ready, hcT_ready, diff_ready, prob_ready):
                    dve.sem_inc(s, CREDIT)
                lnk = Chain(dve, a0_dve, LN_LINKS + 3)
                with dve.Fori(0, B // 2) as i:
                    for par in range(2):
                        n = i * 2 + par
                        lnk.base, lnk.k = i * 2 * (LN_LINKS + 3) + par * LN_LINKS, 0
                        dve.wait_ge(hc_saved, free(n))
                        dve.wait_ge(hcT_psum, free(n))
                        layer_norm(dve, lnk, xt(n), ln_out[par][:], par, hc_ready)
                        assert lnk.k == LN_LINKS
                    for par in range(2):
                        n = i * 2 + par
                        dve.wait_ge(hcT_psum, done(n))
                        dve.wait_ge(sim_psum, free(n))
                        dve.wait_ge(hcT_saved, free(n))
                        nc.vector.tensor_copy(xT_s[par][:], T[par][:, 0:2 * P]).then_inc(hcT_ready, 1)
                    for par in range(2):
                        n = i * 2 + par
                        lnk.base, lnk.k = i * 2 * (LN_LINKS + 3) + 2 * LN_LINKS + par, 0
                        s = S[par][:, 0:2 * L].rearrange("p (t l) -> p t l", t=2)
                        dve.wait_ge(sim_psum, done(n))
                        m = m_all[:, bass.ds(n * TPB, TPB)]
                        lnk(nc.vector.tensor_reduce(m, s, AX, ALU.max))
                        dve.wait_ge(exp_ready, free(n))
                        nc.vector.tensor_tensor(diff[par][:], s, m.rearrange("p (t o) -> p t o", o=1).broadcast_to([P, 2, L]),
                                                ALU.subtract).then_inc(diff_ready, 1)
                    for par in range(2):
                        n = i * 2 + par
                        lnk.base, lnk.k = i * 2 * (LN_LINKS + 3) + 2 * LN_LINKS + 2 + 2 * par, 0
                        dve.wait_ge(exp_ready, done(n))
                        lnk(nc.vector.tensor_reduce(den[par][:], diff[par][:], AX, ALU.add))
                        lnk(nc.vector.reciprocal(den[par][:], den[par][:]))
                        dve.wait_ge(AT_psum, free(n))
                        nc.vector.tensor_tensor(prob[par][:], diff[par][:],
                                                den[par][:].rearrange("p (t o) -> p t o", o=1).broadcast_to([P, 2, L]),
                                                ALU.mult).then_inc(prob_ready, 1)

            @block.scalar
            def _(act):
                for s in (hcT_saved, exp_ready, AT_saved):
                    act.sem_inc(s, CREDIT)
                with act.Fori(0, B // 2) as i:
                    for par in range(2):
                        n = i * 2 + par
                        act.wait_ge(hcT_ready, done(n))
                        nc.scalar.copy(hcT[:, bass.ds(n * SEQ, SEQ)], xT_s[par][:]).then_inc(hcT_saved, 1)
                    for par in range(2):
                        n = i * 2 + par
                        act.wait_ge(diff_ready, done(n))
                        nc.scalar.activation(diff[par][:], diff[par][:], ACT.Exp).then_inc(exp_ready, 1)
                    for par in range(2):
                        n = i * 2 + par
                        act.wait_ge(AT_psum, done(n))
                        nc.scalar.copy(AT[0:L, bass.ds(n * SEQ, SEQ)], A[par][0:L, 0:SEQ]).then_inc(AT_saved, 1)

            @block.tensor
            def _(pe):
                for s in (hcT_psum, sim_psum, AT_psum):
                    pe.sem_inc(s, CREDIT)
                with pe.Fori(0, B // 2) as i:
                    for par in range(2):
                        n = i * 2 + par
                        pe.wait_ge(hc_ready, done(n))
                        pe.wait_ge(hcT_ready, free(n))
                        for j in range(2):
                            ins = nc.tensor.transpose(T[par][:, j * P:(j + 1) * P], ln_out[par][:, j, :], ident)
                        ins.then_inc(hcT_psum, 1)
                    for par in range(2):
                        n = i * 2 + par
                        pe.wait_ge(hcT_ready, done(n))
                        pe.wait_ge(diff_ready, free(n))
                        for j in range(2):
                            o = S[par][:, j * L:(j + 1) * L]
                            nc.tensor.matmul(o, xT_s[par][:, j * P:(j + 1) * P], MT[:, bass.ds(n * L, L)], start=True, stop=False)
                            ins = nc.tensor.matmul(o, ones[0:1, :], srow[0:1, 0, bass.ds(n * L, L)], start=False, stop=True)
                        ins.then_inc(sim_psum, 1)
                    for par in range(2):
                        n = i * 2 + par
                        pe.wait_ge(prob_ready, done(n))
                        pe.wait_ge(AT_saved, free(n))
                        hold(pe, "pe")
                        for j in range(2):
                            ins = nc.tensor.transpose(A[par][0:L, j * P:(j + 1) * P], prob[par][:, j, :], ident)
                        ins.then_inc(AT_psum, 1)

        hcb = sb("hcb", [P, B])
        batt = sb("batt", [P, NT])
        tgs = sb("tgs", [P, 2])
        pm = sb("pm", [P, B])
        m32 = sb("m32", [NT, 1])
        with nc.Block() as block:
            p_pe, p_dve, p_act = sem("p0_pe"), sem("p0_dve"), sem("p0_act")

            @block.tensor
            def _(pe):
                nc.tensor.transpose(banks[0][0:NT, 0:P], m_all[:], ident).then_inc(p_pe, 1)
                pe.wait_ge(p_dve, 1)
                nc.tensor.matmul(banks[1][0:1, 0:NT], m32[:], ident[0:NT, 0:NT], start=True, stop=True).then_inc(p_pe, 1)
                pe.wait_ge(p_dve, 2)
                nc.tensor.matmul(banks[2][:, 0:B], ones[0:1, :], pm[0:1, :], start=True, stop=True).then_inc(p_pe, 1)
                pe.wait_ge(p_act, 1)
                nc.tensor.matmul(banks[3][:, 0:NT], ones[:], batt[:], start=True, stop=True).then_inc(p_pe, 1)
                pe.wait_ge(p_dve, 6)
                for t in range(NT):
                    ins = nc.tensor.matmul(banks[4][:, t // TPB:t // TPB + 1], hc[:, t, :], batt[:, t:t + 1],
                                           start=(t % TPB == 0), stop=(t % TPB == TPB - 1))
                ins.then_inc(p_pe, 1)

            @block.scalar
            def _(act):
                act.wait_ge(p_dve, 3)
                nc.scalar.activation(batt[:], batt[:], ACT.Exp).then_inc(p_act, 1)

            @block.vector
            def _(dve):
                link = Chain(dve, p_dve)
                dve.wait_ge(p_pe, 1)
                link(nc.vector.tensor_reduce(m32[:], banks[0][0:NT, 0:P], AX, ALU.max))
                dve.wait_ge(p_pe, 2)
                link(nc.vector.tensor_reduce(pm[0:1, :], banks[1][0:1, 0:NT].rearrange("p (b t) -> p b t", t=TPB), AX, ALU.max))
                dve.wait_ge(p_pe, 3)

                def by_batch(ap):
                    return ap.rearrange("p (b t) -> p b t", t=TPB)

                def spread(ap):
                    return ap.rearrange("p (b o) -> p b o", o=1).broadcast_to([P, B, TPB])

                link(nc.vector.tensor_tensor(by_batch(batt[:]), by_batch(m_all[:]), spread(banks[2][:, 0:B]), ALU.subtract))
                dve.wait_ge(p_pe, 4)
                link(nc.vector.tensor_reduce(pm[:], by_batch(banks[3][:, 0:NT]), AX, ALU.add))
                link(nc.vector.reciprocal(pm[:], pm[:]))
                link(nc.vector.tensor_tensor(by_batch(batt[:]), by_batch(batt[:]), spread(pm[:]), ALU.mult))
                nc.vector.tensor_scalar(tgs[:, 0:1], tg[:, 2:3], UN2, None, ALU.mult)
                nc.vector.tensor_scalar(tgs[:, 1:2], tg[:, 3:4], UN2 / K1, None, ALU.mult)
                dve.wait_ge(p_pe, 5)
                link(nc.vector.tensor_copy(hcb[:], banks[4][:, 0:B]))

        ctx_s, AT_s = pair("ctx_s", [L, D]), pair("AT_s", [L, SEQ])
        prod, Wp = pair("prod", [P, SEQ]), pair("Wp", [P, D])
        u16 = pair("u16", [P, 2, 2 * D], F16)
        lg, v8, i8 = pair("lg", [P, 2, E0]), pair("v8", [P, 2, 8]), pair("i8", [P, 2, 8], U32)
        el, idxf = pair("el", [P, 2, E0]), pair("idxf", [P, 6])
        oh, ohx = pair("oh", [P, 6, E0]), pair("ohx", [P, 6, E0])
        Msum, M16, Gs = pair("Msum", [P, 2, E0]), pair("M16", [P, 2, E0], F16), pair("Gs", [P, 2, E0 + 1])
        S16, posf = pair("S16", [P, E0], F16), pair("posf", [P, 6])
        pos_s, pos = pair("pos_s", [P, 6], I32), sb("pos", [P, NT * K0])
        gk = sb("gk", [P, NT * K0])
        gsel = pair("gsel", [P, 6])
        ctmp = sb("ctmp", [P, E0])
        GT = hc[:].rearrange("p t d -> p (t d)")[0:E0 + 1, :]
        scat = [sem(f"scattered{i}") for i in range(2)]

        with nc.Block() as block:
            (st_ready, q_psum, wp_ready, prod_ready, o_psum, u16_ready, ut_psum, ut_saved, lg_psum, d_ready,
             e_ready, m_ready, r_psum, idx_ready, g_ready, gt_psum, gt_saved, x_done, r0_dve) = (
                sem("r0_" + s) for s in (
                    "st_ready", "q_psum", "wp_ready", "prod_ready", "o_psum", "u16_ready", "ut_psum", "ut_saved",
                    "lg_psum", "d_ready", "e_ready", "m_ready", "r_psum", "idx_ready", "g_ready", "gt_psum",
                    "gt_saved", "x_done", "chain"))
            ctx_ld = [sem(f"r0_ctx_loaded{i}") for i in range(2)]
            Q, O, TU, LG = banks[0:2], banks[2:4], banks[4:6], banks[6:8]
            counted = sem("r0_counted")
            LA, LB, LD, START = LN_LINKS + 4, 7, 8, 2
            PER = 2 * (LA + LB + LD)

            @block.sync
            def _(sp):
                with sp.Fori(0, B // 2) as i:
                    for par in range(2):
                        n = i * 2 + par
                        sp.wait_ge(q_psum, free(n))
                        sp.dma_start(ctx_s[par][:], a["ctx_1024"][bass.ds(n, 1)].rearrange("o s d -> (o s) d")
                                     ).then_inc(ctx_ld[par], 16)

            @block.gpsimd
            def _(pool):
                for par in range(2):
                    r0 = E0 * REGION + par * P
                    pool.dma_start(sorted_rows[r0:r0 + P, :], zeros[:, 0:2 * D]).then_inc(scat[par], 16)
                with pool.Fori(0, B // 2) as i:
                    for par in range(2):
                        n = i * 2 + par
                        pool.wait_ge(idx_ready, done(n))
                        hold(pool, "pool")
                        for c in range(2 * K0):
                            nc.gpsimd.indirect_dma_start(
                                out=sorted_rows, out_offset=bass.IndirectOffsetOnAxis(ap=pos_s[par][:, c:c + 1], axis=0),
                                in_=u16[par][:, c // K0, :], in_offset=None).then_inc(scat[par], 16)

            @block.scalar
            def _(act):
                for s in (st_ready, ut_saved, e_ready, gt_saved):
                    act.sem_inc(s, CREDIT)
                with act.Fori(0, B // 2) as i:
                    for par in range(2):
                        n = i * 2 + par
                        act.wait_ge(o_psum, free(n))
                        act.wait_ge(prod_ready, free(n))
                        nc.scalar.copy(AT_s[par][:], AT[0:L, bass.ds(n * SEQ, SEQ)])
                        nc.scalar.copy(xT_s[par][:], hcT[:, bass.ds(n * SEQ, SEQ)]).then_inc(st_ready, 1)
                    for par in range(2):
                        n = i * 2 + par
                        act.wait_ge(ut_psum, done(n))
                        nc.scalar.copy(uT[:, :, bass.ds(n * SEQ, SEQ)],
                                       TU[par][:, 0:SEQ].bitcast(F16).rearrange("p (h t) -> p h t", h=2)).then_inc(ut_saved, 1)
                    for par in range(2):
                        n = i * 2 + par
                        act.wait_ge(d_ready, done(n))
                        nc.scalar.activation(el[par][:], el[par][:], ACT.Exp).then_inc(e_ready, 1)
                    for par in range(2):
                        n = i * 2 + par
                        act.wait_ge(gt_psum, done(n))
                        nc.scalar.copy(GT[:, bass.ds(n * SEQ, SEQ)], Q[par][0:E0 + 1, 0:SEQ]).then_inc(gt_saved, 1)

            @block.vector
            def _(dve):
                for s in (wp_ready, prod_ready, u16_ready, d_ready, m_ready, idx_ready, g_ready, x_done):
                    dve.sem_inc(s, CREDIT)
                lnk = Chain(dve, r0_dve)
                nc.vector.memset(S16[0][:], 0.0).then_inc(counted, 1)
                dve.wait_ge(counted, 1)
                for par in range(2):
                    lnk(nc.vector.memset(Gs[par][:], 1.0))
                with dve.Fori(0, B // 2) as i:
                    for par in range(2):
                        n = i * 2 + par
                        dve.wait_ge(o_psum, free(n))
                        nc.vector.scalar_tensor_tensor(Wp[par][:], Wqv[:, 3, :], hcb[:, bass.ds(n, 1)], Wqv[:, 0, :],
                                                       ALU.mult, ALU.add).then_inc(wp_ready, 1)
                    for par in range(2):
                        n = i * 2 + par
                        dve.wait_ge(q_psum, done(n))
                        dve.wait_ge(st_ready, done(n))
                        nc.vector.tensor_tensor(prod[par][:], xT_s[par][:], Q[par][:, 0:SEQ], ALU.mult).then_inc(prod_ready, 1)
                    for par in range(2):
                        n = i * 2 + par
                        lnk.base, lnk.k = i * PER + START + par * LA, 0
                        dve.wait_ge(o_psum, done(n))
                        lnk(nc.vector.scalar_tensor_tensor(xt(n), O[par][:, 0:SEQ].rearrange("p (t d) -> p t d", t=2),
                                                           tg[:, 0:1], xt(n), ALU.mult, ALU.add))
                        layer_norm(dve, lnk, xt(n), ln_out[par][:], par, None)
                        dve.wait_ge(scat[par], i * 96 + 16)
                        dve.wait_ge(ut_psum, free(n))
                        hi, lo = u16[par][:, :, 0:D], u16[par][:, :, D:2 * D]
                        lnk(nc.vector.tensor_scalar(hi, ln_out[par][:], SU, None, ALU.mult))
                        lnk(nc.vector.scalar_tensor_tensor(xt(n), ln_out[par][:], tg[:, 2:3], xt(n), ALU.mult, ALU.add))
                        nc.vector.scalar_tensor_tensor(lo, ln_out[par][:], SU, hi, ALU.mult, ALU.subtract).then_inc(u16_ready, 1)
                        assert lnk.k == LA
                    for par in range(2):
                        n = i * 2 + par
                        lnk.base, lnk.k = i * PER + START + 2 * LA + par * LB, 0
                        dve.wait_ge(lg_psum, done(n))
                        lnk(nc.vector.tensor_scalar(lg[par][:], LG[par][:, 0:2 * 16].rearrange("p (t e) -> p t e", e=16)[:, :, 0:E0],
                                                    UN1, None, ALU.mult))
                        hold(dve, "dve")
                        for j in range(2):
                            ins = nc.vector.max(v8[par][:, j, :], lg[par][:, j, :])
                        lnk(ins)
                        hold(dve, "dve")
                        for j in range(2):
                            ins = nc.vector.max_index(i8[par][:, j, :], v8[par][:, j, :], lg[par][:, j, :])
                        lnk(ins)
                        nc.vector.tensor_tensor(el[par][:], lg[par][:], v8[par][:, :, 0:1].broadcast_to([P, 2, E0]),
                                                ALU.subtract).then_inc(d_ready, 1)
                        lnk(nc.vector.tensor_copy(idxf[par][:].rearrange("p (t k) -> p t k", k=K0), i8[par][:, :, 0:K0]))
                        lnk(nc.vector.tensor_tensor(
                            oh[par][:], idxf[par][:].rearrange("p (c o) -> p c o", o=1).broadcast_to([P, 6, E0]),
                            cst[:, C_IOTA:C_IOTA + 6 * E0].rearrange("p (c e) -> p c e", e=E0), ALU.is_equal))
                        lnk(nc.vector.tensor_reduce(Msum[par][:], oh[par][:].rearrange("p (t k) e -> p t e k", k=K0), AX, ALU.add))
                        nc.vector.tensor_copy(M16[par][:], Msum[par][:]).then_inc(m_ready, 1)
                        lnk(nc.vector.tensor_tensor(ctmp[:], Msum[par][:, 0, :], Msum[par][:, 1, :], ALU.add))
                        dve.wait_ge(r_psum, n + CREDIT)
                        nc.vector.tensor_tensor(S16[1 - par][:], S16[par][:], ctmp[:], ALU.add).then_inc(counted, 1)
                        assert lnk.k == LB
                    for par in range(2):
                        n = i * 2 + par
                        lnk.base, lnk.k = i * PER + START + 2 * (LA + LB) + par * LD, 0
                        oh4 = oh[par][:].rearrange("p (t k) e -> p t k e", k=K0)
                        ohx4 = ohx[par][:].rearrange("p (t k) e -> p t k e", k=K0)
                        dve.wait_ge(e_ready, done(n))
                        lnk(nc.vector.tensor_reduce(den[par][:], el[par][:], AX, ALU.add))
                        lnk(nc.vector.reciprocal(den[par][:], den[par][:]))
                        lnk(nc.vector.tensor_tensor(el[par][:], el[par][:],
                                                    den[par][:].rearrange("p (t o) -> p t o", o=1).broadcast_to([P, 2, E0]), ALU.mult))
                        dve.wait_ge(gt_psum, free(n))
                        nc.vector.tensor_tensor(Gs[par][:, :, 0:E0], el[par][:], Msum[par][:], ALU.mult).then_inc(g_ready, 1)
                        lnk(nc.vector.tensor_tensor(
                            ohx4, oh4, el[par][:].rearrange("p t (o e) -> p t o e", o=1).broadcast_to([P, 2, K0, E0]), ALU.mult))
                        lnk(nc.vector.tensor_reduce(gsel[par][:], ohx[par][:], AX, ALU.add))
                        nc.vector.tensor_scalar(gk[:, bass.ds(n * 6, 6)], gsel[par][:], tgs[:, 0:1], None, ALU.mult)
                        dve.wait_ge(r_psum, done(n))
                        r3 = LG[par][:, 64:64 + 2 * 16].rearrange("p (t e) -> p t e", e=16)[:, :, 0:E0]
                        base = cst[:, C_BASE:C_BASE + E0].rearrange("p (o e) -> p o e", o=1).broadcast_to([P, 2, E0])
                        lnk(nc.vector.tensor_tensor(lg[par][:], r3, base, ALU.add))
                        lnk(nc.vector.tensor_tensor(
                            ohx4, oh4, lg[par][:].rearrange("p t (o e) -> p t o e", o=1).broadcast_to([P, 2, K0, E0]), ALU.mult))
                        lnk(nc.vector.tensor_reduce(posf[par][:], ohx[par][:], AX, ALU.add))
                        nc.vector.tensor_copy(pos[:, bass.ds(n * 6, 6)], posf[par][:])
                        dve.wait_ge(scat[par], i * 96 + 16)
                        nc.vector.tensor_copy(pos_s[par][:], posf[par][:]).then_inc(idx_ready, 1)

            @block.tensor
            def _(pe):
                mm = nc.tensor.matmul
                for s in (q_psum, o_psum, ut_psum, lg_psum, r_psum, gt_psum):
                    pe.sem_inc(s, CREDIT)
                with pe.Fori(0, B // 2) as i:
                    for par in range(2):
                        n = i * 2 + par
                        pe.wait_ge(ctx_ld[par], i * 16 + 16)
                        pe.wait_ge(st_ready, done(n))
                        pe.wait_ge(gt_saved, free(n))
                        mm(Q[par][:, 0:SEQ], ctx_s[par][:], AT_s[par][:], start=True, stop=True).then_inc(q_psum, 1)
                    for par in range(2):
                        n = i * 2 + par
                        pe.wait_ge(wp_ready, done(n))
                        pe.wait_ge(prod_ready, done(n))
                        pe.wait_ge(u16_ready, free(n))
                        for j in range(2):
                            o = O[par][:, j * D:(j + 1) * D]
                            js = slice(j * P, (j + 1) * P)
                            mm(o, xT_s[par][:, js], Wp[par][:], start=True, stop=False)
                            mm(o, prod[par][:, js], Wqv[:, 2, :], start=False, stop=False)
                            ins = mm(o, AT_s[par][:, js], HW1[:, bass.ds(n, 1), :].rearrange("p o d -> p (o d)"),
                                     start=False, stop=True)
                        ins.then_inc(o_psum, 1)
                    for par in range(2):
                        n = i * 2 + par
                        pe.wait_ge(u16_ready, done(n))
                        pe.wait_ge(ut_saved, free(n))
                        t16 = TU[par][:, 0:SEQ].bitcast(F16)
                        for j in range(2):
                            for h in range(2):
                                ins = nc.tensor.transpose(t16[:, h * SEQ + j * P:h * SEQ + (j + 1) * P],
                                                          u16[par][:, j, h * D:(h + 1) * D], ident16[:])
                        ins.then_inc(ut_psum, 1)
                    for par in range(2):
                        n = i * 2 + par
                        pe.wait_ge(ut_saved, done(n))
                        pe.wait_ge(idx_ready, free(n))
                        for j in range(2):
                            o = LG[par][:, j * 16:j * 16 + E0]
                            uh, ul = (uT[:, h, bass.ds(n * SEQ + j * P, P)] for h in range(2))
                            mm(o, uh, gw16[:, 0, 0:E0], start=True, stop=False)
                            mm(o, uh, gw16[:, 1, 0:E0], start=False, stop=False)
                            mm(o, ul, gw16[:, 0, 0:E0], start=False, stop=False)
                            ins = mm(o, ones[0:1, :], rows[0:1, 2, 0:E0], start=False, stop=True)
                        ins.then_inc(lg_psum, 1)
                    for par in range(2):
                        n = i * 2 + par
                        pe.wait_ge(m_ready, done(n))
                        pe.wait_ge(counted, n + 1)
                        for j in range(2):
                            o = LG[par][:, 64 + j * 16:64 + j * 16 + E0]
                            mm(o, tri16[:], M16[par][:, j, :], start=True, stop=False)
                            if j:
                                mm(o, ones16[:], M16[par][:, 0, :], start=False, stop=False)
                            ins = mm(o, ones16[:], S16[par][:], start=False, stop=True)
                        ins.then_inc(r_psum, 1)
                    for par in range(2):
                        n = i * 2 + par
                        pe.wait_ge(g_ready, done(n))
                        hold(pe, "pe")
                        for j in range(2):
                            ins = nc.tensor.transpose(Q[par][0:E0 + 1, j * P:(j + 1) * P], Gs[par][:, j, :], ident)
                        ins.then_inc(gt_psum, 1)

        tw = sb("tw", [P, 8, E0])
        tcum = sb("tcum", [P, E0, E0])
        ti = sb("ti", [P, 2, E0], I32)
        tabc = sb("tabc", [P, 2])
        moved = AT[:, 0:NT * K0 * (E0 - 1)].rearrange("p (c e) -> p c e", e=E0 - 1)
        shift = sb("shift", [P, NT * K0])
        places = sb("places", [P, NT * K0], I32)
        tab = sb("tab", [1, 2, P], I32)
        crow = sb("crow", [1, E0], I32)
        with nc.Block() as block:
            t_pe, t_dve, t_pad = sem("t_pe"), sem("t_dve"), sem("t_pad")

            @block.tensor
            def _(pe):
                nc.tensor.matmul(banks[0][:, 0:E0], ones16[:], S16[0][:], start=True, stop=True).then_inc(t_pe, 1)
                pe.wait_ge(t_dve, 16)
                for k in range(2):
                    ins = nc.tensor.matmul(banks[1][0:1, k * P:(k + 1) * P], tabc[:, k:k + 1], ident, start=True, stop=True)
                ins.then_inc(t_pe, 1)

            @block.vector
            def _(dve):
                link = Chain(dve, t_dve)
                cnt, tiles, cum, before, tmp = (tw[:, k, :] for k in range(5))
                part = cst[:, C_PART:C_PART + 1]
                dve.wait_ge(t_pe, 1)
                link(nc.vector.tensor_copy(cnt, banks[0][:, 0:E0]))
                link(nc.vector.tensor_tensor(tmp, cnt, cst[:, C_BASE:C_BASE + E0], ALU.add))
                link(nc.vector.tensor_copy(crow[:], tw[0:1, 4, :]))
                link(nc.vector.tensor_scalar(ti[:, 0, :], cnt, float(BLK - 1), None, ALU.add))
                link(nc.vector.tensor_scalar(ti[:, 1, :], ti[:, 0, :], BLK.bit_length() - 1, None, ALU.logical_shift_right))
                link(nc.vector.tensor_copy(tiles, ti[:, 1, :]))
                link(nc.vector.tensor_tensor(tcum[:], cst[:, C_LE:C_LE + E0 * E0].rearrange("p (e f) -> p e f", f=E0),
                                             tw[:, 1:2, :].broadcast_to([P, E0, E0]), ALU.mult))
                link(nc.vector.tensor_reduce(cum, tcum[:], AX, ALU.add))
                link(nc.vector.tensor_scalar(before, cum, part, None, ALU.is_le))
                link(nc.vector.tensor_reduce(tw[:, 5, 0:1], before, AX, ALU.add))
                link(nc.vector.tensor_tensor(tmp, before, tiles, ALU.mult))
                link(nc.vector.tensor_reduce(tw[:, 5, 1:2], tmp, AX, ALU.add))
                link(nc.vector.tensor_tensor(tw[:, 5, 2:3], part, tw[:, 5, 1:2], ALU.subtract))
                link(nc.vector.tensor_scalar(tw[:, 5, 3:4], tw[:, 5, 2:3], float(BLK), None, ALU.mult))
                nc.vector.tensor_scalar(tabc[:, 0:1], tw[:, 5, 0:1], float(E0 - 1), None, ALU.min)
                link(nc.vector.scalar_tensor_tensor(tw[:, 5, 4:5], tw[:, 5, 0:1], float(REGION), tw[:, 5, 3:4],
                                                    ALU.mult, ALU.add))
                link(nc.vector.tensor_scalar(tabc[:, 1:2], tw[:, 5, 4:5], float(E0 * REGION), None, ALU.min))
                nc.vector.tensor_scalar(tw[:, 6, 0:E0 - 1], tw[:, 1, 0:E0 - 1], float(BLK), -float(REGION), ALU.mult, ALU.add)
                link(nc.vector.tensor_tensor(
                    moved, pos[:].rearrange("p (c o) -> p c o", o=1).broadcast_to([P, NT * K0, E0 - 1]),
                    cst[:, C_BASE + 1:C_BASE + E0].rearrange("p (o e) -> p o e", o=1).broadcast_to([P, NT * K0, E0 - 1]),
                    ALU.is_ge))
                link(nc.vector.tensor_tensor(moved, moved, tw[:, 6:7, 0:E0 - 1].broadcast_to([P, NT * K0, E0 - 1]), ALU.mult))
                link(nc.vector.tensor_reduce(shift[:], moved, AX, ALU.add))
                link(nc.vector.tensor_tensor(places[:], pos[:], shift[:], ALU.add))
                dve.wait_ge(t_pe, 2)
                link(nc.vector.tensor_copy(tab[:], banks[1][0:1, 0:2 * P].rearrange("p (k i) -> p k i", k=2)))

            @block.sync
            def _(sp):
                sp.wait_ge(t_dve, 3)
                for e in range(E0):
                    r = sp.value_load(crow[0:1, e:e + 1], min_val=0, max_val=ROWS - BLK)
                    sp.dma_start(sorted_rows[bass.ds(r, BLK), :].rearrange("(t q) d -> q t d", q=P),
                                 zeros[:].rearrange("p (t d) -> p t d", t=2)).then_inc(t_pad, 16)
                sp.wait_ge(t_pad, 16 * E0)
                for par in range(2):
                    sp.wait_ge(scat[par], 96 * (B // 2) + 16)

        def add_shared(dve, t_psum, x_sem, par, g):
            dve.wait_ge(t_psum, done(g))
            xg = X[:, bass.ds(g * 4, 4), :]
            nc.vector.scalar_tensor_tensor(xg, banks[4 + par][:].rearrange("p (t d) -> p t d", t=4), tgs[:, 0:1], xg,
                                           ALU.mult, ALU.add).then_inc(x_sem, 1)

        hf = [AT[:, 512 * k:512 * k + 512] for k in range(2)]
        hid = hcT[:].bitcast(F16).rearrange("p (g h c t) -> p g h c t", g=2, h=2, c=4)
        yT = [AT[:, 1024 + 512 * k:1536 + 512 * k] for k in range(2)]
        with nc.Block() as block:
            s_h, s_hf, s_lo, s_y, s_yc, s_t, s_x, s_lk = (sem("sh_" + s) for s in (
                "h_psum", "gelu", "split", "y_psum", "y_copied", "t_psum", "x", "chain"))
            G = TOK // 512

            @block.tensor
            def _(pe):
                mm = nc.tensor.matmul
                for s in (s_h, s_y, s_t):
                    pe.sem_inc(s, CREDIT)

                def transpose_back(par, g):
                    pe.wait_ge(s_yc, done(g))
                    pe.wait_ge(s_x, free(g))
                    for j in range(4):
                        ins = nc.tensor.transpose(banks[4 + par][:, j * P:(j + 1) * P], yT[par][:, j * P:(j + 1) * P], ident)
                    ins.then_inc(s_t, 1)

                with pe.Fori(0, G // 2) as i:
                    for par in range(2):
                        g = i * 2 + par
                        ug, ul = (uT[:, h, bass.ds(g * 512, 512)] for h in range(2))
                        for c in range(4):
                            q = g * 4 + c
                            cs = slice(c * P, (c + 1) * P)
                            pe.wait_ge(s_hf, free(q))
                            mm(banks[c % 2][:], S1[:, 0, cs], ug, start=True, stop=False)
                            mm(banks[c % 2][:], S1[:, 1, cs], ug, start=False, stop=False)
                            mm(banks[c % 2][:], S1[:, 0, cs], ul, start=False, stop=True).then_inc(s_h, 1)
                        if par:
                            transpose_back(0, i * 2)
                        Y = banks[2 + par]
                        pe.wait_ge(s_yc, free(g))
                        mm(Y[:], b2a[:], GT[:, bass.ds(g * 512, 512)], start=True, stop=False)
                        for c in range(4):
                            q = g * 4 + c
                            cs = slice(c * P, (c + 1) * P)
                            pe.wait_ge(s_lo, done(q))
                            mm(Y[:], S2[:, 0, cs], hid[:, par, 0, c, :], start=False, stop=False)
                            mm(Y[:], S2[:, 1, cs], hid[:, par, 0, c, :], start=False, stop=False)
                            ins = mm(Y[:], S2[:, 0, cs], hid[:, par, 1, c, :], start=False, stop=(c == 3))
                        ins.then_inc(s_y, 1)
                    transpose_back(1, i * 2 + 1)

            @block.scalar
            def _(act):
                act.sem_inc(s_hf, CREDIT)
                act.sem_inc(s_yc, CREDIT)
                with act.Fori(0, G // 2) as i:
                    for par in range(2):
                        g = i * 2 + par
                        for c in range(4):
                            q = g * 4 + c
                            act.wait_ge(s_h, done(q))
                            act.wait_ge(s_lo, free(q))
                            nc.scalar.activation(hf[c % 2], banks[c % 2][:], ACT.Gelu,
                                                 bias=cols[:, V_SB1 + c:V_SB1 + c + 1], scale=UN1).then_inc(s_hf, 1)
                        act.wait_ge(s_y, done(g))
                        act.wait_ge(s_t, free(g))
                        nc.scalar.copy(yT[par][:], banks[2 + par][:]).then_inc(s_yc, 1)

            @block.vector
            def _(dve):
                dve.sem_inc(s_lo, CREDIT)
                dve.sem_inc(s_x, CREDIT)
                lnk = Chain(dve, s_lk)
                with dve.Fori(0, G // 2) as i:
                    for par in range(2):
                        g = i * 2 + par
                        for c in range(4):
                            q = g * 4 + c
                            lnk.base, lnk.k = q, 0
                            dve.wait_ge(s_hf, done(q))
                            dve.wait_ge(s_y, free(g))
                            lnk(nc.vector.tensor_scalar(hid[:, par, 0, c, :], hf[c % 2], SH, None, ALU.mult))
                            nc.vector.scalar_tensor_tensor(hid[:, par, 1, c, :], hf[c % 2], SH, hid[:, par, 0, c, :],
                                                           ALU.mult, ALU.subtract).then_inc(s_lo, 1)
                        if par:
                            add_shared(dve, s_t, s_x, 0, i * 2)
                    add_shared(dve, s_t, s_x, 1, i * 2 + 1)

        h16 = hcT[:].bitcast(F16)
        xp = [h16[:, 4096 + 512 * k:4608 + 512 * k].rearrange("p (t d) -> p t d", t=2) for k in range(4)]
        DEEP, WDEEP = 4, 8
        we = [hc[:].rearrange("p t d -> p (t d)")[:, WEW * k:WEW * (k + 1)] for k in range(WDEEP - 1)]
        we.append(AT[:, 2560:2560 + WEW])
        we16, web = [w.bitcast(F16) for w in we], [w[:, 2 * F0:2 * F0 + 2] for w in we]
        xpT = [h16[:, 1024 + 512 * k:1536 + 512 * k].rearrange("p (h t) -> p h t", h=2) for k in range(2)]
        hs = [h16[:, 2048 + 1024 * k:3072 + 1024 * k].rearrange("p (h t) -> p h t", h=2) for k in range(2)]
        ys = [AT[:, 2048 + 256 * k:2304 + 256 * k].rearrange("p (t d) -> p t d", t=2) for k in range(2)]
        with nc.Block() as block:
            x_tr, x_cp, x_h, x_hf, x_lo, x_y, x_yc, x_lk = (sem("ex_" + s) for s in (
                "t_psum", "t_copied", "h_psum", "gelu", "split", "y_psum", "y_copied", "chain"))
            x_ld = [sem(f"ex_rows_loaded{i}") for i in range(4)]
            w_ld = [sem(f"ex_weights_loaded{i}") for i in range(WDEEP)]
            x_st = [sem(f"ex_stored{i}") for i in range(2)]
            TB, HB, YB = banks[0:2], banks[2:4], banks[4:6]
            MAIN = BLOCKS // DEEP - 1
            WMAIN = BLOCKS // WDEEP - 1

            @block.sync
            def _(sp):
                def load_rows(b, k):
                    row = sp.value_load(tab[0:1, 1, bass.ds(b, 1)], min_val=0, max_val=ROWS - BLK)
                    sp.dma_start(xp[k], sorted_rows[bass.ds(row, BLK), :].rearrange("(t q) d -> q t d", q=P)
                                 ).then_inc(x_ld[k], 16)

                def store(b, par):
                    sp.wait_ge(x_yc, done(b))
                    sp.dma_start(expert_rows[bass.ds(b * BLK, BLK), :].rearrange("(t q) d -> q t d", q=P),
                                 ys[par]).then_inc(x_st[par], 16)

                for par in range(2):
                    sp.sem_inc(x_st[par], 16)
                def next_rows(b, k):
                    sp.wait_ge(x_tr, done(b))
                    hold(sp, "sp")
                    load_rows(b + DEEP, k)

                for b in range(DEEP):
                    load_rows(b, b)
                next_rows(0, 0)
                next_rows(1, 1)
                with sp.Fori(0, MAIN - 1) as i:
                    for k in range(DEEP):
                        store(i * DEEP + k, k % 2)
                        next_rows(i * DEEP + k + 2, (k + 2) % DEEP)
                for b in range((MAIN - 1) * DEEP, BLOCKS):
                    store(b, b % 2)
                    if b + 2 + DEEP < BLOCKS:
                        next_rows(b + 2, (b + 2) % DEEP)
                for par in range(2):
                    sp.wait_ge(x_st[par], 16 * (BLOCKS // 2) + 16)

            @block.gpsimd
            def _(pool):
                def load_weights(b, k):
                    e = pool.value_load(tab[0:1, 0, bass.ds(b, 1)], min_val=0, max_val=E0 - 1)
                    pool.dma_start(we[k], WE[:, bass.ds(e, 1), :].rearrange("p o f -> p (o f)")).then_inc(w_ld[k], 16)

                for b in range(WDEEP):
                    load_weights(b, b)
                with pool.Fori(0, WMAIN) as i:
                    for k in range(WDEEP):
                        b = i * WDEEP + k
                        pool.wait_ge(x_y, done(b))
                        hold(pool, "pool")
                        load_weights(b + WDEEP, k)

            @block.tensor
            def _(pe):
                mm = nc.tensor.matmul
                for s in (x_tr, x_h, x_y):
                    pe.sem_inc(s, CREDIT)

                def transposes(b, k, use):
                    par = k % 2
                    pe.wait_ge(x_ld[k % DEEP], use)
                    pe.wait_ge(x_cp, free(b))
                    t16 = TB[par][:, 0:SEQ].bitcast(F16)
                    for j in range(2):
                        for h in range(2):
                            ins = nc.tensor.transpose(t16[:, h * SEQ + j * P:h * SEQ + (j + 1) * P],
                                                      xp[k % DEEP][:, j, h * D:(h + 1) * D], ident16[:])
                    ins.then_inc(x_tr, 1)

                def hidden(b, k, use):
                    par = k % 2
                    pe.wait_ge(w_ld[k], use)
                    pe.wait_ge(x_cp, done(b))
                    pe.wait_ge(x_hf, free(b))
                    xh, xl = (xpT[par][:, h, :] for h in range(2))
                    for c in range(2):
                        wh, wl = (we16[k][:, h * F0 + c * P:h * F0 + (c + 1) * P] for h in range(2))
                        o = HB[par][:, c * BLK:(c + 1) * BLK]
                        mm(o, wh, xh, start=True, stop=False)
                        mm(o, wh, xl, start=False, stop=False)
                        ins = mm(o, wl, xh, start=False, stop=True)
                    ins.then_inc(x_h, 1)

                def outputs(b, k):
                    par = k % 2
                    pe.wait_ge(x_lo, done(b))
                    pe.wait_ge(x_yc, free(b))
                    for j in range(2):
                        o = YB[par][:, j * D:(j + 1) * D]
                        for c in range(2):
                            hh, hl = (hs[par][:, h, c * BLK + j * P:c * BLK + (j + 1) * P] for h in range(2))
                            wh, wl = (we16[k][:, 2 * F0 + h * 2 * D + c * D:2 * F0 + h * 2 * D + (c + 1) * D] for h in range(2))
                            mm(o, hh, wh, start=(c == 0), stop=False)
                            mm(o, hh, wl, start=False, stop=False)
                            ins = mm(o, hl, wh, start=False, stop=(c == 1))
                    ins.then_inc(x_y, 1)

                def step(i, k, last=False):
                    b = i * WDEEP + k
                    if not (last and k >= WDEEP - 2):
                        transposes(b + 2, (k + 2) % WDEEP, i * 32 + ((k + 2) // DEEP) * 16 + 16)
                    if not (last and k >= WDEEP - 1):
                        hidden(b + 1, (k + 1) % WDEEP, (i + (k + 1) // WDEEP) * 16 + 16)
                    outputs(b, k)

                transposes(0, 0, 16)
                transposes(1, 1, 16)
                hidden(0, 0, 16)
                with pe.Fori(0, WMAIN) as i:
                    for k in range(WDEEP):
                        step(i, k)
                for k in range(WDEEP):
                    step(WMAIN, k, last=True)

            @block.vector
            def _(dve):
                dve.sem_inc(x_cp, CREDIT)
                dve.sem_inc(x_lo, CREDIT)
                lnk = Chain(dve, x_lk)

                def copy_rows(b, par):
                    dve.wait_ge(x_tr, done(b))
                    dve.wait_ge(x_h, free(b))
                    nc.vector.tensor_copy(xpT[par], TB[par][:, 0:SEQ].bitcast(F16).rearrange("p (h t) -> p h t", h=2)
                                          ).then_inc(x_cp, 1)

                def split(b, par):
                    lnk.base, lnk.k = b, 0
                    dve.wait_ge(x_hf, done(b))
                    dve.wait_ge(x_y, free(b))
                    lnk(nc.vector.tensor_scalar(hs[par][:, 0, :], hf[par], SH, None, ALU.mult))
                    nc.vector.scalar_tensor_tensor(hs[par][:, 1, :], hf[par], SH, hs[par][:, 0, :],
                                                   ALU.mult, ALU.subtract).then_inc(x_lo, 1)

                copy_rows(0, 0)
                copy_rows(1, 1)
                split(0, 0)
                with dve.Fori(0, BLOCKS // 2 - 1) as i:
                    for par in range(2):
                        copy_rows(i * 2 + 2 + par, par)
                        split(i * 2 + 1 + par, 1 - par)
                split(BLOCKS - 1, 1)

            @block.scalar
            def _(act):
                act.sem_inc(x_hf, CREDIT)
                act.sem_inc(x_yc, CREDIT)

                def gelu(b, k):
                    par = k % 2
                    act.wait_ge(x_h, done(b))
                    act.wait_ge(x_lo, free(b))
                    for c in range(2):
                        s = slice(c * BLK, (c + 1) * BLK)
                        ins = nc.scalar.activation(hf[par][:, s], HB[par][:, s], ACT.Gelu, bias=web[k][:, c:c + 1], scale=UN1)
                    ins.then_inc(x_hf, 1)

                def copy_out(b, par, stores):
                    act.wait_ge(x_y, done(b))
                    act.wait_ge(x_st[par], stores)
                    nc.scalar.copy(ys[par], YB[par][:, 0:SEQ].rearrange("p (t d) -> p t d", t=2)).then_inc(x_yc, 1)

                gelu(0, 0)
                gelu(1, 1)
                copy_out(0, 0, 16)
                with act.Fori(0, WMAIN) as i:
                    for k in range(WDEEP):
                        b = i * WDEEP + k
                        gelu(b + 2, (k + 2) % WDEEP)
                        copy_out(b + 1, (k + 1) % 2, i * 64 + 16 * ((k + 1) // 2) + 16)
                for b in range(WMAIN * WDEEP, BLOCKS):
                    if b + 2 < BLOCKS:
                        gelu(b + 2, (b + 2) % WDEEP)
                    if b + 1 < BLOCKS:
                        copy_out(b + 1, (b + 1) % 2, 16 * ((b + 1) // 2) + 16)

        Yg = [AT[:, 2560 + 768 * k:3328 + 768 * k].rearrange("p (c d) -> p c d", d=D) for k in range(2)]
        mh = [Gs[k][:, :, 0:HEADS] for k in range(2)]
        pTs = AT_s
        pos_g = pos_s
        with nc.Block() as block:
            (v_ready, vT_psum, vT_ready, sc_psum, sc_ready, ex_ready, pr_ready, pT_psum, pT_ready, o_psum, x_ready, got_in,
             b_dve, b_pool) = (sem("a1_" + s) for s in (
                "v_ready", "vT_psum", "vT_ready", "sc_psum", "sc_ready", "exp_ready", "prob_ready", "pT_psum", "pT_ready",
                "o_psum", "x_ready", "combined", "chain", "pos"))
            gat = [sem(f"a1_gathered{i}") for i in range(2)]
            T, S, A, O = banks[0:2], banks[2:4], banks[4:6], banks[6:8]
            LA, LB, LC = K0 + LN_LINKS, 1, 2
            PER = 2 * (LA + LB + LC)

            @block.gpsimd
            def _(pool):
                with pool.Fori(0, B // 2) as i:
                    for par in range(2):
                        n = i * 2 + par
                        pool.wait_ge(got_in, free(n))
                        nc.gpsimd.tensor_copy(pos_g[par][:], places[:, bass.ds(n * 6, 6)]).then_inc(b_pool, 1)
                        pool.wait_ge(b_pool, n + 1)
                        hold(pool, "pool")
                        for c in range(2 * K0):
                            nc.gpsimd.indirect_dma_start(
                                out=Yg[par][:, c, :], out_offset=None, in_=expert_rows,
                                in_offset=bass.IndirectOffsetOnAxis(ap=pos_g[par][:, c:c + 1], axis=0)).then_inc(gat[par], 16)

            @block.vector
            def _(dve):
                for s in (v_ready, vT_ready, sc_ready, pr_ready, x_ready, got_in):
                    dve.sem_inc(s, CREDIT)
                lnk = Chain(dve, b_dve)

                def by_head(ap):
                    return ap.rearrange("p t (s h) -> p t h s", h=HEADS)

                def per_head(ap):
                    return ap.rearrange("p t (o h) -> p t o h", o=1).broadcast_to([P, 2, L // HEADS, HEADS])

                with dve.Fori(0, B // 2) as i:
                    for par in range(2):
                        n = i * 2 + par
                        lnk.base, lnk.k = i * PER + par * LA, 0
                        dve.wait_ge(gat[par], i * 96 + 96)
                        for k in range(K0):
                            for j in range(2):
                                xj = X[:, bass.ds(n * TPB + j, 1), :].rearrange("p o d -> p (o d)")
                                ins = nc.vector.scalar_tensor_tensor(
                                    xj, Yg[par][:, j * K0 + k, :], gk[:, bass.ds(n * 6 + (j * K0 + k), 1)], xj, ALU.mult, ALU.add)
                            lnk(ins)
                        dve.sem_inc(got_in, 1)
                        dve.wait_ge(vT_psum, free(n))
                        layer_norm(dve, lnk, xt(n), ln_out[par][:], par, v_ready)
                        assert lnk.k == LA
                    for par in range(2):
                        n = i * 2 + par
                        dve.wait_ge(vT_psum, done(n))
                        dve.wait_ge(sc_psum, free(n))
                        nc.vector.tensor_copy(xT_s[par][:], T[par][:, 0:2 * P]).then_inc(vT_ready, 1)
                    for par in range(2):
                        n = i * 2 + par
                        lnk.base, lnk.k = i * PER + 2 * LA + par, 0
                        s = S[par][:, 0:2 * L].rearrange("p (t l) -> p t l", t=2)
                        dve.wait_ge(sc_psum, done(n))
                        lnk(nc.vector.tensor_reduce(mh[par], by_head(s), AX, ALU.max))
                        nc.vector.tensor_tensor(diff[par][:].rearrange("p t (s h) -> p t s h", h=HEADS),
                                                s.rearrange("p t (s h) -> p t s h", h=HEADS), per_head(mh[par]),
                                                ALU.subtract).then_inc(sc_ready, 1)
                    for par in range(2):
                        n = i * 2 + par
                        lnk.base, lnk.k = i * PER + 2 * LA + 2 + par * LC, 0
                        dve.wait_ge(ex_ready, done(n))
                        lnk(nc.vector.tensor_reduce(mh[par], by_head(diff[par][:]), AX, ALU.add))
                        lnk(nc.vector.reciprocal(mh[par], mh[par]))
                        dve.wait_ge(pT_psum, free(n))
                        nc.vector.tensor_tensor(prob[par][:].rearrange("p t (s h) -> p t s h", h=HEADS),
                                                diff[par][:].rearrange("p t (s h) -> p t s h", h=HEADS), per_head(mh[par]),
                                                ALU.mult).then_inc(pr_ready, 1)
                    for par in range(2):
                        n = i * 2 + par
                        dve.wait_ge(o_psum, done(n))
                        nc.vector.scalar_tensor_tensor(xt(n), O[par][:, 0:SEQ].rearrange("p (t d) -> p t d", t=2),
                                                       tg[:, 1:2], xt(n), ALU.mult, ALU.add).then_inc(x_ready, 1)

            @block.scalar
            def _(act):
                for s in (ex_ready, pT_ready):
                    act.sem_inc(s, CREDIT)
                with act.Fori(0, B // 2) as i:
                    for par in range(2):
                        n = i * 2 + par
                        act.wait_ge(sc_ready, done(n))
                        nc.scalar.activation(diff[par][:], diff[par][:], ACT.Exp).then_inc(ex_ready, 1)
                    for par in range(2):
                        n = i * 2 + par
                        act.wait_ge(pT_psum, done(n))
                        act.wait_ge(o_psum, free(n))
                        nc.scalar.copy(pTs[par][:], A[par][0:L, 0:SEQ]).then_inc(pT_ready, 1)

            @block.tensor
            def _(pe):
                mm = nc.tensor.matmul
                for s in (vT_psum, sc_psum, pT_psum, o_psum):
                    pe.sem_inc(s, CREDIT)
                with pe.Fori(0, B // 2) as i:
                    for par in range(2):
                        n = i * 2 + par
                        pe.wait_ge(v_ready, done(n))
                        pe.wait_ge(vT_ready, free(n))
                        for j in range(2):
                            ins = nc.tensor.transpose(T[par][:, j * P:(j + 1) * P], ln_out[par][:, j, :], ident)
                        ins.then_inc(vT_psum, 1)
                    for par in range(2):
                        n = i * 2 + par
                        pe.wait_ge(vT_ready, done(n))
                        pe.wait_ge(sc_ready, free(n))
                        for j in range(2):
                            o = S[par][:, j * L:(j + 1) * L]
                            mm(o, xT_s[par][:, j * P:(j + 1) * P], QK[:, bass.ds(n * L, L)], start=True, stop=False)
                            ins = mm(o, ones[0:1, :], srow[0:1, 1, bass.ds(n * L, L)], start=False, stop=True)
                        ins.then_inc(sc_psum, 1)
                    for par in range(2):
                        n = i * 2 + par
                        pe.wait_ge(pr_ready, done(n))
                        pe.wait_ge(pT_ready, free(n))
                        hold(pe, "pe")
                        for j in range(2):
                            ins = nc.tensor.transpose(A[par][0:L, j * P:(j + 1) * P], prob[par][:, j, :], ident)
                        ins.then_inc(pT_psum, 1)
                    for par in range(2):
                        n = i * 2 + par
                        pe.wait_ge(pT_ready, done(n))
                        pe.wait_ge(x_ready, free(n))
                        for j in range(2):
                            ins = mm(O[par][:, j * D:(j + 1) * D], pTs[par][:, j * P:(j + 1) * P],
                                     VO[:, bass.ds(n, 1), :].rearrange("p o d -> p (o d)"), start=True, stop=True)
                        ins.then_inc(o_psum, 1)

        idx1 = sb("idx1", [1, B * K1], I32)
        with nc.Block() as block:
            r_dve, w_ready, wt_psum, wt_saved, s_psum, s_read = (sem("r1_" + s) for s in (
                "chain", "w_ready", "wT_psum", "wT_saved", "s_psum", "s_read"))
            TU, LG = banks[0:2], banks[2:4]
            LA, LB = LN_LINKS + 2, 3
            PER = 2 * (LA + LB)

            @block.vector
            def _(dve):
                for s in (w_ready, s_read):
                    dve.sem_inc(s, CREDIT)
                lnk = Chain(dve, r_dve)
                with dve.Fori(0, B // 2) as i:
                    for par in range(2):
                        n = i * 2 + par
                        lnk.base, lnk.k = i * PER + par * LA, 0
                        layer_norm(dve, lnk, xt(n), ln_out[par][:], par, None)
                        dve.wait_ge(wt_psum, free(n))
                        hi, lo = u16[par][:, :, 0:D], u16[par][:, :, D:2 * D]
                        lnk(nc.vector.tensor_scalar(hi, ln_out[par][:], SU, None, ALU.mult))
                        nc.vector.scalar_tensor_tensor(lo, ln_out[par][:], SU, hi, ALU.mult, ALU.subtract).then_inc(w_ready, 1)
                        assert lnk.k == LA
                    for par in range(2):
                        n = i * 2 + par
                        lnk.base, lnk.k = i * PER + 2 * LA + par * LB, 0
                        dve.wait_ge(s_psum, done(n))
                        lnk(nc.vector.tensor_scalar(lg[par][0:1, 0, 0:E1], LG[par][0:1, 0:E1], UN1, None, ALU.mult))
                        hold(dve, "dve")
                        lnk(nc.vector.max(v8[par][0:1, 0, :], lg[par][0:1, 0, 0:E1]))
                        hold(dve, "dve")
                        lnk(nc.vector.max_index(i8[par][0:1, 0, :], v8[par][0:1, 0, :], lg[par][0:1, 0, 0:E1]))
                        nc.vector.tensor_copy(idx1[0:1, bass.ds(n * K1, K1)], i8[par][0:1, 0, 0:K1]).then_inc(s_read, 1)

            @block.scalar
            def _(act):
                act.sem_inc(wt_saved, CREDIT)
                with act.Fori(0, B // 2) as i:
                    for par in range(2):
                        n = i * 2 + par
                        act.wait_ge(wt_psum, done(n))
                        nc.scalar.copy(uT[:, :, bass.ds(n * SEQ, SEQ)],
                                       TU[par][:, 0:SEQ].bitcast(F16).rearrange("p (h t) -> p h t", h=2)).then_inc(wt_saved, 1)

            @block.tensor
            def _(pe):
                mm = nc.tensor.matmul
                for s in (wt_psum, s_psum):
                    pe.sem_inc(s, CREDIT)
                with pe.Fori(0, B // 2) as i:
                    for par in range(2):
                        n = i * 2 + par
                        pe.wait_ge(w_ready, done(n))
                        pe.wait_ge(wt_saved, free(n))
                        t16 = TU[par][:, 0:SEQ].bitcast(F16)
                        for j in range(2):
                            for h in range(2):
                                ins = nc.tensor.transpose(t16[:, h * SEQ + j * P:h * SEQ + (j + 1) * P],
                                                          u16[par][:, j, h * D:(h + 1) * D], ident16[:])
                        ins.then_inc(wt_psum, 1)
                    for par in range(2):
                        n = i * 2 + par
                        pe.wait_ge(wt_saved, done(n))
                        pe.wait_ge(s_read, free(n))
                        o = LG[par][:, 0:E1]
                        uh, ul = (uT[:, h, bass.ds(n * SEQ, P)] for h in range(2))
                        mm(o, uh, wr16[:, 0, :], start=True, stop=False)
                        mm(o, uh, wr16[:, 1, :], start=False, stop=False)
                        mm(o, ul, wr16[:, 0, :], start=False, stop=False)
                        mm(o, ones[0:1, :], rows[0:1, 3, 0:E1], start=False, stop=True).then_inc(s_psum, 1)

        xo = [AT[:, 1024 + 512 * k:1280 + 512 * k].rearrange("p (t d) -> p t d", t=2) for k in range(2)]
        with nc.Block() as block:
            m_h, m_hf, m_lo, m_y, m_x, m_lk = (sem("m1_" + s) for s in ("h_psum", "gelu", "split", "y_psum", "x", "chain"))
            m_st = [sem(f"m1_stored{i}") for i in range(2)]
            HB, YB = banks[0:2], banks[2:4]

            def chosen(eng, n, k):
                return eng.value_load(idx1[0:1, bass.ds(n * K1 + k, 1)], min_val=0, max_val=E1 - 1)

            @block.tensor
            def _(pe):
                mm = nc.tensor.matmul
                for s in (m_h, m_y):
                    pe.sem_inc(s, CREDIT)

                def hidden(n, par):
                    pe.wait_ge(m_hf, free(n))
                    hold(pe, "pe")
                    uh, ul = (uT[:, h, bass.ds(n * SEQ, SEQ)] for h in range(2))
                    for k in range(K1):
                        e = chosen(pe, n, k)
                        wh, wl = (M1[:, h, bass.ds(e, 1), :].rearrange("p o f -> p (o f)") for h in range(2))
                        o = HB[par][:, k * SEQ:(k + 1) * SEQ]
                        mm(o, wh, uh, start=True, stop=False)
                        mm(o, wh, ul, start=False, stop=False)
                        ins = mm(o, wl, uh, start=False, stop=True)
                    ins.then_inc(m_h, 1)

                def outputs(n, par):
                    pe.wait_ge(m_lo, done(n))
                    pe.wait_ge(m_x, free(n))
                    hold(pe, "pe")
                    for j in range(2):
                        o = YB[par][:, j * D:(j + 1) * D]
                        for k in range(K1):
                            e = chosen(pe, n, k)
                            hh, hl = (hs[par][:, h, k * SEQ + j * P:k * SEQ + (j + 1) * P] for h in range(2))
                            wh, wl = (M2[:, h, bass.ds(e, 1), :].rearrange("p o f -> p (o f)") for h in range(2))
                            mm(o, hh, wh, start=(k == 0), stop=False)
                            mm(o, hh, wl, start=False, stop=False)
                            mm(o, hl, wh, start=False, stop=False)
                            ins = mm(o, ones[0:1, :], b2m[0:1, bass.ds(e, 1), :].rearrange("p o d -> p (o d)"),
                                     start=False, stop=(k == K1 - 1))
                    ins.then_inc(m_y, 1)

                hidden(0, 0)
                with pe.Fori(0, B // 2 - 1) as i:
                    for par in range(2):
                        hidden(i * 2 + 1 + par, 1 - par)
                        outputs(i * 2 + par, par)
                hidden(B - 1, 1)
                outputs(B - 2, 0)
                outputs(B - 1, 1)

            @block.scalar
            def _(act):
                act.sem_inc(m_hf, CREDIT)
                with act.Fori(0, B // 2) as i:
                    for par in range(2):
                        n = i * 2 + par
                        act.wait_ge(m_h, done(n))
                        act.wait_ge(m_lo, free(n))
                        hold(act, "act")
                        for k in range(K1):
                            e = chosen(act, n, k)
                            ins = nc.scalar.activation(hf[par][:, k * SEQ:(k + 1) * SEQ], HB[par][:, k * SEQ:(k + 1) * SEQ],
                                                       ACT.Gelu, bias=cols[:, bass.ds(e + V_B1, 1)], scale=UN1)
                        ins.then_inc(m_hf, 1)

            @block.vector
            def _(dve):
                for s in (m_lo, m_x):
                    dve.sem_inc(s, CREDIT)
                lnk = Chain(dve, m_lk)

                def split(n, par):
                    lnk.base, lnk.k = n, 0
                    dve.wait_ge(m_hf, done(n))
                    dve.wait_ge(m_y, free(n))
                    lnk(nc.vector.tensor_scalar(hs[par][:, 0, :], hf[par], SH, None, ALU.mult))
                    nc.vector.scalar_tensor_tensor(hs[par][:, 1, :], hf[par], SH, hs[par][:, 0, :],
                                                   ALU.mult, ALU.subtract).then_inc(m_lo, 1)

                def add(n, par):
                    dve.wait_ge(m_y, done(n))
                    nc.vector.scalar_tensor_tensor(xt(n), YB[par][:, 0:SEQ].rearrange("p (t d) -> p t d", t=2),
                                                   tgs[:, 1:2], xt(n), ALU.mult, ALU.add).then_inc(m_x, 1)

                split(0, 0)
                with dve.Fori(0, B // 2 - 1) as i:
                    for par in range(2):
                        split(i * 2 + 1 + par, 1 - par)
                        add(i * 2 + par, par)
                split(B - 1, 1)
                add(B - 2, 0)
                add(B - 1, 1)

            @block.sync
            def _(sp):
                out_v = out.rearrange("b (t p) d -> p (b t) d", p=P)
                with sp.Fori(0, B) as n:
                    sp.wait_ge(m_x, done(n))
                    sp.dma_start(out_v[:, bass.ds(n * TPB, TPB), :], xt(n)).then_inc(m_st[0], 16)
                sp.wait_ge(m_st[0], 16 * B)


_INS = ['x', 'ctx_1024', 'g_xattn', 'g_ffn', 'L0_xattn_w_sim', 'L0_xattn_b_sim', 'L0_xattn_W_qv', 'L0_xattn_b_qv',
        'L0_ffn_sW1', 'L0_ffn_sb1', 'L0_ffn_sW2', 'L0_ffn_sb2', 'L0_ffn_rW1', 'L0_ffn_rb1', 'L0_ffn_rW2',
        'L0_ffn_rb2', 'L0_ffn_gW', 'L0_ffn_gb', 'L1_xattn_Wq', 'L1_xattn_bq', 'L1_xattn_Wk', 'L1_xattn_bk',
        'L1_xattn_Wv', 'L1_xattn_bv', 'L1_xattn_Wo', 'L1_xattn_bo', 'L1_ffn_Wr', 'L1_ffn_br', 'L1_ffn_W1',
        'L1_ffn_b1', 'L1_ffn_W2', 'L1_ffn_b2']


def constants():
    import numpy as np
    c = np.zeros((P, NCONST), np.float32)
    c[:, C_ID:C_ID + P] = np.eye(P)
    c[:, C_TRI:C_TRI + P] = np.triu(np.ones((P, P)), 1)
    c[:, C_MASK:C_MASK + L] = np.arange(P)[:, None] // HD == np.arange(L)[None, :] % HEADS
    c[:, C_IOTA:C_IOTA + 6 * E0] = np.tile(np.arange(E0), 6)
    c[:, C_BASE:C_BASE + E0] = np.arange(E0) * REGION
    c[:, C_LE:C_LE + E0 * E0] = np.tril(np.ones((E0, E0))).reshape(-1)
    c[:, C_PART] = np.arange(P)
    return c


def kernel(**inputs):
    import numpy as np
    import concourse.bacc as bacc
    from concourse.bass_utils import run_bass_kernel_spmd as run

    nc = bacc.Bacc("TRN2", target_bir_lowering=False, num_devices=1)
    arrays, aps = {}, {}
    for name in _INS:
        arr = np.ascontiguousarray(inputs[name])
        arrays["in_" + name] = arr
        aps[name] = nc.dram_tensor("in_" + name, arr.shape, mybir.dt.from_np(arr.dtype), kind="ExternalInput").ap()
    arrays["in_const"] = constants()
    const = nc.dram_tensor("in_const", (P, NCONST), F32, kind="ExternalInput").ap()
    out = nc.dram_tensor("out", (B, SEQ, D), F32, kind="ExternalOutput").ap()
    build(nc, aps, const, out)
    return run(nc, [arrays], core_ids=[0]).results[0]["out"]
```

```python
from contextlib import ExitStack

import concourse.bass as bass
from concourse import mybir

F32 = mybir.dt.float32
F16 = mybir.dt.float16
I32 = mybir.dt.int32
U32 = mybir.dt.uint32
ALU = mybir.AluOpType
ACT = mybir.ActivationFunctionType
AX = mybir.AxisListType.X

P = 128
B = 16
SEQ = 256
TPB = SEQ // P
NT = B * TPB
TOK = B * SEQ
TQ = 4
NQ = NT // TQ
QTOK = TQ * P
D = 128
L = 64
HEADS = 8
HD = D // HEADS
E0 = 15
F0 = 256
K0 = 3
FS = 512
E1 = 8
K1 = 2
EPS = 1e-5

SU = 256.0
SW = 1024.0
SH = 64.0
UN1 = 1.0 / (SU * SW)
UN2 = 1.0 / (SH * SW)

BLK = 256
REGION = TOK + BLK
BLOCKS = (TOK * K0) // BLK + E0 + 1
ROWS = E0 * REGION + BLK
WEW = F0 + 2 * D + 2

V_WSIM, V_BQ, V_BK, V_BV, V_RB1, V_SB1, V_B1 = 0, 3, 4, 5, 6, 36, 40
NVEC = 48
C_ID, C_TRI, C_MASK, C_IOTA, C_BASE, C_LE, C_PART = 0, 128, 256, 320, 410, 425, 650
NCONST = 651

CREDIT = 2


def done(n):
    return n + 1 + CREDIT


def free(n):
    return n + 1


def pipelined(eng, *stages):
    first = max(lag for lag, _ in stages)
    pairs = (NQ - first) // 2

    def step(s, static, use):
        for lag, stage in stages:
            if 0 <= static - lag < NQ:
                q = static - lag
                stage(s - lag, q % 2, use + q // 2)

    for s in range(first):
        step(s, s, 0)
    with eng.Fori(0, pairs) as i:
        for u in range(2):
            step(i * 2 + (first + u), first + u, i)
    for s in range(first + 2 * pairs, NQ + first):
        step(s, s, 0)


class Chain:

    def __init__(self, eng, sem):
        self.eng, self.sem, self.base, self.k = eng, sem, 0, 0

    def start(self, count):
        self.base, self.k = count, 0

    def __call__(self, ins):
        ins.then_inc(self.sem, 1)
        self.k += 1
        self.eng.wait_ge(self.sem, self.base + self.k)


def build(nc, a, const, out):
    with ExitStack() as ctx:
        def sb(name, shape, dt=F32):
            return ctx.enter_context(nc.sbuf_tensor(name, shape, dt))

        def sem(name):
            return ctx.enter_context(nc.semaphore(name))

        banks = [ctx.enter_context(nc.psum_tensor(f"bank{i}", [P, 512], F32)) for i in range(8)]

        sorted_rows = nc.dram_tensor("sorted_rows", (ROWS, 2 * D), F16, kind="Internal").ap()
        expert_rows = nc.dram_tensor("expert_rows", (BLOCKS * BLK, D), F32, kind="Internal").ap()

        X = sb("X", [P, NT, D])
        hc = sb("hc", [P, NT, D])
        hcT = sb("hcT", [P, TOK])
        AT = sb("AT", [P, TOK])
        uT = sb("uT", [P, 2, TOK], F16)

        cst = sb("cst", [P, NCONST])
        ident = cst[:, C_ID:C_ID + P]
        ident16 = sb("ident16", [P, P], F16)
        tri16 = sb("tri16", [P, P], F16)
        ones16 = sb("ones16", [P, P], F16)
        ones = sb("ones", [P, P])
        vecs = sb("vecs", [NVEC, P])
        cols = sb("cols", [P, NVEC])
        rows = sb("rows", [1, 4, P])
        gates = sb("gates", [P, 4])
        tg = sb("tg", [P, 4])
        bsim = sb("bsim", [1, 1])

        early = uT[:].rearrange("p h t -> p (h t)").bitcast(F32)
        ctxk = early[:, 0:1024].rearrange("p (t d) -> p t d", d=D)
        ctxT = early[:, 1024:2048]
        VmT = early[:, 2048:3072]
        Wa = early[:, 3072:3584].rearrange("p (w d) -> p w d", d=D)
        WqT = early[:, 3584:3712]
        MT = sb("MT", [P, B * L])
        KmT = sb("KmT", [P, B * L])
        QK = sb("QK", [P, B * L])
        srow = sb("srow", [1, 2, B * L])
        HW1 = sb("HW1", [L, B, D])
        VO = sb("VO", [L, B, D])
        Wqv = sb("Wqv", [P, 4, D])

        WE = sb("WE", [P, E0, WEW])
        WE16 = WE[:].rearrange("p e w -> p (e w)").bitcast(F16).rearrange("p (e w) -> p e w", e=E0)
        W1 = WE16[:, :, 0:2 * F0].rearrange("p e (h f) -> p h e f", h=2)
        W2 = WE16[:, :, 2 * F0:2 * F0 + 4 * D].rearrange("p e (h f) -> p h e f", h=2)
        S1 = sb("S1", [P, 2, FS], F16)
        S2 = sb("S2", [P, 2, FS], F16)
        M1 = sb("M1", [P, 2, E1, D], F16)
        M2 = sb("M2", [P, 2, E1, D], F16)
        gw = sb("gw", [P, E0])
        gw16 = sb("gw16", [P, 2, E0 + 1], F16)
        wr = sb("wr", [P, E1])
        wr16 = sb("wr16", [P, 2, E1], F16)
        b2a = sb("b2a", [E0 + 1, D])
        b2m = sb("b2m", [1, E1, D])

        st_W1 = hcT[:, 0:E0 * F0].rearrange("p (e f) -> p e f", e=E0)
        st_W2 = hc[:].rearrange("p t d -> p (t d)")[:, 0:E0 * 2 * D].rearrange("p (e f) -> p e f", e=E0)
        st_S1 = AT[:, 0:512]
        st_S2 = AT[:, 512:1024]
        st_M1 = AT[:, 1024:2048].rearrange("p (e f) -> p e f", e=E1)
        st_M2 = AT[:, 2048:3072].rearrange("p (e f) -> p e f", e=E1)

        stats = sb("stats", [P, TQ, 6])
        mv = [sb(f"mv{i}", [P, TQ, 2]) for i in range(2)]
        rs = [sb(f"rs{i}", [P, 5, TQ]) for i in range(2)]

        def pair(name, shape, dt=F32):
            return [sb(f"{name}{i}", shape, dt) for i in range(2)]

        LN_LINKS = 11

        def row_scales(dve, link, x, par, done_sem):
            hold(dve, "dve")
            for j in range(TQ):
                ins = nc.vector.bn_stats(stats[:, j, :], x[:, j, :])
            link(ins)
            hold(dve, "dve")
            for j in range(TQ):
                ins = nc.vector.bn_aggr(mv[par][:, j, :], stats[:, j, :])
            link(ins)
            v, y, t, w, shift = (rs[par][:, i, :] for i in range(5))
            link(nc.vector.tensor_scalar(v, mv[par][:, :, 1], EPS, None, ALU.add))
            link(nc.vector.tensor_scalar(t.bitcast(I32), v.bitcast(I32), 1, None, ALU.logical_shift_right))
            link(nc.vector.tensor_scalar(y.bitcast(I32), t.bitcast(I32), -1.0, float(0x5f1ffff9), ALU.mult, ALU.add))
            for b, c in ((0.703952253, 0.703952253 * 2.38924456), (0.5 * (1 + 3.2e-7), 1.5 * (1 + 3.2e-7))):
                link(nc.vector.scalar_tensor_tensor(t, y, -b, y, ALU.mult, ALU.mult))
                link(nc.vector.tensor_tensor(w, t, v, ALU.mult))
                link(nc.vector.scalar_tensor_tensor(y, w, c, y, ALU.add, ALU.mult))
            nc.vector.scalar_tensor_tensor(shift, mv[par][:, :, 0], -1.0, y, ALU.mult, ALU.mult).then_inc(done_sem, 1)

        def normalise_rows(x, dst, par):
            for j in range(TQ):
                ins = nc.scalar.activation(dst[:, j, :], x[:, j, :], ACT.Identity,
                                           bias=rs[par][:, 4, j:j + 1], scale=rs[par][:, 1, j:j + 1])
            return ins

        held = {e: sem("held_" + e) for e in ("pe", "dve", "act", "pool", "sp")}

        def hold(eng, name):
            eng.sem_inc(held[name], 1)

        def xt(n):
            return X[:, bass.ds(n * TPB, TPB), :]

        def xq(n):
            return X[:, bass.ds(n * TQ, TQ), :]

        def tiles(ap):
            return ap.rearrange("p (t d) -> p t d", t=TQ)

        def spread(ap, width):
            return ap.rearrange("p (t o) -> p t o", o=1).broadcast_to([P, TQ, width])

        ld_small, ld_ctx, ld_x, ld_wa, ld_w = (sem(s) for s in ("ld_small", "ld_ctx", "ld_x", "ld_wa", "ld_w"))
        s_pe, s_dve, s_act, s_pool, s_consts = (
            sem(s) for s in ("setup_pe", "setup_dve", "setup_act", "setup_pool", "setup_consts"))
        zeros = sb("zeros", [P, 4 * D], F16)
        with nc.Block() as block:
            @block.sync
            def _(sp):
                sp.dma_start(cst[:], const).then_inc(ld_small, 16)
                r = [(V_WSIM, 3, a["L0_xattn_w_sim"].rearrange("(r c) -> r c", c=P)),
                     (V_BQ, 1, a["L1_xattn_bq"].rearrange("(r c) -> r c", c=P)),
                     (V_BK, 1, a["L1_xattn_bk"].rearrange("(r c) -> r c", c=P)),
                     (V_BV, 1, a["L1_xattn_bv"].rearrange("(r c) -> r c", c=P)),
                     (V_RB1, 30, a["L0_ffn_rb1"].rearrange("e (r c) -> (e r) c", c=P)),
                     (V_SB1, 4, a["L0_ffn_sb1"].rearrange("e (r c) -> (e r) c", c=P)),
                     (V_B1, 8, a["L1_ffn_b1"])]
                for at, n, src in r:
                    sp.dma_start(vecs[at:at + n, :], src).then_inc(ld_small, 16)
                for i, (name, n) in enumerate((("L0_xattn_b_qv", D), ("L1_xattn_bo", D), ("L0_ffn_gb", E0),
                                               ("L1_ffn_br", E1))):
                    sp.dma_start(rows[:, i, 0:n], a[name].rearrange("(r c) -> r c", r=1)).then_inc(ld_small, 16)
                sp.dma_start(bsim[:], a["L0_xattn_b_sim"].rearrange("(r c) -> r c", r=1)).then_inc(ld_small, 16)
                for i, name in enumerate(("g_xattn", "g_ffn")):
                    sp.dma_start(gates[:, 2 * i:2 * i + 2],
                                 a[name].rearrange("(r c) -> r c", r=1).broadcast_to([P, 2])).then_inc(ld_small, 16)
                sp.dma_start(gw[:], a["L0_ffn_gW"]).then_inc(ld_small, 16)
                sp.dma_start(wr[:], a["L1_ffn_Wr"]).then_inc(ld_small, 16)
                sp.dma_start(b2a[0:E0, :], a["L0_ffn_rb2"]).then_inc(ld_small, 16)
                sp.dma_start(b2a[E0:E0 + 1, :], a["L0_ffn_sb2"]).then_inc(ld_small, 16)
                sp.dma_start(b2m[:], a["L1_ffn_b2"].rearrange("(o e) d -> o e d", o=1)).then_inc(ld_small, 16)

            N_SMALL = 20

            @block.gpsimd
            def _(pool):
                nc.gpsimd.memset(zeros[:], 0.0)
                nc.gpsimd.memset(ones[:], 1.0).then_inc(s_pool, 1)
                nc.gpsimd.memset(ones16[:], 1.0).then_inc(s_pool, 1)
                pool.wait_ge(ld_small, 16 * N_SMALL)
                nc.gpsimd.tensor_copy(ident16[:], ident).then_inc(s_pool, 1)
                nc.gpsimd.tensor_copy(tri16[:], cst[:, C_TRI:C_TRI + P]).then_inc(s_pool, 1)

            @block.scalar
            def _(act):
                act.dma_start(ctxk, a["ctx_1024"].rearrange("(t b) s d -> (b s) t d", b=P // L)).then_inc(ld_ctx, 16)
                act.dma_start(Wqv[:], a["L0_xattn_W_qv"].rearrange("(c p) d -> p c d", p=P)).then_inc(ld_wa, 16)
                for i, name in enumerate(("L1_xattn_Wq", "L1_xattn_Wk", "L1_xattn_Wv", "L1_xattn_Wo")):
                    act.dma_start(Wa[:, i, :], a[name]).then_inc(ld_wa, 16)
                act.dma_start(st_W1, a["L0_ffn_rW1"].rearrange("e p f -> p e f")).then_inc(ld_w, 16)
                act.dma_start(st_W2.rearrange("p e (c d) -> p e c d", c=2),
                              a["L0_ffn_rW2"].rearrange("e (c p) d -> p e c d", p=P)).then_inc(ld_w, 16)
                act.dma_start(st_S1, a["L0_ffn_sW1"].rearrange("e p f -> p (e f)")).then_inc(ld_w, 16)
                act.dma_start(st_S2.rearrange("p (c d) -> p c d", c=4),
                              a["L0_ffn_sW2"].rearrange("e (c p) d -> p (e c) d", p=P)).then_inc(ld_w, 16)
                act.dma_start(st_M1, a["L1_ffn_W1"].rearrange("e p f -> p e f")).then_inc(ld_w, 16)
                act.dma_start(st_M2, a["L1_ffn_W2"].rearrange("e p f -> p e f")).then_inc(ld_w, 16)
                for g in range(4):
                    act.dma_start(X[:, 8 * g:8 * g + 8, :],
                                  a["x"].rearrange("b (t p) d -> p (b t) d", p=P)[:, 8 * g:8 * g + 8, :]).then_inc(ld_x, 16)
                act.wait_ge(ld_small, 16 * N_SMALL)
                nc.scalar.activation(tg[:], gates[:], ACT.Tanh).then_inc(s_consts, 1)
                act.wait_ge(ld_w, 16 * 6)
                for dst, src in ((W1, st_W1), (W2, st_W2), (S1, st_S1), (S2, st_S2), (M1, st_M1), (M2, st_M2)):
                    nc.scalar.activation(dst[:, 0], src, ACT.Copy, scale=SW).then_inc(s_act, 1)

            @block.vector
            def _(dve):
                link = Chain(dve, s_dve)
                dve.wait_ge(ld_small, 16 * N_SMALL)
                nc.vector.tensor_scalar(gw16[:, 0, 0:E0], gw[:], SW, None, ALU.mult)
                nc.vector.tensor_scalar(rows[:, 1, :], rows[:, 1, :], 1.0 / HEADS, None, ALU.mult)
                nc.vector.tensor_scalar(rows[:, 2, 0:E0], rows[:, 2, 0:E0], SU * SW, None, ALU.mult)
                nc.vector.tensor_scalar(rows[:, 3, 0:E1], rows[:, 3, 0:E1], SU * SW, None, ALU.mult)
                nc.vector.tensor_scalar(b2a[:], b2a[:], SH * SW, None, ALU.mult)
                nc.vector.tensor_scalar(b2m[:], b2m[:], SH * SW, None, ALU.mult)
                link(nc.vector.tensor_scalar(wr16[:, 0, :], wr[:], SW, None, ALU.mult))
                nc.vector.scalar_tensor_tensor(gw16[:, 1, 0:E0], gw[:], SW, gw16[:, 0, 0:E0], ALU.mult, ALU.subtract)
                link(nc.vector.scalar_tensor_tensor(wr16[:, 1, :], wr[:], SW, wr16[:, 0, :], ALU.mult, ALU.subtract))
                dve.wait_ge(s_pe, 1)
                link(nc.vector.tensor_copy(cols[:], banks[0][:, 0:NVEC]))
                nc.vector.tensor_copy(WE[:, :, F0 + 2 * D:WEW],
                                      cols[:, V_RB1:V_RB1 + 2 * E0].rearrange("p (e c) -> p e c", c=2))
                dve.wait_ge(s_pe, 2)
                link(nc.vector.tensor_copy(WqT, banks[1][:, 0:D]))
                for h in range(2):
                    dve.wait_ge(s_pe, 3 + h)
                    link(nc.vector.tensor_copy(ctxT[:, 512 * h:512 * h + 512], banks[2 + h][:]))
                link(nc.vector.tensor_scalar(MT[:], ctxT, cols[:, V_WSIM + 2:V_WSIM + 3],
                                             cols[:, V_WSIM:V_WSIM + 1], ALU.mult, ALU.add))
                mask = cst[:, C_MASK:C_MASK + L].rearrange("p (o s) -> p o s", o=1).broadcast_to([P, 8, L])
                for h in range(2):
                    dve.wait_ge(s_pe, 5 + h)
                    link(nc.vector.scalar_tensor_tensor(
                        KmT[:, 512 * h:512 * h + 512].rearrange("p (b s) -> p b s", s=L),
                        banks[4 + h][:].rearrange("p (b s) -> p b s", s=L),
                        cols[:, V_BK:V_BK + 1], mask, ALU.add, ALU.mult))
                link(nc.vector.tensor_scalar(KmT[:], KmT[:], float(HD) ** -0.5, None, ALU.mult))
                for h in range(2):
                    dve.wait_ge(s_pe, 7 + h)
                    link(nc.vector.scalar_tensor_tensor(
                        VmT[:, 512 * h:512 * h + 512].rearrange("p (b s) -> p b s", s=L),
                        banks[6 + h][:].rearrange("p (b s) -> p b s", s=L),
                        cols[:, V_BV:V_BV + 1], mask, ALU.add, ALU.mult))
                for h in range(2):
                    dve.wait_ge(s_pe, 9 + h)
                    link(nc.vector.tensor_scalar(srow[0:1, 0, 512 * h:512 * h + 512], banks[h][0:1, :], bsim[0:1, 0:1],
                                                 None, ALU.add))
                for h in range(2):
                    dve.wait_ge(s_pe, 11 + h)
                    link(nc.vector.tensor_copy(srow[0:1, 1, 512 * h:512 * h + 512], banks[2 + h][0:1, :]))
                for h in range(2):
                    dve.wait_ge(s_pe, 13 + h)
                    link(nc.vector.tensor_copy(QK[:, 512 * h:512 * h + 512], banks[4 + h][:]))
                for q in range(4):
                    dve.wait_ge(s_pe, 15 + q)
                    link(nc.vector.tensor_copy(HW1[:, 4 * q:4 * q + 4, :],
                                               banks[q][0:L, :].rearrange("p (b d) -> p b d", d=D)))
                for q in range(4):
                    dve.wait_ge(s_pe, 19 + q)
                    link(nc.vector.tensor_copy(VO[:, 4 * q:4 * q + 4, :],
                                               banks[4 + q][0:L, :].rearrange("p (b d) -> p b d", d=D)))
                dve.wait_ge(s_act, 6)
                for dst, src in ((W1, st_W1), (W2, st_W2), (S1, st_S1), (S2, st_S2), (M1, st_M1), (M2, st_M2)):
                    ins = nc.vector.scalar_tensor_tensor(dst[:, 1], src, SW, dst[:, 0], ALU.mult, ALU.subtract)
                link(ins)
                dve.wait_ge(ld_x, 16 * 4)

            @block.tensor
            def _(pe):
                mm = nc.tensor.matmul
                pe.wait_ge(ld_small, 16 * N_SMALL)
                pe.wait_ge(s_pool, 4)
                nc.tensor.transpose(banks[0][:, 0:NVEC], vecs[:], ident[0:NVEC, 0:NVEC]).then_inc(s_pe, 1)
                pe.wait_ge(ld_wa, 16 * 5)
                nc.tensor.transpose(banks[1][:, 0:D], Wa[:, 0, :], ident).then_inc(s_pe, 1)
                pe.wait_ge(ld_ctx, 16)
                for h in range(2):
                    for t in range(4):
                        ins = nc.tensor.transpose(banks[2 + h][:, t * P:(t + 1) * P], ctxk[:, 4 * h + t, :], ident)
                    ins.then_inc(s_pe, 1)
                pe.wait_ge(s_dve, 6)
                for h in range(2):
                    mm(banks[4 + h][:], Wa[:, 1, :], ctxT[:, 512 * h:512 * h + 512], start=True, stop=True).then_inc(s_pe, 1)
                for h in range(2):
                    mm(banks[6 + h][:], Wa[:, 2, :], ctxT[:, 512 * h:512 * h + 512], start=True, stop=True).then_inc(s_pe, 1)
                for h in range(2):
                    mm(banks[h][0:1, :], cols[:, V_WSIM + 1:V_WSIM + 2], ctxT[:, 512 * h:512 * h + 512],
                       start=True, stop=True).then_inc(s_pe, 1)
                pe.wait_ge(s_dve, 10)
                for h in range(2):
                    mm(banks[2 + h][0:1, :], cols[:, V_BQ:V_BQ + 1], KmT[:, 512 * h:512 * h + 512],
                       start=True, stop=True).then_inc(s_pe, 1)
                for h in range(2):
                    mm(banks[4 + h][:], WqT, KmT[:, 512 * h:512 * h + 512], start=True, stop=True).then_inc(s_pe, 1)
                for q in range(4):
                    pe.wait_ge(s_dve, 13 + q)
                    for b in range(4 * q, 4 * q + 4):
                        o = banks[q][0:L, (b % 4) * D:(b % 4 + 1) * D]
                        mm(o, ctxT[:, b * L:(b + 1) * L], Wqv[:, 1, :], start=True, stop=False)
                        ins = mm(o, ones[0:1, 0:L], rows[0:1, 0, :], start=False, stop=True)
                    ins.then_inc(s_pe, 1)
                for q in range(4):
                    pe.wait_ge(s_dve, 18)
                    for b in range(4 * q, 4 * q + 4):
                        o = banks[4 + q][0:L, (b % 4) * D:(b % 4 + 1) * D]
                        mm(o, VmT[:, b * L:(b + 1) * L], Wa[:, 3, :], start=True, stop=False)
                        ins = mm(o, ones[0:1, 0:L], rows[0:1, 1, :], start=False, stop=True)
                    ins.then_inc(s_pe, 1)

        uTf = uT[:].rearrange("p h t -> p (h t)").bitcast(F32)
        diff = [tiles(uTf[:, 256 * k:256 * k + 256]) for k in range(2)]
        prob = [tiles(uTf[:, 512 + 256 * k:768 + 256 * k]) for k in range(2)]
        ln_out, xT_s = pair("ln_out", [P, TQ, D]), pair("xT_s", [P, QTOK])
        m_all = sb("m_all", [P, NT])
        den = pair("den", [P, TQ])

        with nc.Block() as block:
            (hc_ready, hc_saved, hcT_psum, hcT_ready, hcT_saved, sim_psum, diff_ready, exp_ready, prob_ready,
             AT_psum, AT_saved, a0_scales, a0_ln, a0_max, a0_sum) = (sem("a0_" + s) for s in (
                "hc_ready", "hc_saved", "hcT_psum", "hcT_ready", "hcT_saved", "sim_psum", "diff_ready", "exp_ready",
                "prob_ready", "AT_psum", "AT_saved", "row_scales", "ln_chain", "max_chain", "sum_chain"))
            T, S, A = banks[0:2], banks[2:4], banks[4:6]

            @block.gpsimd
            def _(pool):
                pool.sem_inc(hc_saved, CREDIT)

                def save(n, par, use):
                    pool.wait_ge(hc_ready, done(n))
                    nc.gpsimd.tensor_copy(hc[:, bass.ds(n * TQ, TQ), :], ln_out[par][:]).then_inc(hc_saved, 1)

                pipelined(pool, (0, save))

            @block.vector
            def _(dve):
                for s in (a0_scales, diff_ready, prob_ready):
                    dve.sem_inc(s, CREDIT)
                ln_link, max_link, sum_link = Chain(dve, a0_ln), Chain(dve, a0_max), Chain(dve, a0_sum)

                def scales(n, par, use):
                    ln_link.start(n * (LN_LINKS))
                    dve.wait_ge(hc_ready, free(n))
                    row_scales(dve, ln_link, xq(n), par, a0_scales)

                def less_maximum(n, par, use):
                    max_link.start(n)
                    s = tiles(S[par][:, 0:TQ * L])
                    dve.wait_ge(sim_psum, done(n))
                    m = m_all[:, bass.ds(n * TQ, TQ)]
                    max_link(nc.vector.tensor_reduce(m, s, AX, ALU.max))
                    nc.vector.tensor_tensor(diff[par], s, spread(m, L), ALU.subtract).then_inc(diff_ready, 1)

                def probabilities(n, par, use):
                    sum_link.start(2 * n)
                    dve.wait_ge(exp_ready, done(n))
                    sum_link(nc.vector.tensor_reduce(den[par][:], diff[par], AX, ALU.add))
                    sum_link(nc.vector.reciprocal(den[par][:], den[par][:]))
                    dve.wait_ge(AT_psum, free(n))
                    nc.vector.tensor_tensor(prob[par], diff[par], spread(den[par][:], L), ALU.mult).then_inc(prob_ready, 1)

                pipelined(dve, (2, probabilities), (0, scales), (1, less_maximum))

            @block.scalar
            def _(act):
                for s in (hc_ready, hcT_ready, hcT_saved, exp_ready, AT_saved):
                    act.sem_inc(s, CREDIT)

                def normalise(n, par, use):
                    act.wait_ge(a0_scales, done(n))
                    act.wait_ge(hc_saved, free(n))
                    act.wait_ge(hcT_psum, free(n))
                    normalise_rows(xq(n), ln_out[par], par).then_inc(hc_ready, 1)

                def exponentials(n, par, use):
                    act.wait_ge(diff_ready, done(n))
                    nc.scalar.activation(diff[par], diff[par], ACT.Exp).then_inc(exp_ready, 1)

                def save_tokens(n, par, use):
                    act.wait_ge(hcT_psum, done(n))
                    act.wait_ge(sim_psum, free(n))
                    nc.scalar.copy(xT_s[par][:], T[par][:]).then_inc(hcT_ready, 1)
                    nc.scalar.copy(hcT[:, bass.ds(n * QTOK, QTOK)], T[par][:]).then_inc(hcT_saved, 1)

                def save_probabilities(n, par, use):
                    act.wait_ge(AT_psum, done(n))
                    nc.scalar.copy(AT[0:L, bass.ds(n * QTOK, QTOK)], A[par][0:L, :]).then_inc(AT_saved, 1)

                pipelined(act, (2, save_probabilities), (1, exponentials), (0, normalise), (0, save_tokens))

            @block.tensor
            def _(pe):
                for s in (hcT_psum, sim_psum, AT_psum):
                    pe.sem_inc(s, CREDIT)

                def transpose_tokens(n, par, use):
                    pe.wait_ge(hc_ready, done(n))
                    pe.wait_ge(hcT_saved, free(n))
                    for j in range(TQ):
                        ins = nc.tensor.transpose(T[par][:, j * P:(j + 1) * P], ln_out[par][:, j, :], ident)
                    ins.then_inc(hcT_psum, 1)

                def similarity(n, par, use):
                    pe.wait_ge(hcT_ready, done(n))
                    pe.wait_ge(diff_ready, free(n))
                    for j in range(TQ):
                        keys = bass.ds((n * 2 + j // TPB) * L, L)
                        o = S[par][:, j * L:(j + 1) * L]
                        nc.tensor.matmul(o, xT_s[par][:, j * P:(j + 1) * P], MT[:, keys], start=True, stop=False)
                        ins = nc.tensor.matmul(o, ones[0:1, :], srow[0:1, 0, keys], start=False, stop=True)
                    ins.then_inc(sim_psum, 1)

                def transpose_probabilities(n, par, use):
                    pe.wait_ge(prob_ready, done(n))
                    pe.wait_ge(AT_saved, free(n))
                    hold(pe, "pe")
                    for j in range(TQ):
                        ins = nc.tensor.transpose(A[par][0:L, j * P:(j + 1) * P], prob[par][:, j, :], ident)
                    ins.then_inc(AT_psum, 1)

                pipelined(pe, (2, transpose_probabilities), (0, transpose_tokens), (0, similarity))

        hcb = sb("hcb", [P, B])
        batt = sb("batt", [P, NT])
        tgs = sb("tgs", [P, 2])
        pm = sb("pm", [P, B])
        m32 = sb("m32", [NT, 1])
        with nc.Block() as block:
            p_pe, p_dve, p_act = sem("p0_pe"), sem("p0_dve"), sem("p0_act")

            @block.tensor
            def _(pe):
                nc.tensor.transpose(banks[0][0:NT, 0:P], m_all[:], ident).then_inc(p_pe, 1)
                pe.wait_ge(p_dve, 1)
                nc.tensor.matmul(banks[1][0:1, 0:NT], m32[:], ident[0:NT, 0:NT], start=True, stop=True).then_inc(p_pe, 1)
                pe.wait_ge(p_dve, 2)
                nc.tensor.matmul(banks[2][:, 0:B], ones[0:1, :], pm[0:1, :], start=True, stop=True).then_inc(p_pe, 1)
                pe.wait_ge(p_act, 1)
                nc.tensor.matmul(banks[3][:, 0:NT], ones[:], batt[:], start=True, stop=True).then_inc(p_pe, 1)
                pe.wait_ge(p_dve, 6)
                for t in range(NT):
                    ins = nc.tensor.matmul(banks[4][:, t // TPB:t // TPB + 1], hc[:, t, :], batt[:, t:t + 1],
                                           start=(t % TPB == 0), stop=(t % TPB == TPB - 1))
                ins.then_inc(p_pe, 1)

            @block.scalar
            def _(act):
                act.wait_ge(p_dve, 3)
                nc.scalar.activation(batt[:], batt[:], ACT.Exp).then_inc(p_act, 1)

            @block.vector
            def _(dve):
                link = Chain(dve, p_dve)
                dve.wait_ge(p_pe, 1)
                link(nc.vector.tensor_reduce(m32[:], banks[0][0:NT, 0:P], AX, ALU.max))
                dve.wait_ge(p_pe, 2)
                link(nc.vector.tensor_reduce(pm[0:1, :], banks[1][0:1, 0:NT].rearrange("p (b t) -> p b t", t=TPB), AX, ALU.max))
                dve.wait_ge(p_pe, 3)

                def by_batch(ap):
                    return ap.rearrange("p (b t) -> p b t", t=TPB)

                def spread(ap):
                    return ap.rearrange("p (b o) -> p b o", o=1).broadcast_to([P, B, TPB])

                link(nc.vector.tensor_tensor(by_batch(batt[:]), by_batch(m_all[:]), spread(banks[2][:, 0:B]), ALU.subtract))
                dve.wait_ge(p_pe, 4)
                link(nc.vector.tensor_reduce(pm[:], by_batch(banks[3][:, 0:NT]), AX, ALU.add))
                link(nc.vector.reciprocal(pm[:], pm[:]))
                link(nc.vector.tensor_tensor(by_batch(batt[:]), by_batch(batt[:]), spread(pm[:]), ALU.mult))
                nc.vector.tensor_scalar(tgs[:, 0:1], tg[:, 2:3], UN2, None, ALU.mult)
                nc.vector.tensor_scalar(tgs[:, 1:2], tg[:, 3:4], UN2 / K1, None, ALU.mult)
                dve.wait_ge(p_pe, 5)
                link(nc.vector.tensor_copy(hcb[:], banks[4][:, 0:B]))

        NK = TQ * K0
        hcf = hc[:].rearrange("p t d -> p (t d)")
        u16 = hcf.bitcast(F16).rearrange("p (t w) -> p t w", w=2 * D)
        AT_s = [MT[0:L, QTOK * k:QTOK * (k + 1)] for k in range(2)]
        prod = [KmT[:, QTOK * k:QTOK * (k + 1)] for k in range(2)]
        ctx_s, Wp = pair("ctx_s", [L, 2, D]), pair("Wp", [P, 2, D])
        v8, i8 = pair("v8", [P, TQ, 8]), pair("i8", [P, TQ, 8], U32)
        el, idxf = pair("el", [P, TQ, E0]), pair("idxf", [P, NK])
        oh, ohx = pair("oh", [P, NK, E0]), sb("ohx", [P, NK, E0])
        Msum, M16, Gs = pair("Msum", [P, TQ, E0]), pair("M16", [P, TQ, E0], F16), pair("Gs", [P, TQ, E0 + 1])
        S16 = pair("S16", [P, E0], F16)
        pos = sb("pos", [P, NT * K0], I32)
        gk = sb("gk", [P, NT * K0])
        ctmp = sb("ctmp", [P, E0])
        GT = hcT[0:E0 + 1, :]
        scat = [sem(f"scattered{i}") for i in range(2)]

        with nc.Block() as block:
            (st_ready, q_psum, wp_ready, prod_ready, o_psum, o_read, u16_ready, ut_psum, ut_saved, lg_psum, d_ready,
             e_ready, m_ready, r_psum, idx_ready, g_ready, gt_psum, gt_saved, counted, r0_scales, ln_ready, hi_ready, x_done, gk_done, ln_chain, top_chain, idx_chain) = (
                sem("r0_" + s) for s in (
                    "st_ready", "q_psum", "wp_ready", "prod_ready", "o_psum", "o_read", "u16_ready", "ut_psum", "ut_saved",
                    "lg_psum", "d_ready", "e_ready", "m_ready", "r_psum", "idx_ready", "g_ready", "gt_psum",
                    "gt_saved", "counted", "row_scales", "ln_ready", "hi_ready", "x_done", "gk_done", "ln_chain", "top_chain", "idx_chain"))
            ctx_ld = [sem(f"r0_ctx_loaded{i}") for i in range(2)]
            Q, O, TU, LG, GB = banks[0:2], banks[2:4], banks[4], banks[5:7], banks[7]
            LA, LB, LD = 1 + LN_LINKS, 6, 6

            def column(bank, at):
                return bank[:, at:at + TQ * 16].rearrange("p (t e) -> p t e", e=16)[:, :, 0:E0]

            @block.sync
            def _(sp):
                def load_context(n, par, use):
                    sp.wait_ge(q_psum, free(n))
                    sp.dma_start(ctx_s[par][:], a["ctx_1024"][bass.ds(n * 2, 2)].rearrange("o s d -> s o d")
                                 ).then_inc(ctx_ld[par], 16)

                pipelined(sp, (0, load_context))

            @block.gpsimd
            def _(pool):
                for par in range(2):
                    r0 = E0 * REGION + par * P
                    pool.dma_start(sorted_rows[r0:r0 + P, :], zeros[:, 0:2 * D]).then_inc(scat[par], 16)

                def scatter(n):
                    pool.wait_ge(idx_ready, done(n))
                    hold(pool, "pool")
                    for c in range(NK):
                        nc.gpsimd.indirect_dma_start(
                            out=sorted_rows, out_offset=bass.IndirectOffsetOnAxis(ap=pos[:, n * NK + c:n * NK + c + 1], axis=0),
                            in_=u16[:, n * TQ + c // K0, :], in_offset=None).then_inc(scat[n % 2], 16)

                for n in range(NQ):
                    scatter(n)

            @block.scalar
            def _(act):
                for s in (st_ready, ut_saved, e_ready, gt_saved, ln_ready, hi_ready):
                    act.sem_inc(s, CREDIT)

                def split_high(n, par, use):
                    act.wait_ge(r0_scales, done(n))
                    act.wait_ge(o_read, done(n))
                    normalise_rows(xq(n), ln_out[par], par).then_inc(ln_ready, 1)
                    act.wait_ge(ln_ready, done(n))
                    nc.scalar.activation(u16[:, bass.ds(n * TQ, TQ), 0:D], ln_out[par][:], ACT.Copy, scale=SU
                                         ).then_inc(hi_ready, 1)

                def stage_tokens(n, par, use):
                    act.wait_ge(o_psum, free(n))
                    act.wait_ge(prod_ready, free(n))
                    nc.scalar.copy(AT_s[par], AT[0:L, bass.ds(n * QTOK, QTOK)])
                    nc.scalar.copy(xT_s[par][:], hcT[:, bass.ds(n * QTOK, QTOK)]).then_inc(st_ready, 1)

                def exponentials(n, par, use):
                    act.wait_ge(d_ready, done(n))
                    nc.scalar.activation(el[par][:], el[par][:], ACT.Exp, scale=UN1).then_inc(e_ready, 1)

                def save_rows(n, par, use):
                    act.wait_ge(ut_psum, done(n))
                    nc.scalar.copy(uT[:, :, bass.ds(n * QTOK, QTOK)],
                                   TU[:].bitcast(F16).rearrange("p (h t) -> p h t", h=2)).then_inc(ut_saved, 1)

                def save_gates(n, par, use):
                    act.wait_ge(gt_psum, done(n))
                    nc.scalar.copy(GT[:, bass.ds(n * QTOK, QTOK)], GB[0:E0 + 1, :]).then_inc(gt_saved, 1)

                pipelined(act, (0, stage_tokens), (3, exponentials), (1, split_high), (3, save_gates), (1, save_rows))

            @block.vector
            def _(dve):
                for s in (wp_ready, prod_ready, o_read, r0_scales, u16_ready, d_ready, m_ready, idx_ready, g_ready):
                    dve.sem_inc(s, CREDIT)
                ln_link, top_link, idx_link = Chain(dve, ln_chain), Chain(dve, top_chain), Chain(dve, idx_chain)
                for par in range(2):
                    nc.vector.memset(Gs[par][:], 1.0)
                nc.vector.tensor_scalar(S16[0][:], cst[:, C_BASE:C_BASE + E0], 1.0 / P, None, ALU.mult).then_inc(counted, 1)
                dve.wait_ge(counted, 1)

                def pooled_weights(n, par, use):
                    dve.wait_ge(o_psum, free(n))
                    for k in range(2):
                        ins = nc.vector.scalar_tensor_tensor(Wp[par][:, k, :], Wqv[:, 3, :], hcb[:, bass.ds(n * 2 + k, 1)],
                                                             Wqv[:, 0, :], ALU.mult, ALU.add)
                    ins.then_inc(wp_ready, 1)

                def product(n, par, use):
                    dve.wait_ge(q_psum, done(n))
                    dve.wait_ge(st_ready, done(n))
                    nc.vector.tensor_tensor(prod[par], xT_s[par][:], Q[par][:], ALU.mult).then_inc(prod_ready, 1)

                def add_attention(n, par, use):
                    ln_link.start(n * LA)
                    dve.wait_ge(o_psum, done(n))
                    ln_link(nc.vector.scalar_tensor_tensor(xq(n), tiles(O[par][:]), tg[:, 0:1], xq(n), ALU.mult, ALU.add))
                    dve.sem_inc(o_read, 1)
                    row_scales(dve, ln_link, xq(n), par, r0_scales)

                def split_low(n, par, use):
                    hi, lo = (u16[:, bass.ds(n * TQ, TQ), h * D:(h + 1) * D] for h in range(2))
                    dve.wait_ge(hi_ready, done(n))
                    nc.vector.scalar_tensor_tensor(lo, ln_out[par][:], SU, hi, ALU.mult, ALU.subtract).then_inc(u16_ready, 1)
                    nc.vector.scalar_tensor_tensor(xq(n), ln_out[par][:], tg[:, 2:3], xq(n), ALU.mult, ALU.add
                                                   ).then_inc(x_done, 1)

                def choose(n, par, use):
                    top_link.start(n * LB)
                    dve.wait_ge(lg_psum, done(n))
                    hold(dve, "dve")
                    for j in range(TQ):
                        ins = nc.vector.max(v8[par][:, j, :], LG[par][:, j * 16:j * 16 + E0])
                    top_link(ins)
                    hold(dve, "dve")
                    for j in range(TQ):
                        ins = nc.vector.max_index(i8[par][:, j, :], v8[par][:, j, :], LG[par][:, j * 16:j * 16 + E0])
                    top_link(ins)
                    nc.vector.tensor_tensor(el[par][:], column(LG[par], 0), v8[par][:, :, 0:1].broadcast_to([P, TQ, E0]),
                                            ALU.subtract).then_inc(d_ready, 1)
                    top_link(nc.vector.tensor_copy(idxf[par][:].rearrange("p (t k) -> p t k", k=K0), i8[par][:, :, 0:K0]))
                    top_link(nc.vector.tensor_tensor(
                        oh[par][:], idxf[par][:].rearrange("p (c o) -> p c o", o=1).broadcast_to([P, NK, E0]),
                        cst[:, C_IOTA:C_IOTA + E0].rearrange("p (o e) -> p o e", o=1).broadcast_to([P, NK, E0]),
                        ALU.is_equal))
                    top_link(nc.vector.tensor_reduce(Msum[par][:], oh[par][:].rearrange("p (t k) e -> p t e k", k=K0), AX, ALU.add))
                    nc.vector.tensor_copy(M16[par][:], Msum[par][:]).then_inc(m_ready, 1)
                    top_link(nc.vector.tensor_reduce(ctmp[:], Msum[par][:].rearrange("p t e -> p e t"), AX, ALU.add))
                    dve.wait_ge(r_psum, n + CREDIT)
                    nc.vector.tensor_tensor(S16[1 - par][:], S16[par][:], ctmp[:], ALU.add).then_inc(counted, 1)
                    assert top_link.k == LB

                def places_and_gates(n, par, use):
                    idx_link.start(n * LD)
                    oh4 = oh[par][:].rearrange("p (t k) e -> p t k e", k=K0)
                    ohx4 = ohx[:].rearrange("p (t k) e -> p t k e", k=K0)

                    def by_choice(ap):
                        return ap.rearrange("p t (o e) -> p t o e", o=1).broadcast_to([P, TQ, K0, E0])

                    dve.wait_ge(r_psum, done(n))
                    idx_link(nc.vector.tensor_tensor(ohx4, oh4, by_choice(column(LG[par], 64)), ALU.mult))
                    with nc.allow_low_precision("whole numbers below 2^17: exact"):
                        idx_link(nc.vector.tensor_reduce(pos[:, bass.ds(n * NK, NK)], ohx[:], AX, ALU.add))
                    dve.sem_inc(idx_ready, 1)
                    dve.wait_ge(e_ready, done(n))
                    idx_link(nc.vector.tensor_reduce(den[par][:], el[par][:], AX, ALU.add))
                    idx_link(nc.vector.reciprocal(den[par][:], den[par][:]))
                    idx_link(nc.vector.tensor_tensor(el[par][:], el[par][:], spread(den[par][:], E0), ALU.mult))
                    dve.wait_ge(gt_psum, free(n))
                    nc.vector.tensor_tensor(Gs[par][:, :, 0:E0], el[par][:], Msum[par][:], ALU.mult).then_inc(g_ready, 1)
                    idx_link(nc.vector.tensor_tensor(ohx4, oh4, by_choice(el[par][:]), ALU.mult))
                    nc.vector.tensor_reduce(gk[:, bass.ds(n * NK, NK)], ohx[:], AX, ALU.add).then_inc(gk_done, 1)
                    assert idx_link.k == LD

                pipelined(dve, (3, choose), (1, add_attention), (0, pooled_weights), (0, product), (3, places_and_gates), (1, split_low))

            @block.tensor
            def _(pe):
                mm = nc.tensor.matmul
                for s in (q_psum, o_psum, ut_psum, lg_psum, r_psum, gt_psum):
                    pe.sem_inc(s, CREDIT)

                def ranks(n, par, use):
                    pe.wait_ge(m_ready, done(n))
                    pe.wait_ge(counted, n + 1)
                    for j in range(TQ):
                        o = LG[par][:, 64 + j * 16:64 + j * 16 + E0]
                        mm(o, tri16[:], M16[par][:, j, :], start=True, stop=False)
                        for k in range(j):
                            mm(o, ones16[:], M16[par][:, k, :], start=False, stop=False)
                        ins = mm(o, ones16[:], S16[par][:], start=False, stop=True)
                    ins.then_inc(r_psum, 1)

                def attended(n, par, use):
                    pe.wait_ge(ctx_ld[par], use * 16 + 16)
                    pe.wait_ge(st_ready, done(n))
                    pe.wait_ge(prod_ready, free(n))
                    for k in range(2):
                        ks = slice(k * SEQ, (k + 1) * SEQ)
                        ins = mm(Q[par][:, ks], ctx_s[par][:, k, :], AT_s[par][:, ks], start=True, stop=True)
                    ins.then_inc(q_psum, 1)

                def transpose_rows(n, par, use):
                    pe.wait_ge(u16_ready, done(n))
                    pe.wait_ge(ut_saved, done(n - 1))
                    t16 = TU[:].bitcast(F16)
                    for j in range(TQ):
                        for h in range(2):
                            ins = nc.tensor.transpose(
                                t16[:, h * QTOK + j * P:h * QTOK + (j + 1) * P],
                                u16[:, bass.ds(n * TQ + j, 1), h * D:(h + 1) * D].rearrange("p o d -> p (o d)"), ident16[:])
                    ins.then_inc(ut_psum, 1)

                def attention_output(n, par, use):
                    pe.wait_ge(wp_ready, done(n))
                    pe.wait_ge(o_read, free(n))
                    pe.wait_ge(prod_ready, done(n))
                    for j in range(TQ):
                        o = O[par][:, j * D:(j + 1) * D]
                        js = slice(j * P, (j + 1) * P)
                        mm(o, xT_s[par][:, js], Wp[par][:, j // TPB, :], start=True, stop=False)
                        mm(o, prod[par][:, js], Wqv[:, 2, :], start=False, stop=False)
                        ins = mm(o, AT_s[par][:, js], HW1[:, bass.ds(n * 2 + j // TPB, 1), :].rearrange("p o d -> p (o d)"),
                                 start=False, stop=True)
                    ins.then_inc(o_psum, 1)

                def logits(n, par, use):
                    pe.wait_ge(ut_saved, done(n))
                    pe.wait_ge(idx_ready, free(n))
                    for j in range(TQ):
                        o = LG[par][:, j * 16:j * 16 + E0]
                        uh, ul = (uT[:, h, bass.ds(n * QTOK + j * P, P)] for h in range(2))
                        mm(o, uh, gw16[:, 0, 0:E0], start=True, stop=False)
                        mm(o, uh, gw16[:, 1, 0:E0], start=False, stop=False)
                        mm(o, ul, gw16[:, 0, 0:E0], start=False, stop=False)
                        ins = mm(o, ones[0:1, :], rows[0:1, 2, 0:E0], start=False, stop=True)
                    ins.then_inc(lg_psum, 1)

                def transpose_gates(n, par, use):
                    pe.wait_ge(g_ready, done(n))
                    pe.wait_ge(gt_saved, done(n - 1))
                    hold(pe, "pe")
                    for j in range(TQ):
                        ins = nc.tensor.transpose(GB[0:E0 + 1, j * P:(j + 1) * P], Gs[par][:, j, :], ident)
                    ins.then_inc(gt_psum, 1)

                pipelined(pe, (0, attended), (3, ranks), (2, logits), (0, attention_output), (3, transpose_gates),
                          (1, transpose_rows))

        tw = sb("tw", [P, 8, E0])
        tcum = sb("tcum", [P, E0, E0])
        ti = sb("ti", [P, 2, E0], I32)
        tabc = sb("tabc", [P, 2])
        moved = AT[:, 0:NT * K0 * (E0 - 1)].rearrange("p (c e) -> p c e", e=E0 - 1)
        shift = sb("shift", [P, NT * K0])
        places = sb("places", [P, NT * K0], I32)
        tab = sb("tab", [1, 2, P], I32)
        crow = sb("crow", [1, E0], I32)
        with nc.Block() as block:
            t_pe, t_dve, t_pad = sem("t_pe"), sem("t_dve"), sem("t_pad")

            @block.tensor
            def _(pe):
                nc.tensor.matmul(banks[0][:, 0:E0], ones16[:], S16[0][:], start=True, stop=True).then_inc(t_pe, 1)
                pe.wait_ge(t_dve, 16)
                for k in range(2):
                    ins = nc.tensor.matmul(banks[1][0:1, k * P:(k + 1) * P], tabc[:, k:k + 1], ident, start=True, stop=True)
                ins.then_inc(t_pe, 1)

            @block.vector
            def _(dve):
                link = Chain(dve, t_dve)
                cnt, tiles, cum, before, tmp = (tw[:, k, :] for k in range(5))
                part = cst[:, C_PART:C_PART + 1]
                dve.wait_ge(t_pe, 1)
                nc.vector.tensor_scalar(gk[:], gk[:], tgs[:, 0:1], None, ALU.mult)
                link(nc.vector.tensor_copy(tmp, banks[0][:, 0:E0]))
                link(nc.vector.tensor_tensor(cnt, tmp, cst[:, C_BASE:C_BASE + E0], ALU.subtract))
                link(nc.vector.tensor_copy(crow[:], tw[0:1, 4, :]))
                link(nc.vector.tensor_scalar(ti[:, 0, :], cnt, float(BLK - 1), None, ALU.add))
                link(nc.vector.tensor_scalar(ti[:, 1, :], ti[:, 0, :], BLK.bit_length() - 1, None, ALU.logical_shift_right))
                link(nc.vector.tensor_copy(tiles, ti[:, 1, :]))
                link(nc.vector.tensor_tensor(tcum[:], cst[:, C_LE:C_LE + E0 * E0].rearrange("p (e f) -> p e f", f=E0),
                                             tw[:, 1:2, :].broadcast_to([P, E0, E0]), ALU.mult))
                link(nc.vector.tensor_reduce(cum, tcum[:], AX, ALU.add))
                link(nc.vector.tensor_scalar(before, cum, part, None, ALU.is_le))
                link(nc.vector.tensor_reduce(tw[:, 5, 0:1], before, AX, ALU.add))
                link(nc.vector.tensor_tensor(tmp, before, tiles, ALU.mult))
                link(nc.vector.tensor_reduce(tw[:, 5, 1:2], tmp, AX, ALU.add))
                link(nc.vector.tensor_tensor(tw[:, 5, 2:3], part, tw[:, 5, 1:2], ALU.subtract))
                link(nc.vector.tensor_scalar(tw[:, 5, 3:4], tw[:, 5, 2:3], float(BLK), None, ALU.mult))
                nc.vector.tensor_scalar(tabc[:, 0:1], tw[:, 5, 0:1], float(E0 - 1), None, ALU.min)
                link(nc.vector.scalar_tensor_tensor(tw[:, 5, 4:5], tw[:, 5, 0:1], float(REGION), tw[:, 5, 3:4],
                                                    ALU.mult, ALU.add))
                link(nc.vector.tensor_scalar(tabc[:, 1:2], tw[:, 5, 4:5], float(E0 * REGION), None, ALU.min))
                nc.vector.tensor_scalar(tw[:, 6, 0:E0 - 1], tw[:, 1, 0:E0 - 1], float(BLK), -float(REGION), ALU.mult, ALU.add)
                link(nc.vector.tensor_tensor(
                    moved, pos[:].rearrange("p (c o) -> p c o", o=1).broadcast_to([P, NT * K0, E0 - 1]),
                    cst[:, C_BASE + 1:C_BASE + E0].rearrange("p (o e) -> p o e", o=1).broadcast_to([P, NT * K0, E0 - 1]),
                    ALU.is_ge))
                link(nc.vector.tensor_tensor(moved, moved, tw[:, 6:7, 0:E0 - 1].broadcast_to([P, NT * K0, E0 - 1]), ALU.mult))
                link(nc.vector.tensor_reduce(shift[:], moved, AX, ALU.add))
                link(nc.vector.tensor_tensor(places[:], pos[:], shift[:], ALU.add))
                dve.wait_ge(t_pe, 2)
                link(nc.vector.tensor_copy(tab[:], banks[1][0:1, 0:2 * P].rearrange("p (k i) -> p k i", k=2)))

            @block.sync
            def _(sp):
                sp.wait_ge(t_dve, 3)
                for e in range(E0):
                    r = sp.value_load(crow[0:1, e:e + 1], min_val=0, max_val=ROWS - BLK)
                    sp.dma_start(sorted_rows[bass.ds(r, BLK), :].rearrange("(t q) d -> q t d", q=P),
                                 zeros[:].rearrange("p (t d) -> p t d", t=2)).then_inc(t_pad, 16)
                sp.wait_ge(t_pad, 16 * E0)
                for par in range(2):
                    sp.wait_ge(scat[par], 16 * NK * (NQ // 2) + 16)

        def add_shared(dve, t_psum, x_sem, par, g):
            dve.wait_ge(t_psum, done(g))
            xg = X[:, bass.ds(g * 4, 4), :]
            nc.vector.scalar_tensor_tensor(xg, banks[4 + par][:].rearrange("p (t d) -> p t d", t=4), tgs[:, 0:1], xg,
                                           ALU.mult, ALU.add).then_inc(x_sem, 1)

        hf = [hcf[:, 512 * k:512 * k + 512] for k in range(2)]
        hid = AT[:].bitcast(F16).rearrange("p (g h c t) -> p g h c t", g=2, h=2, c=4)
        yT = [hcf[:, 1024 + 512 * k:1536 + 512 * k] for k in range(2)]
        with nc.Block() as block:
            s_h, s_hf, s_lo, s_y, s_yc, s_t, s_x, s_lk = (sem("sh_" + s) for s in (
                "h_psum", "gelu", "split", "y_psum", "y_copied", "t_psum", "x", "chain"))
            G = TOK // 512

            @block.tensor
            def _(pe):
                mm = nc.tensor.matmul
                for s in (s_h, s_y, s_t):
                    pe.sem_inc(s, CREDIT)

                def transpose_back(par, g):
                    pe.wait_ge(s_yc, done(g))
                    pe.wait_ge(s_x, free(g))
                    for j in range(4):
                        ins = nc.tensor.transpose(banks[4 + par][:, j * P:(j + 1) * P], yT[par][:, j * P:(j + 1) * P], ident)
                    ins.then_inc(s_t, 1)

                with pe.Fori(0, G // 2) as i:
                    for par in range(2):
                        g = i * 2 + par
                        ug, ul = (uT[:, h, bass.ds(g * 512, 512)] for h in range(2))
                        for c in range(4):
                            q = g * 4 + c
                            cs = slice(c * P, (c + 1) * P)
                            pe.wait_ge(s_hf, free(q))
                            mm(banks[c % 2][:], S1[:, 0, cs], ug, start=True, stop=False)
                            mm(banks[c % 2][:], S1[:, 1, cs], ug, start=False, stop=False)
                            mm(banks[c % 2][:], S1[:, 0, cs], ul, start=False, stop=True).then_inc(s_h, 1)
                        if par:
                            transpose_back(0, i * 2)
                        Y = banks[2 + par]
                        pe.wait_ge(s_yc, free(g))
                        mm(Y[:], b2a[:], GT[:, bass.ds(g * 512, 512)], start=True, stop=False)
                        for c in range(4):
                            q = g * 4 + c
                            cs = slice(c * P, (c + 1) * P)
                            pe.wait_ge(s_lo, done(q))
                            mm(Y[:], S2[:, 0, cs], hid[:, par, 0, c, :], start=False, stop=False)
                            mm(Y[:], S2[:, 1, cs], hid[:, par, 0, c, :], start=False, stop=False)
                            ins = mm(Y[:], S2[:, 0, cs], hid[:, par, 1, c, :], start=False, stop=(c == 3))
                        ins.then_inc(s_y, 1)
                    transpose_back(1, i * 2 + 1)

            @block.scalar
            def _(act):
                act.sem_inc(s_hf, CREDIT)
                act.sem_inc(s_yc, CREDIT)
                with act.Fori(0, G // 2) as i:
                    for par in range(2):
                        g = i * 2 + par
                        for c in range(4):
                            q = g * 4 + c
                            act.wait_ge(s_h, done(q))
                            act.wait_ge(s_lo, free(q))
                            nc.scalar.activation(hf[c % 2], banks[c % 2][:], ACT.Gelu,
                                                 bias=cols[:, V_SB1 + c:V_SB1 + c + 1], scale=UN1).then_inc(s_hf, 1)
                        act.wait_ge(s_y, done(g))
                        act.wait_ge(s_t, free(g))
                        nc.scalar.copy(yT[par][:], banks[2 + par][:]).then_inc(s_yc, 1)

            @block.vector
            def _(dve):
                dve.sem_inc(s_lo, CREDIT)
                dve.sem_inc(s_x, CREDIT)
                lnk = Chain(dve, s_lk)
                with dve.Fori(0, G // 2) as i:
                    for par in range(2):
                        g = i * 2 + par
                        for c in range(4):
                            q = g * 4 + c
                            lnk.base, lnk.k = q, 0
                            dve.wait_ge(s_hf, done(q))
                            dve.wait_ge(s_y, free(g))
                            lnk(nc.vector.tensor_scalar(hid[:, par, 0, c, :], hf[c % 2], SH, None, ALU.mult))
                            nc.vector.scalar_tensor_tensor(hid[:, par, 1, c, :], hf[c % 2], SH, hid[:, par, 0, c, :],
                                                           ALU.mult, ALU.subtract).then_inc(s_lo, 1)
                        if par:
                            add_shared(dve, s_t, s_x, 0, i * 2)
                    add_shared(dve, s_t, s_x, 1, i * 2 + 1)

        h16 = hcT[:].bitcast(F16)
        hf = [AT[:, 512 * k:512 * k + 512] for k in range(2)]
        xp = [h16[:, 4096 + 512 * k:4608 + 512 * k].rearrange("p (t d) -> p t d", t=2) for k in range(4)]
        DEEP, WDEEP = 4, 8
        we = [hcf[:, WEW * k:WEW * (k + 1)] for k in range(WDEEP - 1)]
        we.append(AT[:, 2560:2560 + WEW])
        we16, web = [w.bitcast(F16) for w in we], [w[:, 2 * F0:2 * F0 + 2] for w in we]
        xpT = [h16[:, 1024 + 512 * k:1536 + 512 * k].rearrange("p (h t) -> p h t", h=2) for k in range(2)]
        hs = [h16[:, 2048 + 1024 * k:3072 + 1024 * k].rearrange("p (h t) -> p h t", h=2) for k in range(2)]
        ys = [AT[:, 2048 + 256 * k:2304 + 256 * k].rearrange("p (t d) -> p t d", t=2) for k in range(2)]
        with nc.Block() as block:
            x_tr, x_cp, x_h, x_hf, x_lo, x_y, x_yc, x_lk = (sem("ex_" + s) for s in (
                "t_psum", "t_copied", "h_psum", "gelu", "split", "y_psum", "y_copied", "chain"))
            x_ld = [sem(f"ex_rows_loaded{i}") for i in range(4)]
            w_ld = [sem(f"ex_weights_loaded{i}") for i in range(WDEEP)]
            x_st = [sem(f"ex_stored{i}") for i in range(2)]
            TB, HB, YB = banks[0:2], banks[2:4], banks[4:6]
            MAIN = BLOCKS // DEEP - 1
            WMAIN = BLOCKS // WDEEP - 1

            @block.sync
            def _(sp):
                def load_rows(b, k):
                    row = sp.value_load(tab[0:1, 1, bass.ds(b, 1)], min_val=0, max_val=ROWS - BLK)
                    sp.dma_start(xp[k], sorted_rows[bass.ds(row, BLK), :].rearrange("(t q) d -> q t d", q=P)
                                 ).then_inc(x_ld[k], 16)

                def store(b, par):
                    sp.wait_ge(x_yc, done(b))
                    sp.dma_start(expert_rows[bass.ds(b * BLK, BLK), :].rearrange("(t q) d -> q t d", q=P),
                                 ys[par]).then_inc(x_st[par], 16)

                for par in range(2):
                    sp.sem_inc(x_st[par], 16)
                def next_rows(b, k):
                    sp.wait_ge(x_tr, done(b))
                    hold(sp, "sp")
                    load_rows(b + DEEP, k)

                for b in range(DEEP):
                    load_rows(b, b)
                next_rows(0, 0)
                next_rows(1, 1)
                with sp.Fori(0, MAIN - 1) as i:
                    for k in range(DEEP):
                        store(i * DEEP + k, k % 2)
                        next_rows(i * DEEP + k + 2, (k + 2) % DEEP)
                for b in range((MAIN - 1) * DEEP, BLOCKS):
                    store(b, b % 2)
                    if b + 2 + DEEP < BLOCKS:
                        next_rows(b + 2, (b + 2) % DEEP)
                for par in range(2):
                    sp.wait_ge(x_st[par], 16 * (BLOCKS // 2) + 16)

            @block.gpsimd
            def _(pool):
                def load_weights(b, k):
                    e = pool.value_load(tab[0:1, 0, bass.ds(b, 1)], min_val=0, max_val=E0 - 1)
                    pool.dma_start(we[k], WE[:, bass.ds(e, 1), :].rearrange("p o f -> p (o f)")).then_inc(w_ld[k], 16)

                for b in range(WDEEP):
                    load_weights(b, b)
                with pool.Fori(0, WMAIN) as i:
                    for k in range(WDEEP):
                        b = i * WDEEP + k
                        pool.wait_ge(x_y, done(b))
                        hold(pool, "pool")
                        load_weights(b + WDEEP, k)

            @block.tensor
            def _(pe):
                mm = nc.tensor.matmul
                for s in (x_tr, x_h, x_y):
                    pe.sem_inc(s, CREDIT)

                def transposes(b, k, use):
                    par = k % 2
                    pe.wait_ge(x_ld[k % DEEP], use)
                    pe.wait_ge(x_cp, free(b))
                    t16 = TB[par][:, 0:SEQ].bitcast(F16)
                    for j in range(2):
                        for h in range(2):
                            ins = nc.tensor.transpose(t16[:, h * SEQ + j * P:h * SEQ + (j + 1) * P],
                                                      xp[k % DEEP][:, j, h * D:(h + 1) * D], ident16[:])
                    ins.then_inc(x_tr, 1)

                def hidden(b, k, use):
                    par = k % 2
                    pe.wait_ge(w_ld[k], use)
                    pe.wait_ge(x_cp, done(b))
                    pe.wait_ge(x_hf, free(b))
                    xh, xl = (xpT[par][:, h, :] for h in range(2))
                    for c in range(2):
                        wh, wl = (we16[k][:, h * F0 + c * P:h * F0 + (c + 1) * P] for h in range(2))
                        o = HB[par][:, c * BLK:(c + 1) * BLK]
                        mm(o, wh, xh, start=True, stop=False)
                        mm(o, wh, xl, start=False, stop=False)
                        ins = mm(o, wl, xh, start=False, stop=True)
                    ins.then_inc(x_h, 1)

                def outputs(b, k):
                    par = k % 2
                    pe.wait_ge(x_lo, done(b))
                    pe.wait_ge(x_yc, free(b))
                    for j in range(2):
                        o = YB[par][:, j * D:(j + 1) * D]
                        for c in range(2):
                            hh, hl = (hs[par][:, h, c * BLK + j * P:c * BLK + (j + 1) * P] for h in range(2))
                            wh, wl = (we16[k][:, 2 * F0 + h * 2 * D + c * D:2 * F0 + h * 2 * D + (c + 1) * D] for h in range(2))
                            mm(o, hh, wh, start=(c == 0), stop=False)
                            mm(o, hh, wl, start=False, stop=False)
                            ins = mm(o, hl, wh, start=False, stop=(c == 1))
                    ins.then_inc(x_y, 1)

                def step(i, k, last=False):
                    b = i * WDEEP + k
                    if not (last and k >= WDEEP - 2):
                        transposes(b + 2, (k + 2) % WDEEP, i * 32 + ((k + 2) // DEEP) * 16 + 16)
                    if not (last and k >= WDEEP - 1):
                        hidden(b + 1, (k + 1) % WDEEP, (i + (k + 1) // WDEEP) * 16 + 16)
                    outputs(b, k)

                transposes(0, 0, 16)
                transposes(1, 1, 16)
                hidden(0, 0, 16)
                with pe.Fori(0, WMAIN) as i:
                    for k in range(WDEEP):
                        step(i, k)
                for k in range(WDEEP):
                    step(WMAIN, k, last=True)

            @block.vector
            def _(dve):
                dve.sem_inc(x_cp, CREDIT)
                dve.sem_inc(x_lo, CREDIT)
                lnk = Chain(dve, x_lk)

                def copy_rows(b, par):
                    dve.wait_ge(x_tr, done(b))
                    dve.wait_ge(x_h, free(b))
                    nc.vector.tensor_copy(xpT[par], TB[par][:, 0:SEQ].bitcast(F16).rearrange("p (h t) -> p h t", h=2)
                                          ).then_inc(x_cp, 1)

                def split(b, par):
                    lnk.base, lnk.k = b, 0
                    dve.wait_ge(x_hf, done(b))
                    dve.wait_ge(x_y, free(b))
                    lnk(nc.vector.tensor_scalar(hs[par][:, 0, :], hf[par], SH, None, ALU.mult))
                    nc.vector.scalar_tensor_tensor(hs[par][:, 1, :], hf[par], SH, hs[par][:, 0, :],
                                                   ALU.mult, ALU.subtract).then_inc(x_lo, 1)

                copy_rows(0, 0)
                copy_rows(1, 1)
                split(0, 0)
                with dve.Fori(0, BLOCKS // 2 - 1) as i:
                    for par in range(2):
                        copy_rows(i * 2 + 2 + par, par)
                        split(i * 2 + 1 + par, 1 - par)
                split(BLOCKS - 1, 1)

            @block.scalar
            def _(act):
                act.sem_inc(x_hf, CREDIT)
                act.sem_inc(x_yc, CREDIT)

                def gelu(b, k):
                    par = k % 2
                    act.wait_ge(x_h, done(b))
                    act.wait_ge(x_lo, free(b))
                    for c in range(2):
                        s = slice(c * BLK, (c + 1) * BLK)
                        ins = nc.scalar.activation(hf[par][:, s], HB[par][:, s], ACT.Gelu, bias=web[k][:, c:c + 1], scale=UN1)
                    ins.then_inc(x_hf, 1)

                def copy_out(b, par, stores):
                    act.wait_ge(x_y, done(b))
                    act.wait_ge(x_st[par], stores)
                    nc.scalar.copy(ys[par], YB[par][:, 0:SEQ].rearrange("p (t d) -> p t d", t=2)).then_inc(x_yc, 1)

                gelu(0, 0)
                gelu(1, 1)
                copy_out(0, 0, 16)
                with act.Fori(0, WMAIN) as i:
                    for k in range(WDEEP):
                        b = i * WDEEP + k
                        gelu(b + 2, (k + 2) % WDEEP)
                        copy_out(b + 1, (k + 1) % 2, i * 64 + 16 * ((k + 1) // 2) + 16)
                for b in range(WMAIN * WDEEP, BLOCKS):
                    if b + 2 < BLOCKS:
                        gelu(b + 2, (b + 2) % WDEEP)
                    if b + 1 < BLOCKS:
                        copy_out(b + 1, (b + 1) % 2, 16 * ((b + 1) // 2) + 16)

        Yg = [AT[:, 1024 + NK * D * k:1024 + NK * D * (k + 1)].rearrange("p (c d) -> p c d", d=D) for k in range(2)]
        mh = [Gs[k][:, :, 0:HEADS] for k in range(2)]
        pTs = AT_s
        with nc.Block() as block:
            (scales_ready, v_ready, vT_psum, vT_ready, sc_psum, sc_ready, ex_ready, pr_ready, pT_psum, pT_ready, o_psum,
             x_ready, got_in, ln_chain, max_chain, sum_chain) = (sem("a1_" + s) for s in (
                "row_scales", "v_ready", "vT_psum", "vT_ready", "sc_psum", "sc_ready", "exp_ready", "prob_ready", "pT_psum",
                "pT_ready", "o_psum", "x_ready", "combined", "ln_chain", "max_chain", "sum_chain"))
            gat = [sem(f"a1_gathered{i}") for i in range(2)]
            T, S, A, O = banks[0:2], banks[2:4], banks[4:6], banks[6:8]
            LA, LC = K0 + LN_LINKS, 2

            @block.gpsimd
            def _(pool):
                def gather(n):
                    pool.wait_ge(got_in, free(n))
                    hold(pool, "pool")
                    for c in range(NK):
                        nc.gpsimd.indirect_dma_start(
                            out=Yg[n % 2][:, c, :], out_offset=None, in_=expert_rows,
                            in_offset=bass.IndirectOffsetOnAxis(ap=places[:, n * NK + c:n * NK + c + 1], axis=0)
                        ).then_inc(gat[n % 2], 16)

                for n in range(NQ):
                    gather(n)

            @block.vector
            def _(dve):
                for s in (scales_ready, sc_ready, pr_ready, x_ready, got_in):
                    dve.sem_inc(s, CREDIT)
                ln_link, max_link, sum_link = Chain(dve, ln_chain), Chain(dve, max_chain), Chain(dve, sum_chain)

                def by_head(ap):
                    return ap.rearrange("p t (s h) -> p t h s", h=HEADS)

                def per_head(ap):
                    return ap.rearrange("p t (o h) -> p t o h", o=1).broadcast_to([P, TQ, L // HEADS, HEADS])

                def split_heads(ap):
                    return ap.rearrange("p t (s h) -> p t s h", h=HEADS)

                def combine(n, par, use):
                    ln_link.start(n * LA)
                    dve.wait_ge(gat[par], (use + 1) * 16 * NK)
                    for k in range(K0):
                        for j in range(TQ):
                            xj = X[:, bass.ds(n * TQ + j, 1), :].rearrange("p o d -> p (o d)")
                            ins = nc.vector.scalar_tensor_tensor(
                                xj, Yg[par][:, j * K0 + k, :], gk[:, bass.ds(n * NK + (j * K0 + k), 1)], xj, ALU.mult, ALU.add)
                        ln_link(ins)
                    dve.sem_inc(got_in, 1)
                    dve.wait_ge(v_ready, free(n))
                    row_scales(dve, ln_link, xq(n), par, scales_ready)

                def less_maximum(n, par, use):
                    max_link.start(n)
                    s = tiles(S[par][:, 0:TQ * L])
                    dve.wait_ge(sc_psum, done(n))
                    max_link(nc.vector.tensor_reduce(mh[par], by_head(s), AX, ALU.max))
                    nc.vector.tensor_tensor(split_heads(diff[par]), split_heads(s), per_head(mh[par]),
                                            ALU.subtract).then_inc(sc_ready, 1)

                def probabilities(n, par, use):
                    sum_link.start(n * LC)
                    dve.wait_ge(ex_ready, done(n))
                    sum_link(nc.vector.tensor_reduce(mh[par], by_head(diff[par]), AX, ALU.add))
                    sum_link(nc.vector.reciprocal(mh[par], mh[par]))
                    dve.wait_ge(pT_psum, free(n))
                    nc.vector.tensor_tensor(split_heads(prob[par]), split_heads(diff[par]), per_head(mh[par]),
                                            ALU.mult).then_inc(pr_ready, 1)

                def add_attention(n, par, use):
                    dve.wait_ge(o_psum, done(n))
                    nc.vector.scalar_tensor_tensor(xq(n), tiles(O[par][:]), tg[:, 1:2], xq(n), ALU.mult, ALU.add
                                                   ).then_inc(x_ready, 1)

                pipelined(dve, (2, probabilities), (0, combine), (1, less_maximum), (2, add_attention))

            @block.scalar
            def _(act):
                for s in (v_ready, vT_ready, ex_ready, pT_ready):
                    act.sem_inc(s, CREDIT)

                def normalise(n, par, use):
                    act.wait_ge(scales_ready, done(n))
                    act.wait_ge(vT_psum, free(n))
                    normalise_rows(xq(n), ln_out[par], par).then_inc(v_ready, 1)

                def stage_tokens(n, par, use):
                    act.wait_ge(vT_psum, done(n))
                    act.wait_ge(sc_psum, free(n))
                    nc.scalar.copy(xT_s[par][:], T[par][:]).then_inc(vT_ready, 1)

                def exponentials(n, par, use):
                    act.wait_ge(sc_ready, done(n))
                    nc.scalar.activation(diff[par], diff[par], ACT.Exp).then_inc(ex_ready, 1)

                def stage_probabilities(n, par, use):
                    act.wait_ge(pT_psum, done(n))
                    act.wait_ge(o_psum, free(n))
                    nc.scalar.copy(pTs[par], A[par][0:L, :]).then_inc(pT_ready, 1)

                pipelined(act, (2, stage_probabilities), (1, exponentials), (0, normalise), (0, stage_tokens))

            @block.tensor
            def _(pe):
                mm = nc.tensor.matmul
                for s in (vT_psum, sc_psum, pT_psum, o_psum):
                    pe.sem_inc(s, CREDIT)

                def transpose_tokens(n, par, use):
                    pe.wait_ge(v_ready, done(n))
                    pe.wait_ge(vT_ready, free(n))
                    for j in range(TQ):
                        ins = nc.tensor.transpose(T[par][:, j * P:(j + 1) * P], ln_out[par][:, j, :], ident)
                    ins.then_inc(vT_psum, 1)

                def scores(n, par, use):
                    pe.wait_ge(vT_ready, done(n))
                    pe.wait_ge(sc_ready, free(n))
                    for j in range(TQ):
                        keys = bass.ds((n * 2 + j // TPB) * L, L)
                        o = S[par][:, j * L:(j + 1) * L]
                        mm(o, xT_s[par][:, j * P:(j + 1) * P], QK[:, keys], start=True, stop=False)
                        ins = mm(o, ones[0:1, :], srow[0:1, 1, keys], start=False, stop=True)
                    ins.then_inc(sc_psum, 1)

                def transpose_probabilities(n, par, use):
                    pe.wait_ge(pr_ready, done(n))
                    pe.wait_ge(pT_ready, free(n))
                    hold(pe, "pe")
                    for j in range(TQ):
                        ins = nc.tensor.transpose(A[par][0:L, j * P:(j + 1) * P], prob[par][:, j, :], ident)
                    ins.then_inc(pT_psum, 1)

                def attention_output(n, par, use):
                    pe.wait_ge(pT_ready, done(n))
                    pe.wait_ge(x_ready, free(n))
                    for j in range(TQ):
                        ins = mm(O[par][:, j * D:(j + 1) * D], pTs[par][:, j * P:(j + 1) * P],
                                 VO[:, bass.ds(n * 2 + j // TPB, 1), :].rearrange("p o d -> p (o d)"), start=True, stop=True)
                    ins.then_inc(o_psum, 1)

                pipelined(pe, (2, transpose_probabilities), (2, attention_output), (0, transpose_tokens), (0, scores))

        idx1 = sb("idx1", [1, B * K1], I32)
        with nc.Block() as block:
            (r1_scales, hi_ready, w_ready, wt_psum, wt_saved, s_psum, s_read, ln_chain, top_chain) = (sem("r1_" + s) for s in (
                "row_scales", "hi_ready", "w_ready", "wT_psum", "wT_saved", "s_psum", "s_read", "ln_chain", "top_chain"))
            ln_ready = sem("r1_ln_ready")
            TU, LG = banks[0:2], banks[2:4]

            @block.vector
            def _(dve):
                for s in (r1_scales, w_ready, s_read):
                    dve.sem_inc(s, CREDIT)
                ln_link, top_link = Chain(dve, ln_chain), Chain(dve, top_chain)

                def scales(n, par, use):
                    ln_link.start(n * LN_LINKS)
                    dve.wait_ge(ln_ready, free(n))
                    row_scales(dve, ln_link, xq(n), par, r1_scales)

                def split_low(n, par, use):
                    hi, lo = (u16[:, bass.ds(n * TQ, TQ), h * D:(h + 1) * D] for h in range(2))
                    dve.wait_ge(hi_ready, done(n))
                    nc.vector.scalar_tensor_tensor(lo, ln_out[par][:], SU, hi, ALU.mult, ALU.subtract).then_inc(w_ready, 1)

                def choose(n, par, use):
                    top_link.start(2 * n)
                    dve.wait_ge(s_psum, done(n))
                    hold(dve, "dve")
                    for k in range(2):
                        ins = nc.vector.max(v8[par][0:1, k, :], LG[par][0:1, k * 16:k * 16 + E1])
                    top_link(ins)
                    hold(dve, "dve")
                    for k in range(2):
                        ins = nc.vector.max_index(i8[par][0:1, k, :], v8[par][0:1, k, :], LG[par][0:1, k * 16:k * 16 + E1])
                    top_link(ins)
                    nc.vector.tensor_copy(idx1[0:1, bass.ds(n * 2 * K1, 2 * K1)].rearrange("p (b k) -> p b k", k=K1),
                                          i8[par][0:1, 0:2, 0:K1]).then_inc(s_read, 1)

                pipelined(dve, (0, scales), (1, split_low), (2, choose))

            @block.scalar
            def _(act):
                for s in (ln_ready, hi_ready, wt_saved):
                    act.sem_inc(s, CREDIT)

                def split_high(n, par, use):
                    act.wait_ge(r1_scales, done(n))
                    act.wait_ge(w_ready, free(n))
                    normalise_rows(xq(n), ln_out[par], par).then_inc(ln_ready, 1)
                    act.wait_ge(ln_ready, done(n))
                    nc.scalar.activation(u16[:, bass.ds(n * TQ, TQ), 0:D], ln_out[par][:], ACT.Copy, scale=SU
                                         ).then_inc(hi_ready, 1)

                def save_rows(n, par, use):
                    act.wait_ge(wt_psum, done(n))
                    nc.scalar.copy(uT[:, :, bass.ds(n * QTOK, QTOK)],
                                   TU[par][:].bitcast(F16).rearrange("p (h t) -> p h t", h=2)).then_inc(wt_saved, 1)

                pipelined(act, (1, save_rows), (0, split_high))

            @block.tensor
            def _(pe):
                mm = nc.tensor.matmul
                for s in (wt_psum, s_psum):
                    pe.sem_inc(s, CREDIT)

                def transpose_rows(n, par, use):
                    pe.wait_ge(w_ready, done(n))
                    pe.wait_ge(wt_saved, free(n))
                    t16 = TU[par][:].bitcast(F16)
                    for j in range(TQ):
                        for h in range(2):
                            ins = nc.tensor.transpose(
                                t16[:, h * QTOK + j * P:h * QTOK + (j + 1) * P],
                                u16[:, bass.ds(n * TQ + j, 1), h * D:(h + 1) * D].rearrange("p o d -> p (o d)"), ident16[:])
                    ins.then_inc(wt_psum, 1)

                def scores(n, par, use):
                    pe.wait_ge(wt_saved, done(n))
                    pe.wait_ge(s_read, free(n))
                    for k in range(2):
                        o = LG[par][:, k * 16:k * 16 + E1]
                        uh, ul = (uT[:, h, bass.ds(n * QTOK + k * SEQ, P)] for h in range(2))
                        mm(o, uh, wr16[:, 0, :], start=True, stop=False)
                        mm(o, uh, wr16[:, 1, :], start=False, stop=False)
                        mm(o, ul, wr16[:, 0, :], start=False, stop=False)
                        ins = mm(o, ones[0:1, :], rows[0:1, 3, 0:E1], start=False, stop=True)
                    ins.then_inc(s_psum, 1)

                pipelined(pe, (1, transpose_rows), (1, scores))

        xo = [AT[:, 1024 + 512 * k:1280 + 512 * k].rearrange("p (t d) -> p t d", t=2) for k in range(2)]
        with nc.Block() as block:
            m_h, m_hf, m_lo, m_y, m_x, m_lk = (sem("m1_" + s) for s in ("h_psum", "gelu", "split", "y_psum", "x", "chain"))
            m_st = [sem(f"m1_stored{i}") for i in range(2)]
            HB, YB = banks[0:2], banks[2:4]

            def chosen(eng, n, k):
                return eng.value_load(idx1[0:1, bass.ds(n * K1 + k, 1)], min_val=0, max_val=E1 - 1)

            @block.tensor
            def _(pe):
                mm = nc.tensor.matmul
                for s in (m_h, m_y):
                    pe.sem_inc(s, CREDIT)

                def hidden(n, par):
                    pe.wait_ge(m_hf, free(n))
                    hold(pe, "pe")
                    uh, ul = (uT[:, h, bass.ds(n * SEQ, SEQ)] for h in range(2))
                    for k in range(K1):
                        e = chosen(pe, n, k)
                        wh, wl = (M1[:, h, bass.ds(e, 1), :].rearrange("p o f -> p (o f)") for h in range(2))
                        o = HB[par][:, k * SEQ:(k + 1) * SEQ]
                        mm(o, wh, uh, start=True, stop=False)
                        mm(o, wh, ul, start=False, stop=False)
                        ins = mm(o, wl, uh, start=False, stop=True)
                    ins.then_inc(m_h, 1)

                def outputs(n, par):
                    pe.wait_ge(m_lo, done(n))
                    pe.wait_ge(m_x, free(n))
                    hold(pe, "pe")
                    for j in range(2):
                        o = YB[par][:, j * D:(j + 1) * D]
                        for k in range(K1):
                            e = chosen(pe, n, k)
                            hh, hl = (hs[par][:, h, k * SEQ + j * P:k * SEQ + (j + 1) * P] for h in range(2))
                            wh, wl = (M2[:, h, bass.ds(e, 1), :].rearrange("p o f -> p (o f)") for h in range(2))
                            mm(o, hh, wh, start=(k == 0), stop=False)
                            mm(o, hh, wl, start=False, stop=False)
                            mm(o, hl, wh, start=False, stop=False)
                            ins = mm(o, ones[0:1, :], b2m[0:1, bass.ds(e, 1), :].rearrange("p o d -> p (o d)"),
                                     start=False, stop=(k == K1 - 1))
                    ins.then_inc(m_y, 1)

                hidden(0, 0)
                with pe.Fori(0, B // 2 - 1) as i:
                    for par in range(2):
                        hidden(i * 2 + 1 + par, 1 - par)
                        outputs(i * 2 + par, par)
                hidden(B - 1, 1)
                outputs(B - 2, 0)
                outputs(B - 1, 1)

            @block.scalar
            def _(act):
                act.sem_inc(m_hf, CREDIT)
                with act.Fori(0, B // 2) as i:
                    for par in range(2):
                        n = i * 2 + par
                        act.wait_ge(m_h, done(n))
                        act.wait_ge(m_lo, free(n))
                        hold(act, "act")
                        for k in range(K1):
                            e = chosen(act, n, k)
                            ins = nc.scalar.activation(hf[par][:, k * SEQ:(k + 1) * SEQ], HB[par][:, k * SEQ:(k + 1) * SEQ],
                                                       ACT.Gelu, bias=cols[:, bass.ds(e + V_B1, 1)], scale=UN1)
                        ins.then_inc(m_hf, 1)

            @block.vector
            def _(dve):
                for s in (m_lo, m_x):
                    dve.sem_inc(s, CREDIT)
                lnk = Chain(dve, m_lk)

                def split(n, par):
                    lnk.base, lnk.k = n, 0
                    dve.wait_ge(m_hf, done(n))
                    dve.wait_ge(m_y, free(n))
                    lnk(nc.vector.tensor_scalar(hs[par][:, 0, :], hf[par], SH, None, ALU.mult))
                    nc.vector.scalar_tensor_tensor(hs[par][:, 1, :], hf[par], SH, hs[par][:, 0, :],
                                                   ALU.mult, ALU.subtract).then_inc(m_lo, 1)

                def add(n, par):
                    dve.wait_ge(m_y, done(n))
                    nc.vector.scalar_tensor_tensor(xt(n), YB[par][:, 0:SEQ].rearrange("p (t d) -> p t d", t=2),
                                                   tgs[:, 1:2], xt(n), ALU.mult, ALU.add).then_inc(m_x, 1)

                split(0, 0)
                with dve.Fori(0, B // 2 - 1) as i:
                    for par in range(2):
                        split(i * 2 + 1 + par, 1 - par)
                        add(i * 2 + par, par)
                split(B - 1, 1)
                add(B - 2, 0)
                add(B - 1, 1)

            @block.sync
            def _(sp):
                out_v = out.rearrange("b (t p) d -> p (b t) d", p=P)
                with sp.Fori(0, B) as n:
                    sp.wait_ge(m_x, done(n))
                    sp.dma_start(out_v[:, bass.ds(n * TPB, TPB), :], xt(n)).then_inc(m_st[0], 16)
                sp.wait_ge(m_st[0], 16 * B)


_INS = ['x', 'ctx_1024', 'g_xattn', 'g_ffn', 'L0_xattn_w_sim', 'L0_xattn_b_sim', 'L0_xattn_W_qv', 'L0_xattn_b_qv',
        'L0_ffn_sW1', 'L0_ffn_sb1', 'L0_ffn_sW2', 'L0_ffn_sb2', 'L0_ffn_rW1', 'L0_ffn_rb1', 'L0_ffn_rW2',
        'L0_ffn_rb2', 'L0_ffn_gW', 'L0_ffn_gb', 'L1_xattn_Wq', 'L1_xattn_bq', 'L1_xattn_Wk', 'L1_xattn_bk',
        'L1_xattn_Wv', 'L1_xattn_bv', 'L1_xattn_Wo', 'L1_xattn_bo', 'L1_ffn_Wr', 'L1_ffn_br', 'L1_ffn_W1',
        'L1_ffn_b1', 'L1_ffn_W2', 'L1_ffn_b2']


def constants():
    import numpy as np
    c = np.zeros((P, NCONST), np.float32)
    c[:, C_ID:C_ID + P] = np.eye(P)
    c[:, C_TRI:C_TRI + P] = np.triu(np.ones((P, P)), 1)
    c[:, C_MASK:C_MASK + L] = np.arange(P)[:, None] // HD == np.arange(L)[None, :] % HEADS
    c[:, C_IOTA:C_IOTA + 6 * E0] = np.tile(np.arange(E0), 6)
    c[:, C_BASE:C_BASE + E0] = np.arange(E0) * REGION
    c[:, C_LE:C_LE + E0 * E0] = np.tril(np.ones((E0, E0))).reshape(-1)
    c[:, C_PART] = np.arange(P)
    return c


def kernel(**inputs):
    import numpy as np
    import concourse.bacc as bacc
    from concourse.bass_utils import run_bass_kernel_spmd as run

    nc = bacc.Bacc("TRN2", target_bir_lowering=False, num_devices=1)
    arrays, aps = {}, {}
    for name in _INS:
        arr = np.ascontiguousarray(inputs[name])
        arrays["in_" + name] = arr
        aps[name] = nc.dram_tensor("in_" + name, arr.shape, mybir.dt.from_np(arr.dtype), kind="ExternalInput").ap()
    arrays["in_const"] = constants()
    const = nc.dram_tensor("in_const", (P, NCONST), F32, kind="ExternalInput").ap()
    out = nc.dram_tensor("out", (B, SEQ, D), F32, kind="ExternalOutput").ap()
    build(nc, aps, const, out)
    return run(nc, [arrays], core_ids=[0]).results[0]["out"]
```

```python
from contextlib import ExitStack

import concourse.bass as bass
from concourse import mybir

F32 = mybir.dt.float32
F16 = mybir.dt.float16
I32 = mybir.dt.int32
U32 = mybir.dt.uint32
ALU = mybir.AluOpType
ACT = mybir.ActivationFunctionType
AX = mybir.AxisListType.X

P = 128
B = 16
SEQ = 256
TPB = SEQ // P
NT = B * TPB
TOK = B * SEQ
TQ = 4
NQ = NT // TQ
QTOK = TQ * P
D = 128
L = 64
HEADS = 8
HD = D // HEADS
E0 = 15
F0 = 256
K0 = 3
FS = 512
E1 = 8
K1 = 2
EPS = 1e-5

SU = 256.0
SW = 1024.0
SH = 64.0
UN1 = 1.0 / (SU * SW)
UN2 = 1.0 / (SH * SW)

BLK = 256
REGION = TOK + BLK
BLOCKS = (TOK * K0 + E0 * (BLK - 1)) // BLK
ROWS = E0 * REGION + BLK
WEW = F0 + 2 * D + 2

MEW = 2 * D + 2

V_WSIM, V_BQ, V_BK, V_BV, V_RB1, V_SB1, V_B1 = 0, 3, 4, 5, 6, 36, 40
NVEC, NFIRST = 48, 6
C_ID, C_TRI, C_MASK, C_IOTA, C_BASE, C_LE, C_PART = 0, 128, 256, 320, 410, 425, 650
NCONST = 651

CREDIT = 2


def done(n):
    return n + 1 + CREDIT


def free(n):
    return n + 1


def pipelined(eng, *stages):
    first = max(lag for lag, *_ in stages)
    pairs = (NQ - first) // 2

    def step(s, static, use):
        for lag, stage, *count in stages:
            if 0 <= static - lag < (count[0] if count else NQ):
                q = static - lag
                stage(s - lag, q % 2, use + q // 2)

    for s in range(first):
        step(s, s, 0)
    with eng.Fori(0, pairs) as i:
        for u in range(2):
            step(i * 2 + (first + u), first + u, i)
    for s in range(first + 2 * pairs, NQ + first):
        step(s, s, 0)


class Chain:

    def __init__(self, eng, sem):
        self.eng, self.sem, self.base, self.k = eng, sem, 0, 0

    def start(self, count):
        self.base, self.k = count, 0

    def __call__(self, ins):
        ins.then_inc(self.sem, 1)
        self.k += 1
        self.eng.wait_ge(self.sem, self.base + self.k)


def build(nc, a, const, out):
    with ExitStack() as ctx:
        def sb(name, shape, dt=F32):
            return ctx.enter_context(nc.sbuf_tensor(name, shape, dt))

        def sem(name):
            return ctx.enter_context(nc.semaphore(name))

        banks = [ctx.enter_context(nc.psum_tensor(f"bank{i}", [P, 512], F32)) for i in range(8)]

        sorted_rows = nc.dram_tensor("sorted_rows", (ROWS, 2 * D), F16, kind="Internal").ap()
        expert_rows = nc.dram_tensor("expert_rows", (BLOCKS * BLK, D), F32, kind="Internal").ap()

        X = sb("X", [P, NT, D])
        hc = sb("hc", [P, NT, D])
        hcT = sb("hcT", [P, TOK])
        AT = sb("AT", [P, TOK])
        uT = sb("uT", [P, 2, TOK], F16)

        cst = sb("cst", [P, NCONST])
        ident = cst[:, C_ID:C_ID + P]
        ident16 = sb("ident16", [P, P], F16)
        tri16 = sb("tri16", [P, P], F16)
        ones16 = sb("ones16", [P, P], F16)
        ones = sb("ones", [P, P])
        vecs, later_vecs = sb("vecs", [NFIRST, P]), sb("later_vecs", [NVEC - NFIRST, P])
        cols = sb("cols", [P, NVEC])
        rows = sb("rows", [1, 2, P])
        row_bias = sb("row_bias", [L, 2, D])
        gates = sb("gates", [P, 4])
        tg = sb("tg", [P, 4])
        bsim = sb("bsim", [1, 1])

        early = uT[:].rearrange("p h t -> p (h t)").bitcast(F32)
        ctxk = early[:, 0:1024].rearrange("p (t d) -> p t d", d=D)
        ctxT = early[:, 1024:2048]
        VmT = early[:, 2048:3072]
        Wa = early[:, 3072:3584].rearrange("p (w d) -> p w d", d=D)
        WqT = early[:, 3584:3712]
        MT = sb("MT", [P, B * L])
        KmT = sb("KmT", [P, B * L])
        QK = sb("QK", [P, B * L])
        srow = sb("srow", [1, 2, B * L])
        HW1 = sb("HW1", [L, B, D])
        VO = sb("VO", [L, B, D])
        Wqv = sb("Wqv", [P, 4, D])

        WE = sb("WE", [P, E0, WEW])
        WE16 = WE[:].rearrange("p e w -> p (e w)").bitcast(F16).rearrange("p (e w) -> p e w", e=E0)
        W1 = WE16[:, :, 0:2 * F0].rearrange("p e (h f) -> p h e f", h=2)
        W2 = WE16[:, :, 2 * F0:2 * F0 + 4 * D].rearrange("p e (h f) -> p h e f", h=2)
        S1 = sb("S1", [P, 2, FS], F16)
        S2 = sb("S2", [P, 2, FS], F16)
        ME = sb("ME", [P, E1, MEW])
        ME16 = ME[:].rearrange("p e w -> p (e w)").bitcast(F16).rearrange("p (e w) -> p e w", e=E1)
        gw = sb("gw", [P, E0])
        gw16 = sb("gw16", [P, 2, E0 + 1], F16)
        wr = sb("wr", [P, E1])
        wr16 = sb("wr16", [P, 2, E1], F16)
        b2a = sb("b2a", [E0 + 1, D])
        b2m = sb("b2m", [E1, D])
        b2m16 = sb("b2m16", [E1, 2, D], F16)

        held = {e: sem("held_" + e) for e in ("pe", "dve", "act", "pool", "sp")}

        def hold(eng, name):
            eng.sem_inc(held[name], 1)

        RAW = 512
        raw = [sb(f"raw{k}", [P, RAW]) for k in range(2)]
        load_s, load_e, load_m = sem("loaded_shared"), sem("loaded_experts"), sem("loaded_rest")
        raw_scaled, high_done, low_done = sem("raw_scaled"), sem("high_done"), sem("low_done")
        ALONE = 8

        def piece_expert(e):
            at = WE16[:, bass.ds(e, 1), 0:4 * F0].rearrange("p o (w h f) -> p h (o w) f", w=2, h=2)
            return WE[:, bass.ds(e, 1), 0:2 * F0].rearrange("p o (w f) -> p (o w) f", w=2), at[:, 0], at[:, 1], 2 * F0

        def piece_layer1(e):
            at = ME16[:, bass.ds(e, 1), 0:4 * D].rearrange("p o (w h f) -> p h (o w) f", w=2, h=2)
            return ME[:, bass.ds(e, 1), 0:2 * D].rearrange("p o (w f) -> p (o w) f", w=2), at[:, 0], at[:, 1], 2 * D

        def piece_shared(w):
            loaded = w[:].rearrange("p h f -> p (h f)").bitcast(F32).rearrange("p (o f) -> p o f", o=1)
            return loaded, w[:, 0:1], w[:, 1:2], FS

        def raw_of(k, piece):
            return raw[k][:, 0:piece[3]].rearrange("p (w f) -> p w f", w=piece[0].shape[1])

        def split_high_half(act, c, k, piece):
            if not isinstance(c, int) or c >= 2:
                act.wait_ge(low_done, c - 1)
            nc.scalar.activation(raw_of(k, piece), piece[0], ACT.Copy, scale=SW).then_inc(raw_scaled, 1)
            act.wait_ge(raw_scaled, c + 1)
            nc.scalar.copy(piece[1], raw_of(k, piece)).then_inc(high_done, 1)

        def split_low_half(pool, c, k, piece):
            pool.wait_ge(high_done, c + 1)
            nc.gpsimd.tensor_tensor(piece[2], raw_of(k, piece), piece[1], ALU.subtract).then_inc(low_done, 1)

        before = [piece_shared(S1), piece_shared(S2)] + [piece_expert(e) for e in range(ALONE, E0)]

        stats = sb("stats", [P, TQ, 6])
        mv = [sb(f"mv{i}", [P, 2 * TQ, 2]) for i in range(2)]
        rs = [sb(f"rs{i}", [P, 5, 2 * TQ]) for i in range(2)]

        def pair(name, shape, dt=F32):
            return [sb(f"{name}{i}", shape, dt) for i in range(2)]

        LN_LINKS, MV_LINKS = 11, 2

        def mean_variance(dve, link, x, par, second=0):
            hold(dve, "dve")
            for j in range(TQ):
                ins = nc.vector.bn_stats(stats[:, j, :], x[:, j, :])
            link(ins)
            hold(dve, "dve")
            for j in range(TQ):
                ins = nc.vector.bn_aggr(mv[par][:, second * TQ + j, :], stats[:, j, :])
            link(ins)

        def scales_of(dve, link, par, done_sem, norms=1):
            v, y, t, w, shift = (rs[par][:, i, 0:norms * TQ] for i in range(5))
            mean, var = (mv[par][:, 0:norms * TQ, i] for i in range(2))
            link(nc.vector.tensor_scalar(v, var, EPS, None, ALU.add))
            link(nc.vector.tensor_scalar(t.bitcast(I32), v.bitcast(I32), 1, None, ALU.logical_shift_right))
            link(nc.vector.tensor_scalar(y.bitcast(I32), t.bitcast(I32), -1.0, float(0x5f1ffff9), ALU.mult, ALU.add))
            for b, c in ((0.703952253, 0.703952253 * 2.38924456), (0.5 * (1 + 3.2e-7), 1.5 * (1 + 3.2e-7))):
                link(nc.vector.scalar_tensor_tensor(t, y, -b, y, ALU.mult, ALU.mult))
                link(nc.vector.tensor_tensor(w, t, v, ALU.mult))
                link(nc.vector.scalar_tensor_tensor(y, w, c, y, ALU.add, ALU.mult))
            nc.vector.scalar_tensor_tensor(shift, mean, -1.0, y, ALU.mult, ALU.mult).then_inc(done_sem, 1)

        def row_scales(dve, link, x, par, done_sem):
            mean_variance(dve, link, x, par)
            scales_of(dve, link, par, done_sem)

        def normalise_rows(x, dst, par, second=0):
            for j in range(TQ):
                ins = nc.scalar.activation(dst[:, j, :], x[:, j, :], ACT.Identity,
                                           bias=rs[par][:, 4, second * TQ + j:second * TQ + j + 1],
                                           scale=rs[par][:, 1, second * TQ + j:second * TQ + j + 1])
            return ins

        def xt(n):
            return X[:, bass.ds(n * TPB, TPB), :]

        def xq(n):
            return X[:, bass.ds(n * TQ, TQ), :]

        def tiles(ap):
            return ap.rearrange("p (t d) -> p t d", t=TQ)

        def spread(ap, width):
            return ap.rearrange("p (t o) -> p t o", o=1).broadcast_to([P, TQ, width])

        ld_first, ld_late, ld_ctx, ld_x, ld_wa = (sem(s) for s in ("ld_first", "ld_late", "ld_ctx", "ld_x", "ld_wa"))
        s_pe, s_dve, s_pool, s_consts = (sem(s) for s in ("setup_pe", "setup_dve", "setup_pool", "setup_consts"))
        zeros = sb("zeros", [P, 4 * D], F16)
        with nc.Block() as block:
            @block.sync
            def _(sp):
                def column(name):
                    return a[name].rearrange("(r c) -> r c", c=P)

                def row(name):
                    return a[name].rearrange("(r c) -> r c", r=1)

                sp.dma_start(cst[:], const).then_inc(ld_first, 16)
                for at, n, src in ((V_WSIM, 3, column("L0_xattn_w_sim")), (V_BQ, 1, column("L1_xattn_bq")),
                                   (V_BK, 1, column("L1_xattn_bk")), (V_BV, 1, column("L1_xattn_bv"))):
                    sp.dma_start(vecs[at:at + n, :], src).then_inc(ld_first, 16)
                sp.dma_start(bsim[:], row("L0_xattn_b_sim")).then_inc(ld_first, 16)
                for i, name in enumerate(("L0_xattn_b_qv", "L1_xattn_bo")):
                    sp.dma_start(row_bias[:, i, :], row(name).broadcast_to([L, D])).then_inc(ld_first, 16)
                for g in range(4):
                    sp.dma_start(X[:, 8 * g:8 * g + 8, :],
                                 a["x"].rearrange("b (t p) d -> p (b t) d", p=P)[:, 8 * g:8 * g + 8, :]).then_inc(ld_x, 16)
                for at, n, src in ((V_RB1, 30, a["L0_ffn_rb1"].rearrange("e (r c) -> (e r) c", c=P)),
                                   (V_SB1, 4, a["L0_ffn_sb1"].rearrange("e (r c) -> (e r) c", c=P)),
                                   (V_B1, 8, a["L1_ffn_b1"])):
                    sp.dma_start(later_vecs[at - NFIRST:at - NFIRST + n, :], src).then_inc(ld_late, 16)
                for i, (name, n) in enumerate((("L0_ffn_gb", E0), ("L1_ffn_br", E1))):
                    sp.dma_start(rows[:, i, 0:n], row(name)).then_inc(ld_late, 16)
                for i, name in enumerate(("g_xattn", "g_ffn")):
                    sp.dma_start(gates[:, 2 * i:2 * i + 2], row(name).broadcast_to([P, 2])).then_inc(ld_late, 16)
                sp.dma_start(gw[:], a["L0_ffn_gW"]).then_inc(ld_late, 16)
                sp.dma_start(wr[:], a["L1_ffn_Wr"]).then_inc(ld_late, 16)
                sp.dma_start(b2a[0:E0, :], a["L0_ffn_rb2"]).then_inc(ld_late, 16)
                sp.dma_start(b2a[E0:E0 + 1, :], a["L0_ffn_sb2"]).then_inc(ld_late, 16)
                sp.dma_start(b2m[:], a["L1_ffn_b2"]).then_inc(ld_late, 16)

            N_FIRST, N_LATE = 8, 12

            @block.gpsimd
            def _(pool):
                nc.gpsimd.memset(zeros[:], 0.0)
                nc.gpsimd.memset(ones[:], 1.0).then_inc(s_pool, 1)
                nc.gpsimd.memset(ones16[:], 1.0).then_inc(s_pool, 1)
                pool.wait_ge(ld_first, 16 * N_FIRST)
                nc.gpsimd.tensor_copy(ident16[:], ident).then_inc(s_pool, 1)
                nc.gpsimd.tensor_copy(tri16[:], cst[:, C_TRI:C_TRI + P]).then_inc(s_pool, 1)
                for c, piece in enumerate(before):
                    split_low_half(pool, c, c % 2, piece)

            @block.scalar
            def _(act):
                act.dma_start(ctxk, a["ctx_1024"].rearrange("(t b) s d -> (b s) t d", b=P // L)).then_inc(ld_ctx, 16)
                act.dma_start(Wqv[:], a["L0_xattn_W_qv"].rearrange("(c p) d -> p c d", p=P)).then_inc(ld_wa, 16)
                for i, name in enumerate(("L1_xattn_Wq", "L1_xattn_Wk", "L1_xattn_Wv", "L1_xattn_Wo")):
                    act.dma_start(Wa[:, i, :], a[name]).then_inc(ld_wa, 16)
                def raw_loads(e0, e1, s):
                    act.dma_start(WE[:, e0:e1, 0:F0], a["L0_ffn_rW1"].rearrange("e p f -> p e f")[:, e0:e1]).then_inc(s, 16)
                    for c in range(2):
                        act.dma_start(WE[:, e0:e1, F0 + c * D:F0 + (c + 1) * D],
                                      a["L0_ffn_rW2"][e0:e1, c * P:(c + 1) * P, :].rearrange("e p d -> p e d")).then_inc(s, 16)

                def loaded(w):
                    return w[:].rearrange("p h f -> p (h f)").bitcast(F32)

                act.dma_start(loaded(S1), a["L0_ffn_sW1"].rearrange("e p f -> p (e f)")).then_inc(load_s, 16)
                act.dma_start(loaded(S2).rearrange("p (c d) -> p c d", c=4),
                              a["L0_ffn_sW2"].rearrange("e (c p) d -> p (e c) d", p=P)).then_inc(load_s, 16)
                raw_loads(ALONE, E0, load_e)
                raw_loads(0, ALONE, load_m)
                act.dma_start(ME[:, :, 0:D], a["L1_ffn_W1"].rearrange("e p f -> p e f")).then_inc(load_m, 16)
                act.dma_start(ME[:, :, D:2 * D], a["L1_ffn_W2"].rearrange("e p f -> p e f")).then_inc(load_m, 16)
                act.wait_ge(load_s, 16 * 2)
                for c, piece in enumerate(before):
                    if c == 2:
                        act.wait_ge(load_e, 16 * 3)
                    split_high_half(act, c, c % 2, piece)
                act.wait_ge(ld_late, 16 * N_LATE)
                nc.scalar.activation(tg[:], gates[:], ACT.Tanh).then_inc(s_consts, 1)

            @block.vector
            def _(dve):
                link = Chain(dve, s_dve)
                dve.wait_ge(ld_first, 16 * N_FIRST)
                dve.wait_ge(s_pe, 1)
                link(nc.vector.tensor_copy(cols[:, 0:NFIRST], banks[0][:, 0:NFIRST]))
                nc.vector.tensor_scalar(row_bias[:, 1, :], row_bias[:, 1, :], 1.0 / HEADS, None, ALU.mult)
                dve.wait_ge(s_pe, 2)
                link(nc.vector.tensor_copy(WqT, banks[1][:, 0:D]))
                for h in range(2):
                    dve.wait_ge(s_pe, 3 + h)
                    link(nc.vector.tensor_copy(ctxT[:, 512 * h:512 * h + 512], banks[2 + h][:]))
                link(nc.vector.tensor_scalar(MT[:], ctxT, cols[:, V_WSIM + 2:V_WSIM + 3],
                                             cols[:, V_WSIM:V_WSIM + 1], ALU.mult, ALU.add))
                mask = cst[:, C_MASK:C_MASK + L].rearrange("p (o s) -> p o s", o=1).broadcast_to([P, 8, L])
                for h in range(2):
                    dve.wait_ge(s_pe, 5 + h)
                    link(nc.vector.scalar_tensor_tensor(
                        KmT[:, 512 * h:512 * h + 512].rearrange("p (b s) -> p b s", s=L),
                        banks[4 + h][:].rearrange("p (b s) -> p b s", s=L),
                        cols[:, V_BK:V_BK + 1], mask, ALU.add, ALU.mult))
                link(nc.vector.tensor_scalar(KmT[:], KmT[:], float(HD) ** -0.5, None, ALU.mult))
                for h in range(2):
                    dve.wait_ge(s_pe, 7 + h)
                    link(nc.vector.scalar_tensor_tensor(
                        VmT[:, 512 * h:512 * h + 512].rearrange("p (b s) -> p b s", s=L),
                        banks[6 + h][:].rearrange("p (b s) -> p b s", s=L),
                        cols[:, V_BV:V_BV + 1], mask, ALU.add, ALU.mult))
                for h in range(2):
                    dve.wait_ge(s_pe, 9 + h)
                    link(nc.vector.tensor_scalar(srow[0:1, 0, 512 * h:512 * h + 512], banks[h][0:1, :], bsim[0:1, 0:1],
                                                 None, ALU.add))
                for h in range(2):
                    dve.wait_ge(s_pe, 11 + h)
                    link(nc.vector.tensor_copy(srow[0:1, 1, 512 * h:512 * h + 512], banks[2 + h][0:1, :]))
                for h in range(2):
                    dve.wait_ge(s_pe, 13 + h)
                    link(nc.vector.tensor_copy(QK[:, 512 * h:512 * h + 512], banks[4 + h][:]))
                def bias_rows(i):
                    return row_bias[:, i:i + 1, :].broadcast_to([L, 4, D])

                for q in range(4):
                    dve.wait_ge(s_pe, 15 + q)
                    link(nc.vector.tensor_tensor(HW1[:, 4 * q:4 * q + 4, :],
                                                 banks[q][0:L, :].rearrange("p (b d) -> p b d", d=D), bias_rows(0), ALU.add))
                for q in range(4):
                    dve.wait_ge(s_pe, 19 + q)
                    link(nc.vector.tensor_tensor(VO[:, 4 * q:4 * q + 4, :],
                                                 banks[4 + q][0:L, :].rearrange("p (b d) -> p b d", d=D), bias_rows(1), ALU.add))
                dve.wait_ge(ld_late, 16 * N_LATE)
                nc.vector.tensor_scalar(gw16[:, 0, 0:E0], gw[:], SW, None, ALU.mult)
                nc.vector.tensor_scalar(rows[:, 0, 0:E0], rows[:, 0, 0:E0], SU * SW, None, ALU.mult)
                nc.vector.tensor_scalar(rows[:, 1, 0:E1], rows[:, 1, 0:E1], SU * SW, None, ALU.mult)
                nc.vector.tensor_scalar(b2a[:], b2a[:], SH * SW, None, ALU.mult)
                nc.vector.tensor_scalar(b2m16[:, 0, :], b2m[:], SW, None, ALU.mult)
                link(nc.vector.tensor_scalar(wr16[:, 0, :], wr[:], SW, None, ALU.mult))
                nc.vector.scalar_tensor_tensor(gw16[:, 1, 0:E0], gw[:], SW, gw16[:, 0, 0:E0], ALU.mult, ALU.subtract)
                nc.vector.scalar_tensor_tensor(b2m16[:, 1, :], b2m[:], SW, b2m16[:, 0, :], ALU.mult, ALU.subtract)
                nc.vector.scalar_tensor_tensor(wr16[:, 1, :], wr[:], SW, wr16[:, 0, :], ALU.mult, ALU.subtract)
                dve.wait_ge(s_pe, 23)
                link(nc.vector.tensor_copy(cols[:, NFIRST:NVEC], banks[1][:, 0:NVEC - NFIRST]))
                nc.vector.tensor_copy(WE[:, :, F0 + 2 * D:WEW],
                                      cols[:, V_RB1:V_RB1 + 2 * E0].rearrange("p (e c) -> p e c", c=2))
                for c in range(2):
                    nc.vector.tensor_copy(ME[:, :, 2 * D + c:2 * D + c + 1],
                                          cols[:, V_B1:V_B1 + E1].rearrange("p (e o) -> p e o", o=1))
                dve.wait_ge(ld_x, 16 * 4)

            @block.tensor
            def _(pe):
                mm = nc.tensor.matmul
                pe.wait_ge(ld_first, 16 * N_FIRST)
                pe.wait_ge(s_pool, 4)
                nc.tensor.transpose(banks[0][:, 0:NFIRST], vecs[:], ident[0:NFIRST, 0:NFIRST]).then_inc(s_pe, 1)
                pe.wait_ge(ld_wa, 16 * 5)
                nc.tensor.transpose(banks[1][:, 0:D], Wa[:, 0, :], ident).then_inc(s_pe, 1)
                pe.wait_ge(ld_ctx, 16)
                for h in range(2):
                    for t in range(4):
                        ins = nc.tensor.transpose(banks[2 + h][:, t * P:(t + 1) * P], ctxk[:, 4 * h + t, :], ident)
                    ins.then_inc(s_pe, 1)
                pe.wait_ge(s_dve, 4)
                for h in range(2):
                    mm(banks[4 + h][:], Wa[:, 1, :], ctxT[:, 512 * h:512 * h + 512], start=True, stop=True).then_inc(s_pe, 1)
                for h in range(2):
                    mm(banks[6 + h][:], Wa[:, 2, :], ctxT[:, 512 * h:512 * h + 512], start=True, stop=True).then_inc(s_pe, 1)
                for h in range(2):
                    mm(banks[h][0:1, :], cols[:, V_WSIM + 1:V_WSIM + 2], ctxT[:, 512 * h:512 * h + 512],
                       start=True, stop=True).then_inc(s_pe, 1)
                pe.wait_ge(s_dve, 8)
                for h in range(2):
                    mm(banks[2 + h][0:1, :], cols[:, V_BQ:V_BQ + 1], KmT[:, 512 * h:512 * h + 512],
                       start=True, stop=True).then_inc(s_pe, 1)
                for h in range(2):
                    mm(banks[4 + h][:], WqT, KmT[:, 512 * h:512 * h + 512], start=True, stop=True).then_inc(s_pe, 1)
                for q in range(4):
                    pe.wait_ge(s_dve, 11 + q)
                    for b in range(4 * q, 4 * q + 4):
                        o = banks[q][0:L, (b % 4) * D:(b % 4 + 1) * D]
                        ins = mm(o, ctxT[:, b * L:(b + 1) * L], Wqv[:, 1, :], start=True, stop=True)
                    ins.then_inc(s_pe, 1)
                for q in range(4):
                    pe.wait_ge(s_dve, 16)
                    for b in range(4 * q, 4 * q + 4):
                        o = banks[4 + q][0:L, (b % 4) * D:(b % 4 + 1) * D]
                        ins = mm(o, VmT[:, b * L:(b + 1) * L], Wa[:, 3, :], start=True, stop=True)
                    ins.then_inc(s_pe, 1)
                pe.wait_ge(ld_late, 16 * N_LATE)
                pe.wait_ge(s_dve, 18)
                nc.tensor.transpose(banks[1][:, 0:NVEC - NFIRST], later_vecs[:],
                                    ident[0:NVEC - NFIRST, 0:NVEC - NFIRST]).then_inc(s_pe, 1)

        uTf = uT[:].rearrange("p h t -> p (h t)").bitcast(F32)
        diff = [tiles(uTf[:, 256 * k:256 * k + 256]) for k in range(2)]
        prob = [tiles(uTf[:, 512 + 256 * k:768 + 256 * k]) for k in range(2)]
        ln_out, xT_s = pair("ln_out", [P, TQ, D]), pair("xT_s", [P, QTOK])
        m_all = sb("m_all", [P, NT])
        den = pair("den", [P, TQ])

        with nc.Block() as block:
            (hc_ready, hc_saved, hcT_psum, hcT_ready, hcT_saved, sim_psum, diff_ready, exp_ready, prob_ready,
             AT_psum, AT_saved, a0_scales, a0_ln, a0_max, a0_sum) = (sem("a0_" + s) for s in (
                "hc_ready", "hc_saved", "hcT_psum", "hcT_ready", "hcT_saved", "sim_psum", "diff_ready", "exp_ready",
                "prob_ready", "AT_psum", "AT_saved", "row_scales", "ln_chain", "max_chain", "sum_chain"))
            T, S, A = banks[0:2], banks[2:4], banks[4:6]
            FIRST = len(before)

            @block.gpsimd
            def _(pool):
                pool.sem_inc(hc_saved, CREDIT)

                def save(n, par, use):
                    pool.wait_ge(hc_ready, done(n))
                    nc.gpsimd.tensor_copy(hc[:, bass.ds(n * TQ, TQ), :], ln_out[par][:]).then_inc(hc_saved, 1)

                def weights(n, par, use):
                    split_low_half(pool, n * 2 + FIRST, FIRST % 2, piece_expert(n))
                    split_low_half(pool, n * 2 + (FIRST + 1), (FIRST + 1) % 2, piece_layer1(n))

                pipelined(pool, (0, save), (0, weights))

            @block.vector
            def _(dve):
                for s in (a0_scales, diff_ready, prob_ready):
                    dve.sem_inc(s, CREDIT)
                ln_link, max_link, sum_link = Chain(dve, a0_ln), Chain(dve, a0_max), Chain(dve, a0_sum)

                def scales(n, par, use):
                    ln_link.start(n * (LN_LINKS))
                    dve.wait_ge(hc_ready, free(n))
                    row_scales(dve, ln_link, xq(n), par, a0_scales)

                def less_maximum(n, par, use):
                    max_link.start(n)
                    s = tiles(S[par][:, 0:TQ * L])
                    dve.wait_ge(sim_psum, done(n))
                    m = m_all[:, bass.ds(n * TQ, TQ)]
                    max_link(nc.vector.tensor_reduce(m, s, AX, ALU.max))
                    nc.vector.tensor_tensor(diff[par], s, spread(m, L), ALU.subtract).then_inc(diff_ready, 1)

                def probabilities(n, par, use):
                    sum_link.start(2 * n)
                    dve.wait_ge(exp_ready, done(n))
                    sum_link(nc.vector.tensor_reduce(den[par][:], diff[par], AX, ALU.add))
                    sum_link(nc.vector.reciprocal(den[par][:], den[par][:]))
                    dve.wait_ge(AT_psum, free(n))
                    nc.vector.tensor_tensor(prob[par], diff[par], spread(den[par][:], L), ALU.mult).then_inc(prob_ready, 1)

                pipelined(dve, (0, scales), (1, less_maximum), (2, probabilities))

            @block.scalar
            def _(act):
                for s in (hc_ready, hcT_ready, hcT_saved, exp_ready, AT_saved):
                    act.sem_inc(s, CREDIT)

                def normalise(n, par, use):
                    act.wait_ge(a0_scales, done(n))
                    act.wait_ge(hc_saved, free(n))
                    act.wait_ge(hcT_psum, free(n))
                    normalise_rows(xq(n), ln_out[par], par).then_inc(hc_ready, 1)

                def exponentials(n, par, use):
                    act.wait_ge(diff_ready, done(n))
                    nc.scalar.activation(diff[par], diff[par], ACT.Exp).then_inc(exp_ready, 1)

                def save_tokens(n, par, use):
                    act.wait_ge(hcT_psum, done(n))
                    act.wait_ge(sim_psum, free(n))
                    nc.scalar.copy(xT_s[par][:], T[par][:]).then_inc(hcT_ready, 1)
                    nc.scalar.copy(hcT[:, bass.ds(n * QTOK, QTOK)], T[par][:]).then_inc(hcT_saved, 1)

                def save_probabilities(n, par, use):
                    act.wait_ge(AT_psum, done(n))
                    nc.scalar.copy(AT[0:L, bass.ds(n * QTOK, QTOK)], A[par][0:L, :]).then_inc(AT_saved, 1)

                def weights(n, par, use):
                    split_high_half(act, n * 2 + FIRST, FIRST % 2, piece_expert(n))
                    split_high_half(act, n * 2 + (FIRST + 1), (FIRST + 1) % 2, piece_layer1(n))

                act.wait_ge(load_m, 16 * 5)
                pipelined(act, (0, normalise), (0, save_tokens), (1, exponentials), (3, save_probabilities), (0, weights))

            @block.tensor
            def _(pe):
                for s in (hcT_psum, sim_psum, AT_psum):
                    pe.sem_inc(s, CREDIT)

                def transpose_tokens(n, par, use):
                    pe.wait_ge(hc_ready, done(n))
                    pe.wait_ge(hcT_saved, free(n))
                    for j in range(TQ):
                        ins = nc.tensor.transpose(T[par][:, j * P:(j + 1) * P], ln_out[par][:, j, :], ident)
                    ins.then_inc(hcT_psum, 1)

                def similarity(n, par, use):
                    pe.wait_ge(hcT_ready, done(n))
                    pe.wait_ge(diff_ready, free(n))
                    for j in range(TQ):
                        keys = bass.ds((n * 2 + j // TPB) * L, L)
                        o = S[par][:, j * L:(j + 1) * L]
                        nc.tensor.matmul(o, xT_s[par][:, j * P:(j + 1) * P], MT[:, keys], start=True, stop=False)
                        ins = nc.tensor.matmul(o, ones[0:1, :], srow[0:1, 0, keys], start=False, stop=True)
                    ins.then_inc(sim_psum, 1)

                def transpose_probabilities(n, par, use):
                    pe.wait_ge(prob_ready, done(n))
                    pe.wait_ge(AT_saved, free(n))
                    hold(pe, "pe")
                    for j in range(TQ):
                        ins = nc.tensor.transpose(A[par][0:L, j * P:(j + 1) * P], prob[par][:, j, :], ident)
                    ins.then_inc(AT_psum, 1)

                pipelined(pe, (0, transpose_tokens), (0, similarity), (2, transpose_probabilities))

        hcb = sb("hcb", [P, B])
        batt = sb("batt", [P, NT])
        tgs = sb("tgs", [P, 2])
        pm = sb("pm", [P, B])
        m32 = sb("m32", [NT, 1])
        spread_w = uTf[:, 0:B * (B * TPB + 1)]
        pooled = sb("pooled", [B, D])
        with nc.Block() as block:
            p_pe, p_dve, p_act, p_zero = sem("p0_pe"), sem("p0_dve"), sem("p0_act"), sem("p0_zero")

            @block.gpsimd
            def _(pool):
                nc.gpsimd.memset(spread_w, 0.0).then_inc(p_zero, 1)

            @block.tensor
            def _(pe):
                nc.tensor.transpose(banks[0][0:NT, 0:P], m_all[:], ident).then_inc(p_pe, 1)
                pe.wait_ge(p_dve, 1)
                nc.tensor.matmul(banks[1][0:1, 0:NT], m32[:], ident[0:NT, 0:NT], start=True, stop=True).then_inc(p_pe, 1)
                pe.wait_ge(p_dve, 2)
                nc.tensor.matmul(banks[2][:, 0:B], ones[0:1, :], pm[0:1, :], start=True, stop=True).then_inc(p_pe, 1)
                pe.wait_ge(p_act, 1)
                nc.tensor.matmul(banks[3][:, 0:NT], ones[:], batt[:], start=True, stop=True).then_inc(p_pe, 1)
                pe.wait_ge(p_dve, 6)
                for t in range(NT):
                    ins = nc.tensor.matmul(banks[4][0:B, 0:D], spread_w[:, t * B:(t + 1) * B], hc[:, t, :],
                                           start=(t == 0), stop=(t == NT - 1))
                ins.then_inc(p_pe, 1)
                pe.wait_ge(p_dve, 7)
                nc.tensor.transpose(banks[5][:, 0:B], pooled[:], ident[0:B, 0:B]).then_inc(p_pe, 1)

            @block.scalar
            def _(act):
                act.wait_ge(p_dve, 3)
                nc.scalar.activation(batt[:], batt[:], ACT.Exp).then_inc(p_act, 1)

            @block.vector
            def _(dve):
                link = Chain(dve, p_dve)
                dve.wait_ge(p_pe, 1)
                link(nc.vector.tensor_reduce(m32[:], banks[0][0:NT, 0:P], AX, ALU.max))
                dve.wait_ge(p_pe, 2)
                link(nc.vector.tensor_reduce(pm[0:1, :], banks[1][0:1, 0:NT].rearrange("p (b t) -> p b t", t=TPB), AX, ALU.max))
                dve.wait_ge(p_pe, 3)

                def by_batch(ap):
                    return ap.rearrange("p (b t) -> p b t", t=TPB)

                def spread(ap):
                    return ap.rearrange("p (b o) -> p b o", o=1).broadcast_to([P, B, TPB])

                link(nc.vector.tensor_tensor(by_batch(batt[:]), by_batch(m_all[:]), spread(banks[2][:, 0:B]), ALU.subtract))
                dve.wait_ge(p_pe, 4)
                link(nc.vector.tensor_reduce(pm[:], by_batch(banks[3][:, 0:NT]), AX, ALU.add))
                link(nc.vector.reciprocal(pm[:], pm[:]))
                dve.wait_ge(p_zero, 1)
                diagonal = spread_w.rearrange("p (b s) -> p b s", b=B)[:, :, 0:B + 1:B]
                link(nc.vector.tensor_tensor(diagonal, by_batch(batt[:]), spread(pm[:]), ALU.mult))
                nc.vector.tensor_scalar(tgs[:, 0:1], tg[:, 2:3], UN2, None, ALU.mult)
                nc.vector.tensor_scalar(tgs[:, 1:2], tg[:, 3:4], UN2 / K1, None, ALU.mult)
                dve.wait_ge(p_pe, 5)
                link(nc.vector.tensor_copy(pooled[:], banks[4][0:B, 0:D]))
                dve.wait_ge(p_pe, 6)
                link(nc.vector.tensor_copy(hcb[:], banks[5][:, 0:B]))

        NK = TQ * K0
        hcf = hc[:].rearrange("p t d -> p (t d)")
        u16 = hcf.bitcast(F16).rearrange("p (t w) -> p t w", w=2 * D)
        AT_s = [MT[0:L, QTOK * k:QTOK * (k + 1)] for k in range(2)]
        prod = [KmT[:, QTOK * k:QTOK * (k + 1)] for k in range(2)]
        ctx_s, Wp = pair("ctx_s", [L, 2, D]), pair("Wp", [P, 2, D])
        v8, i8 = pair("v8", [P, TQ, 8]), pair("i8", [P, TQ, 8], U32)
        el, idxf = pair("el", [P, TQ, E0]), pair("idxf", [P, NK])
        oh, ohx = pair("oh", [P, NK, E0]), sb("ohx", [P, NK, E0])
        Msum, M16, Gs = pair("Msum", [P, TQ, E0]), pair("M16", [P, TQ, E0], F16), pair("Gs", [P, TQ, E0 + 1])
        S16 = pair("S16", [P, E0], F16)
        pos = sb("pos", [P, NT * K0], I32)
        gk = sb("gk", [P, NT * K0])
        ctmp = sb("ctmp", [P, E0])
        GT = hcT[0:E0 + 1, :]
        scat = [sem(f"scattered{i}") for i in range(2)]

        tw = sb("tw", [P, 8, E0])
        tcum = sb("tcum", [P, E0, E0])
        ti = sb("ti", [P, 2, E0], I32)
        tabc = sb("tabc", [P, 2])
        moved = uTf[:, 0:NT * K0 * (E0 - 1)].rearrange("p (c e) -> p c e", e=E0 - 1)
        shift = sb("shift", [P, NT * K0])
        places = sb("places", [P, NT * K0], I32)
        tab = sb("tab", [1, 2, P], I32)
        crow = sb("crow", [1, E0], I32)
        EARLY = NQ - 2
        mix = ([MT[:, QTOK * k:QTOK * (k + 1)] for k in range(2)],
               AT[:].bitcast(F16).rearrange("p (g h c t) -> p g h c t", g=2, h=2, c=4),
               [KmT[:, QTOK * k:QTOK * (k + 1)] for k in range(2)])
        late_mix = ([AT[:, QTOK * k:QTOK * (k + 1)] for k in range(2)],
                    hcf.bitcast(F16).rearrange("p (g h c t) -> p g h c t", g=2, h=2, c=4), mix[2])
        s_h, s_hf, s_lo, s_y, s_yc, s_t, s_x, s_lk = (sem("sh_" + s) for s in (
            "h_psum", "gelu", "split", "y_psum", "y_copied", "t_psum", "x", "chain"))

        def shared_hidden(g, c, pe):
            mm = nc.tensor.matmul
            pe.wait_ge(s_hf, free(g * 4 + c))
            cs = slice(c * P, (c + 1) * P)
            ug, ul = (uT[:, h, bass.ds(g * QTOK, QTOK)] for h in range(2))
            mm(banks[c % 2][:], S1[:, 0, cs], ug, start=True, stop=False)
            mm(banks[c % 2][:], S1[:, 1, cs], ug, start=False, stop=False)
            mm(banks[c % 2][:], S1[:, 0, cs], ul, start=False, stop=True).then_inc(s_h, 1)

        def shared_back(g, par, pe, mix):
            yT = mix[2][par]
            pe.wait_ge(s_yc, done(g))
            pe.wait_ge(s_x, free(g))
            for j in range(TQ):
                ins = nc.tensor.transpose(banks[4 + par][:, j * P:(j + 1) * P], yT[:, j * P:(j + 1) * P], ident)
            ins.then_inc(s_t, 1)

        def shared_outputs(g, par, pe, mix, first=False, last=False):
            mm, hid, Y = nc.tensor.matmul, mix[1], banks[2 + par]
            for c in range(4):
                if not last:
                    shared_hidden(g + 1, c, pe)
                if c == 0:
                    pe.wait_ge(s_yc, free(g))
                    mm(Y[:], b2a[:], GT[:, bass.ds(g * QTOK, QTOK)], start=True, stop=False)
                cs = slice(c * P, (c + 1) * P)
                pe.wait_ge(s_lo, done(g * 4 + c))
                mm(Y[:], S2[:, 0, cs], hid[:, par, 0, c, :], start=False, stop=False)
                mm(Y[:], S2[:, 1, cs], hid[:, par, 0, c, :], start=False, stop=False)
                ins = mm(Y[:], S2[:, 0, cs], hid[:, par, 1, c, :], start=False, stop=(c == 3))
                if c == 3:
                    ins.then_inc(s_y, 1)
                if c == 1 and not first:
                    shared_back(g - 1, 1 - par, pe, mix)

        def shared_gelu(g, c, act, mix):
            q, hf = g * 4 + c, mix[0][c % 2]
            act.wait_ge(s_h, done(q))
            act.wait_ge(s_lo, free(q))
            nc.scalar.activation(hf, banks[c % 2][:], ACT.Gelu, bias=cols[:, V_SB1 + c:V_SB1 + c + 1], scale=UN1
                                 ).then_inc(s_hf, 1)

        def shared_copy(g, par, act, mix):
            act.wait_ge(s_y, done(g))
            act.wait_ge(s_t, free(g))
            nc.scalar.copy(mix[2][par], banks[2 + par][:]).then_inc(s_yc, 1)

        def shared_split(g, par, dve, link, mix):
            for c in range(4):
                q, hf, hid = g * 4 + c, mix[0][c % 2], mix[1]
                link.start(q)
                dve.wait_ge(s_hf, done(q))
                dve.wait_ge(s_y, free(g))
                link(nc.vector.tensor_scalar(hid[:, par, 0, c, :], hf, SH, None, ALU.mult))
                nc.vector.scalar_tensor_tensor(hid[:, par, 1, c, :], hf, SH, hid[:, par, 0, c, :],
                                               ALU.mult, ALU.subtract).then_inc(s_lo, 1)

        def shared_add(g, par, dve):
            dve.wait_ge(s_t, done(g))
            nc.vector.scalar_tensor_tensor(xq(g), tiles(banks[4 + par][:]), tgs[:, 0:1], xq(g),
                                           ALU.mult, ALU.add).then_inc(s_x, 1)

        with nc.Block() as block:
            (st_ready, q_psum, wp_ready, prod_ready, o_psum, o_read, u16_ready, ut_psum, ut_saved, lg_psum, d_ready,
             e_ready, m_ready, r_psum, idx_ready, g_ready, gt_psum, gt_saved, counted, r0_scales, ln_ready, hi_ready, x_done, gk_done, ln_chain, top_chain, idx_chain) = (
                sem("r0_" + s) for s in (
                    "st_ready", "q_psum", "wp_ready", "prod_ready", "o_psum", "o_read", "u16_ready", "ut_psum", "ut_saved",
                    "lg_psum", "d_ready", "e_ready", "m_ready", "r_psum", "idx_ready", "g_ready", "gt_psum",
                    "gt_saved", "counted", "row_scales", "ln_ready", "hi_ready", "x_done", "gk_done", "ln_chain", "top_chain", "idx_chain"))
            ctx_ld = [sem(f"r0_ctx_loaded{i}") for i in range(2)]
            Q, O, TU, LG, GB = banks[0:2], banks[2:4], banks[4], banks[5:7], banks[7]
            LA, LB, LD = 1 + LN_LINKS, 6, 6

            def column(bank, at):
                return bank[:, at:at + TQ * 16].rearrange("p (t e) -> p t e", e=16)[:, :, 0:E0]

            @block.sync
            def _(sp):
                def load_context(n, par, use):
                    sp.wait_ge(q_psum, free(n))
                    sp.dma_start(ctx_s[par][:], a["ctx_1024"][bass.ds(n * 2, 2)].rearrange("o s d -> s o d")
                                 ).then_inc(ctx_ld[par], 16)

                pipelined(sp, (0, load_context))

            @block.gpsimd
            def _(pool):
                for par in range(2):
                    r0 = E0 * REGION + par * P
                    pool.dma_start(sorted_rows[r0:r0 + P, :], zeros[:, 0:2 * D]).then_inc(scat[par], 16)

                def scatter(n):
                    pool.wait_ge(idx_ready, done(n))
                    hold(pool, "pool")
                    for c in range(NK):
                        nc.gpsimd.indirect_dma_start(
                            out=sorted_rows, out_offset=bass.IndirectOffsetOnAxis(ap=pos[:, n * NK + c:n * NK + c + 1], axis=0),
                            in_=u16[:, n * TQ + c // K0, :], in_offset=None).then_inc(scat[n % 2], 16)

                for n in range(NQ):
                    scatter(n)

            @block.scalar
            def _(act):
                for s in (st_ready, ut_saved, e_ready, gt_saved, ln_ready, hi_ready):
                    act.sem_inc(s, CREDIT)

                def split_high(n, par, use):
                    act.wait_ge(r0_scales, done(n))
                    act.wait_ge(o_read, done(n))
                    normalise_rows(xq(n), ln_out[par], par).then_inc(ln_ready, 1)
                    act.wait_ge(ln_ready, done(n))
                    nc.scalar.activation(u16[:, bass.ds(n * TQ, TQ), 0:D], ln_out[par][:], ACT.Copy, scale=SU
                                         ).then_inc(hi_ready, 1)

                def stage_tokens(n, par, use):
                    act.wait_ge(o_psum, free(n))
                    act.wait_ge(prod_ready, free(n))
                    nc.scalar.copy(AT_s[par], AT[0:L, bass.ds(n * QTOK, QTOK)])
                    nc.scalar.copy(xT_s[par][:], hcT[:, bass.ds(n * QTOK, QTOK)]).then_inc(st_ready, 1)

                def exponentials(n, par, use):
                    act.wait_ge(d_ready, done(n))
                    nc.scalar.activation(el[par][:], el[par][:], ACT.Exp, scale=UN1).then_inc(e_ready, 1)

                def save_rows(n, par, use):
                    act.wait_ge(ut_psum, done(n))
                    nc.scalar.copy(uT[:, :, bass.ds(n * QTOK, QTOK)],
                                   TU[:].bitcast(F16).rearrange("p (h t) -> p h t", h=2)).then_inc(ut_saved, 1)

                def save_gates(n, par, use):
                    act.wait_ge(gt_psum, done(n))
                    nc.scalar.copy(GT[:, bass.ds(n * QTOK, QTOK)], GB[0:E0 + 1, :]).then_inc(gt_saved, 1)

                pipelined(act, (0, stage_tokens), (3, exponentials), (1, split_high), (3, save_gates), (1, save_rows))

            @block.vector
            def _(dve):
                for s in (wp_ready, prod_ready, o_read, r0_scales, u16_ready, d_ready, m_ready, idx_ready, g_ready):
                    dve.sem_inc(s, CREDIT)
                ln_link, top_link, idx_link = Chain(dve, ln_chain), Chain(dve, top_chain), Chain(dve, idx_chain)
                for par in range(2):
                    nc.vector.memset(Gs[par][:], 1.0)
                nc.vector.tensor_scalar(S16[0][:], cst[:, C_BASE:C_BASE + E0], 1.0 / P, None, ALU.mult).then_inc(counted, 1)
                dve.wait_ge(counted, 1)

                def pooled_weights(n, par, use):
                    dve.wait_ge(o_psum, free(n))
                    for k in range(2):
                        ins = nc.vector.scalar_tensor_tensor(Wp[par][:, k, :], Wqv[:, 3, :], hcb[:, bass.ds(n * 2 + k, 1)],
                                                             Wqv[:, 0, :], ALU.mult, ALU.add)
                    ins.then_inc(wp_ready, 1)

                def product(n, par, use):
                    dve.wait_ge(q_psum, done(n))
                    dve.wait_ge(st_ready, done(n))
                    nc.vector.tensor_tensor(prod[par], xT_s[par][:], Q[par][:], ALU.mult).then_inc(prod_ready, 1)

                def add_attention(n, par, use):
                    ln_link.start(n * LA)
                    dve.wait_ge(o_psum, done(n))
                    ln_link(nc.vector.scalar_tensor_tensor(xq(n), tiles(O[par][:]), tg[:, 0:1], xq(n), ALU.mult, ALU.add))
                    dve.sem_inc(o_read, 1)
                    row_scales(dve, ln_link, xq(n), par, r0_scales)

                def split_low(n, par, use):
                    hi, lo = (u16[:, bass.ds(n * TQ, TQ), h * D:(h + 1) * D] for h in range(2))
                    dve.wait_ge(hi_ready, done(n))
                    nc.vector.scalar_tensor_tensor(lo, ln_out[par][:], SU, hi, ALU.mult, ALU.subtract).then_inc(u16_ready, 1)
                    nc.vector.scalar_tensor_tensor(xq(n), ln_out[par][:], tg[:, 2:3], xq(n), ALU.mult, ALU.add
                                                   ).then_inc(x_done, 1)

                def choose(n, par, use):
                    top_link.start(n * LB)
                    dve.wait_ge(lg_psum, done(n))
                    hold(dve, "dve")
                    for j in range(TQ):
                        ins = nc.vector.max(v8[par][:, j, :], LG[par][:, j * 16:j * 16 + E0])
                    top_link(ins)
                    hold(dve, "dve")
                    for j in range(TQ):
                        ins = nc.vector.max_index(i8[par][:, j, :], v8[par][:, j, :], LG[par][:, j * 16:j * 16 + E0])
                    top_link(ins)
                    nc.vector.tensor_tensor(el[par][:], column(LG[par], 0), v8[par][:, :, 0:1].broadcast_to([P, TQ, E0]),
                                            ALU.subtract).then_inc(d_ready, 1)
                    top_link(nc.vector.tensor_copy(idxf[par][:].rearrange("p (t k) -> p t k", k=K0), i8[par][:, :, 0:K0]))
                    top_link(nc.vector.tensor_tensor(
                        oh[par][:], idxf[par][:].rearrange("p (c o) -> p c o", o=1).broadcast_to([P, NK, E0]),
                        cst[:, C_IOTA:C_IOTA + E0].rearrange("p (o e) -> p o e", o=1).broadcast_to([P, NK, E0]),
                        ALU.is_equal))
                    top_link(nc.vector.tensor_reduce(Msum[par][:], oh[par][:].rearrange("p (t k) e -> p t e k", k=K0), AX, ALU.add))
                    nc.vector.tensor_copy(M16[par][:], Msum[par][:]).then_inc(m_ready, 1)
                    top_link(nc.vector.tensor_reduce(ctmp[:], Msum[par][:].rearrange("p t e -> p e t"), AX, ALU.add))
                    dve.wait_ge(r_psum, n + CREDIT)
                    nc.vector.tensor_tensor(S16[1 - par][:], S16[par][:], ctmp[:], ALU.add).then_inc(counted, 1)
                    assert top_link.k == LB

                def places_and_gates(n, par, use):
                    idx_link.start(n * LD)
                    oh4 = oh[par][:].rearrange("p (t k) e -> p t k e", k=K0)
                    ohx4 = ohx[:].rearrange("p (t k) e -> p t k e", k=K0)

                    def by_choice(ap):
                        return ap.rearrange("p t (o e) -> p t o e", o=1).broadcast_to([P, TQ, K0, E0])

                    dve.wait_ge(r_psum, done(n))
                    idx_link(nc.vector.tensor_tensor(ohx4, oh4, by_choice(column(LG[par], 64)), ALU.mult))
                    with nc.allow_low_precision("whole numbers below 2^17: exact"):
                        idx_link(nc.vector.tensor_reduce(pos[:, bass.ds(n * NK, NK)], ohx[:], AX, ALU.add))
                    dve.sem_inc(idx_ready, 1)
                    dve.wait_ge(e_ready, done(n))
                    idx_link(nc.vector.tensor_reduce(den[par][:], el[par][:], AX, ALU.add))
                    idx_link(nc.vector.reciprocal(den[par][:], den[par][:]))
                    idx_link(nc.vector.tensor_tensor(el[par][:], el[par][:], spread(den[par][:], E0), ALU.mult))
                    dve.wait_ge(gt_psum, free(n))
                    nc.vector.tensor_tensor(Gs[par][:, :, 0:E0], el[par][:], Msum[par][:], ALU.mult).then_inc(g_ready, 1)
                    idx_link(nc.vector.tensor_tensor(ohx4, oh4, by_choice(el[par][:]), ALU.mult))
                    nc.vector.tensor_reduce(gk[:, bass.ds(n * NK, NK)], ohx[:], AX, ALU.add).then_inc(gk_done, 1)
                    assert idx_link.k == LD

                pipelined(dve, (3, choose), (1, add_attention), (0, pooled_weights), (0, product), (3, places_and_gates), (1, split_low))

            @block.tensor
            def _(pe):
                mm = nc.tensor.matmul
                for s in (q_psum, o_psum, ut_psum, lg_psum, r_psum, gt_psum):
                    pe.sem_inc(s, CREDIT)

                def ranks(n, par, use):
                    pe.wait_ge(m_ready, done(n))
                    pe.wait_ge(counted, n + 1)
                    for j in range(TQ):
                        o = LG[par][:, 64 + j * 16:64 + j * 16 + E0]
                        mm(o, tri16[:], M16[par][:, j, :], start=True, stop=False)
                        for k in range(j):
                            mm(o, ones16[:], M16[par][:, k, :], start=False, stop=False)
                        ins = mm(o, ones16[:], S16[par][:], start=False, stop=True)
                    ins.then_inc(r_psum, 1)

                def attended(n, par, use):
                    pe.wait_ge(ctx_ld[par], use * 16 + 16)
                    pe.wait_ge(st_ready, done(n))
                    pe.wait_ge(prod_ready, free(n))
                    for k in range(2):
                        ks = slice(k * SEQ, (k + 1) * SEQ)
                        ins = mm(Q[par][:, ks], ctx_s[par][:, k, :], AT_s[par][:, ks], start=True, stop=True)
                    ins.then_inc(q_psum, 1)

                def transpose_rows(n, par, use):
                    pe.wait_ge(u16_ready, done(n))
                    pe.wait_ge(ut_saved, done(n - 1))
                    t16 = TU[:].bitcast(F16)
                    for j in range(TQ):
                        for h in range(2):
                            ins = nc.tensor.transpose(
                                t16[:, h * QTOK + j * P:h * QTOK + (j + 1) * P],
                                u16[:, bass.ds(n * TQ + j, 1), h * D:(h + 1) * D].rearrange("p o d -> p (o d)"), ident16[:])
                    ins.then_inc(ut_psum, 1)

                def attention_output(n, par, use):
                    pe.wait_ge(wp_ready, done(n))
                    pe.wait_ge(o_read, free(n))
                    pe.wait_ge(prod_ready, done(n))
                    for j in range(TQ):
                        o = O[par][:, j * D:(j + 1) * D]
                        js = slice(j * P, (j + 1) * P)
                        mm(o, xT_s[par][:, js], Wp[par][:, j // TPB, :], start=True, stop=False)
                        mm(o, prod[par][:, js], Wqv[:, 2, :], start=False, stop=False)
                        ins = mm(o, AT_s[par][:, js], HW1[:, bass.ds(n * 2 + j // TPB, 1), :].rearrange("p o d -> p (o d)"),
                                 start=False, stop=True)
                    ins.then_inc(o_psum, 1)

                def logits(n, par, use):
                    pe.wait_ge(ut_saved, done(n))
                    pe.wait_ge(idx_ready, free(n))
                    for j in range(TQ):
                        o = LG[par][:, j * 16:j * 16 + E0]
                        uh, ul = (uT[:, h, bass.ds(n * QTOK + j * P, P)] for h in range(2))
                        mm(o, uh, gw16[:, 0, 0:E0], start=True, stop=False)
                        mm(o, uh, gw16[:, 1, 0:E0], start=False, stop=False)
                        mm(o, ul, gw16[:, 0, 0:E0], start=False, stop=False)
                        ins = mm(o, ones[0:1, :], rows[0:1, 0, 0:E0], start=False, stop=True)
                    ins.then_inc(lg_psum, 1)

                def transpose_gates(n, par, use):
                    pe.wait_ge(g_ready, done(n))
                    pe.wait_ge(gt_saved, done(n - 1))
                    hold(pe, "pe")
                    for j in range(TQ):
                        ins = nc.tensor.transpose(GB[0:E0 + 1, j * P:(j + 1) * P], Gs[par][:, j, :], ident)
                    ins.then_inc(gt_psum, 1)

                pipelined(pe, (0, attended), (3, ranks), (2, logits), (0, attention_output), (3, transpose_gates),
                          (1, transpose_rows))

            t_pe, t_dve, t_pad = sem("t_pe"), sem("t_dve"), sem("t_pad")
            TBK, T_LINKS = banks[5], 17

            def table_counts(pe):
                pe.wait_ge(counted, NQ + 1)
                pe.wait_ge(idx_ready, done(NQ - 2))
                nc.tensor.matmul(TBK[:, 0:E0], ones16[:], S16[0][:], start=True, stop=True).then_inc(t_pe, 1)

            def table_row(pe):
                pe.wait_ge(t_dve, 16)
                for k in range(2):
                    ins = nc.tensor.matmul(TBK[0:1, (k + 1) * P:(k + 2) * P], tabc[:, k:k + 1], ident, start=True, stop=True)
                ins.then_inc(t_pe, 1)

            def table_blocks(dve, link):
                cnt, tiles, cum, before, tmp = (tw[:, k, :] for k in range(5))
                part = cst[:, C_PART:C_PART + 1]
                dve.wait_ge(t_pe, 1)
                dve.wait_ge(gk_done, NQ)
                dve.wait_ge(idx_ready, done(NQ - 1))
                nc.vector.tensor_scalar(gk[:], gk[:], tgs[:, 0:1], None, ALU.mult)
                link(nc.vector.tensor_copy(tmp, TBK[:, 0:E0]))
                link(nc.vector.tensor_tensor(cnt, tmp, cst[:, C_BASE:C_BASE + E0], ALU.subtract))
                link(nc.vector.tensor_copy(crow[:], tw[0:1, 4, :]))
                link(nc.vector.tensor_scalar(ti[:, 0, :], cnt, float(BLK - 1), None, ALU.add))
                link(nc.vector.tensor_scalar(ti[:, 1, :], ti[:, 0, :], BLK.bit_length() - 1, None, ALU.logical_shift_right))
                link(nc.vector.tensor_copy(tiles, ti[:, 1, :]))
                link(nc.vector.tensor_tensor(tcum[:], cst[:, C_LE:C_LE + E0 * E0].rearrange("p (e f) -> p e f", f=E0),
                                             tw[:, 1:2, :].broadcast_to([P, E0, E0]), ALU.mult))
                link(nc.vector.tensor_reduce(cum, tcum[:], AX, ALU.add))
                link(nc.vector.tensor_scalar(before, cum, part, None, ALU.is_le))
                link(nc.vector.tensor_reduce(tw[:, 5, 0:1], before, AX, ALU.add))
                link(nc.vector.tensor_tensor(tmp, before, tiles, ALU.mult))
                link(nc.vector.tensor_reduce(tw[:, 5, 1:2], tmp, AX, ALU.add))
                link(nc.vector.tensor_tensor(tw[:, 5, 2:3], part, tw[:, 5, 1:2], ALU.subtract))
                link(nc.vector.tensor_scalar(tw[:, 5, 3:4], tw[:, 5, 2:3], float(BLK), None, ALU.mult))
                nc.vector.tensor_scalar(tabc[:, 0:1], tw[:, 5, 0:1], float(E0 - 1), None, ALU.min)
                link(nc.vector.scalar_tensor_tensor(tw[:, 5, 4:5], tw[:, 5, 0:1], float(REGION), tw[:, 5, 3:4],
                                                    ALU.mult, ALU.add))
                link(nc.vector.tensor_scalar(tabc[:, 1:2], tw[:, 5, 4:5], float(E0 * REGION), None, ALU.min))

            def table_copy(dve, link):
                dve.wait_ge(t_pe, 2)
                link(nc.vector.tensor_copy(tab[:], TBK[0:1, P:3 * P].rearrange("p (k i) -> p k i", k=2)))

            @block.sync
            def _(sp):
                sp.wait_ge(t_dve, 3)
                for e in range(E0):
                    r = sp.value_load(crow[0:1, e:e + 1], min_val=0, max_val=ROWS - BLK)
                    sp.dma_start(sorted_rows[bass.ds(r, BLK), :].rearrange("(t q) d -> q t d", q=P),
                                 zeros[:].rearrange("p (t d) -> p t d", t=2)).then_inc(t_pad, 16)
                sp.wait_ge(t_pad, 16 * E0)
                for par in range(2):
                    sp.wait_ge(scat[par], 16 * NK * (NQ // 2) + 16)

            @block.tensor
            def _(pe):
                for s in (s_h, s_y, s_t):
                    pe.sem_inc(s, CREDIT)
                table_counts(pe)
                for c in range(4):
                    shared_hidden(0, c, pe)
                pe.wait_ge(o_read, done(NQ - 1))
                pe.wait_ge(gt_saved, done(NQ - 1))
                shared_outputs(0, 0, pe, mix, first=True)
                table_row(pe)
                pe.wait_ge(t_dve, T_LINKS)
                with pe.Fori(0, EARLY // 2 - 1) as i:
                    shared_outputs(i * 2 + 1, 1, pe, mix)
                    shared_outputs(i * 2 + 2, 0, pe, mix)
                shared_outputs(EARLY - 1, 1, pe, mix, last=True)
                shared_back(EARLY - 1, 1, pe, mix)

            @block.scalar
            def _(act):
                act.sem_inc(s_hf, CREDIT)
                act.sem_inc(s_yc, CREDIT)
                act.wait_ge(o_psum, done(NQ - 1))
                for g in range(2):
                    for c in range(4):
                        shared_gelu(g, c, act, mix)
                with act.Fori(0, EARLY // 2 - 1) as i:
                    for par in range(2):
                        shared_gelu(i * 2 + (2 + par), 0, act, mix)
                        shared_copy(i * 2 + par, par, act, mix)
                        for c in range(1, 4):
                            shared_gelu(i * 2 + (2 + par), c, act, mix)
                shared_copy(EARLY - 2, 0, act, mix)
                shared_copy(EARLY - 1, 1, act, mix)

            @block.vector
            def _(dve):
                dve.sem_inc(s_lo, CREDIT)
                dve.sem_inc(s_x, CREDIT)
                link, t_link = Chain(dve, s_lk), Chain(dve, t_dve)
                dve.wait_ge(x_done, NQ)
                dve.wait_ge(st_ready, done(NQ - 1))
                shared_split(0, 0, dve, link, mix)
                table_blocks(dve, t_link)
                shared_split(1, 1, dve, link, mix)
                table_copy(dve, t_link)
                assert t_link.k == T_LINKS
                with dve.Fori(0, EARLY // 2 - 1) as i:
                    for par in range(2):
                        shared_split(i * 2 + (2 + par), par, dve, link, mix)
                        shared_add(i * 2 + par, par, dve)
                shared_add(EARLY - 2, 0, dve)
                shared_add(EARLY - 1, 1, dve)

        def table_places(dve, link):
            nc.vector.tensor_scalar(tw[:, 6, 0:E0 - 1], tw[:, 1, 0:E0 - 1], float(BLK), -float(REGION), ALU.mult, ALU.add)
            link(nc.vector.tensor_tensor(
                moved, pos[:].rearrange("p (c o) -> p c o", o=1).broadcast_to([P, NT * K0, E0 - 1]),
                cst[:, C_BASE + 1:C_BASE + E0].rearrange("p (o e) -> p o e", o=1).broadcast_to([P, NT * K0, E0 - 1]),
                ALU.is_ge))
            link(nc.vector.tensor_tensor(moved, moved, tw[:, 6:7, 0:E0 - 1].broadcast_to([P, NT * K0, E0 - 1]), ALU.mult))
            link(nc.vector.tensor_reduce(shift[:], moved, AX, ALU.add))
            link(nc.vector.tensor_tensor(places[:], pos[:], shift[:], ALU.add))

        h16 = hcT[:].bitcast(F16)
        hf = [AT[:, 512 * k:512 * k + 512] for k in range(2)]
        xp = [h16[:, 4096 + 512 * k:4608 + 512 * k].rearrange("p (t d) -> p t d", t=2) for k in range(4)]
        DEEP, WDEEP = 4, 8
        we = [hcf[:, WEW * k:WEW * (k + 1)] for k in range(WDEEP - 1)]
        we.append(AT[:, 2560:2560 + WEW])
        we16, web = [w.bitcast(F16) for w in we], [w[:, 2 * F0:2 * F0 + 2] for w in we]
        xpT = [h16[:, 1024 + 512 * k:1536 + 512 * k].rearrange("p (h t) -> p h t", h=2) for k in range(2)]
        hs = [h16[:, 2048 + 1024 * k:3072 + 1024 * k].rearrange("p (h t) -> p h t", h=2) for k in range(2)]
        ys = [AT[:, 1024 + 256 * k:1280 + 256 * k].rearrange("p (t d) -> p t d", t=2) for k in range(DEEP)]
        with nc.Block() as block:
            x_tr, x_cp, x_h, x_hf, x_lo, x_y, x_yc, x_lk = (sem("ex_" + s) for s in (
                "t_psum", "t_copied", "h_psum", "gelu", "split", "y_psum", "y_copied", "chain"))
            x_ld = [sem(f"ex_rows_loaded{i}") for i in range(4)]
            w_ld = [sem(f"ex_weights_loaded{i}") for i in range(WDEEP)]
            x_st = [sem(f"ex_stored{i}") for i in range(DEEP)]
            TB, HB, YB = banks[0:2], banks[2:4], banks[4:6]
            WMAIN = BLOCKS // WDEEP
            assert BLOCKS % 2 == 0 and BLOCKS - WMAIN * WDEEP >= 3

            @block.sync
            def _(sp):
                def load_rows(b, k):
                    row = sp.value_load(tab[0:1, 1, bass.ds(b, 1)], min_val=0, max_val=ROWS - BLK)
                    sp.dma_start(xp[k], sorted_rows[bass.ds(row, BLK), :].rearrange("(t q) d -> q t d", q=P)
                                 ).then_inc(x_ld[k], 16)

                def next_rows(b, k):
                    sp.wait_ge(x_tr, done(b))
                    hold(sp, "sp")
                    load_rows(b + DEEP, k)

                for b in range(DEEP):
                    load_rows(b, b)
                rounds = (BLOCKS - DEEP) // DEEP
                with sp.Fori(0, rounds) as i:
                    for k in range(DEEP):
                        next_rows(i * DEEP + k, k)
                for b in range(rounds * DEEP, BLOCKS - DEEP):
                    next_rows(b, b % DEEP)

            @block.gpsimd
            def _(pool):
                def load_weights(b, k):
                    e = pool.value_load(tab[0:1, 0, bass.ds(b, 1)], min_val=0, max_val=E0 - 1)
                    pool.dma_start(we[k], WE[:, bass.ds(e, 1), :].rearrange("p o f -> p (o f)")).then_inc(w_ld[k], 16)

                def next_weights(b, k):
                    pool.wait_ge(x_y, done(b))
                    hold(pool, "pool")
                    load_weights(b + WDEEP, k)

                for b in range(WDEEP):
                    load_weights(b, b)
                rounds = (BLOCKS - WDEEP) // WDEEP
                with pool.Fori(0, rounds) as i:
                    for k in range(WDEEP):
                        next_weights(i * WDEEP + k, k)
                for b in range(rounds * WDEEP, BLOCKS - WDEEP):
                    next_weights(b, b % WDEEP)

            @block.tensor
            def _(pe):
                mm = nc.tensor.matmul
                for s in (x_tr, x_h, x_y):
                    pe.sem_inc(s, CREDIT)

                def transposes(b, k, use):
                    par = k % 2
                    pe.wait_ge(x_ld[k % DEEP], use)
                    pe.wait_ge(x_cp, free(b))
                    t16 = TB[par][:, 0:SEQ].bitcast(F16)
                    for j in range(2):
                        for h in range(2):
                            ins = nc.tensor.transpose(t16[:, h * SEQ + j * P:h * SEQ + (j + 1) * P],
                                                      xp[k % DEEP][:, j, h * D:(h + 1) * D], ident16[:])
                    ins.then_inc(x_tr, 1)

                def hidden(b, k, use):
                    par = k % 2
                    pe.wait_ge(w_ld[k], use)
                    pe.wait_ge(x_cp, done(b))
                    pe.wait_ge(x_hf, free(b))
                    xh, xl = (xpT[par][:, h, :] for h in range(2))
                    for c in range(2):
                        wh, wl = (we16[k][:, h * F0 + c * P:h * F0 + (c + 1) * P] for h in range(2))
                        o = HB[par][:, c * BLK:(c + 1) * BLK]
                        mm(o, wh, xh, start=True, stop=False)
                        mm(o, wh, xl, start=False, stop=False)
                        ins = mm(o, wl, xh, start=False, stop=True)
                    ins.then_inc(x_h, 1)

                def outputs(b, k):
                    par = k % 2
                    pe.wait_ge(x_lo, done(b))
                    pe.wait_ge(x_yc, free(b))
                    for j in range(2):
                        o = YB[par][:, j * D:(j + 1) * D]
                        for c in range(2):
                            hh, hl = (hs[par][:, h, c * BLK + j * P:c * BLK + (j + 1) * P] for h in range(2))
                            wh, wl = (we16[k][:, 2 * F0 + h * 2 * D + c * D:2 * F0 + h * 2 * D + (c + 1) * D] for h in range(2))
                            mm(o, hh, wh, start=(c == 0), stop=False)
                            mm(o, hh, wl, start=False, stop=False)
                            ins = mm(o, hl, wh, start=False, stop=(c == 1))
                    ins.then_inc(x_y, 1)

                def step(i, k, left=BLOCKS):
                    b = i * WDEEP + k
                    if left > 3:
                        transposes(b + 3, (k + 3) % WDEEP, i * 32 + ((k + 3) // DEEP) * 16 + 16)
                    if left > 2:
                        hidden(b + 2, (k + 2) % WDEEP, (i + (k + 2) // WDEEP) * 16 + 16)
                    outputs(b, k)

                transposes(0, 0, 16)
                transposes(1, 1, 16)
                hidden(0, 0, 16)
                transposes(2, 2, 16)
                hidden(1, 1, 16)
                with pe.Fori(0, WMAIN) as i:
                    for k in range(WDEEP):
                        step(i, k)
                for b in range(WMAIN * WDEEP, BLOCKS):
                    step(WMAIN, b % WDEEP, left=BLOCKS - b)

            @block.vector
            def _(dve):
                dve.sem_inc(x_cp, CREDIT)
                dve.sem_inc(x_lo, CREDIT)
                lnk = Chain(dve, x_lk)

                def copy_rows(b, par):
                    dve.wait_ge(x_tr, done(b))
                    dve.wait_ge(x_h, free(b))
                    nc.vector.tensor_copy(xpT[par], TB[par][:, 0:SEQ].bitcast(F16).rearrange("p (h t) -> p h t", h=2)
                                          ).then_inc(x_cp, 1)

                def split(b, par):
                    lnk.base, lnk.k = b, 0
                    dve.wait_ge(x_hf, done(b))
                    dve.wait_ge(x_y, free(b))
                    lnk(nc.vector.tensor_scalar(hs[par][:, 0, :], hf[par], SH, None, ALU.mult))
                    nc.vector.scalar_tensor_tensor(hs[par][:, 1, :], hf[par], SH, hs[par][:, 0, :],
                                                   ALU.mult, ALU.subtract).then_inc(x_lo, 1)

                for b in range(3):
                    copy_rows(b, b % 2)
                split(0, 0)
                with dve.Fori(0, BLOCKS // 2 - 2) as i:
                    for par in range(2):
                        split(i * 2 + 1 + par, 1 - par)
                        copy_rows(i * 2 + 3 + par, 1 - par)
                split(BLOCKS - 3, 1)
                copy_rows(BLOCKS - 1, 1)
                split(BLOCKS - 2, 0)
                split(BLOCKS - 1, 1)
                t_link = Chain(dve, t_dve)
                t_link.start(T_LINKS)
                table_places(dve, t_link)

            @block.scalar
            def _(act):
                act.sem_inc(x_hf, CREDIT)
                act.sem_inc(x_yc, CREDIT)

                def gelu(b, k):
                    par = k % 2
                    act.wait_ge(x_h, done(b))
                    act.wait_ge(x_lo, free(b))
                    for c in range(2):
                        s = slice(c * BLK, (c + 1) * BLK)
                        ins = nc.scalar.activation(hf[par][:, s], HB[par][:, s], ACT.Gelu, bias=web[k][:, c:c + 1], scale=UN1)
                    ins.then_inc(x_hf, 1)

                def copy_out(b, k, use):
                    act.wait_ge(x_y, done(b))
                    act.wait_ge(x_st[k % DEEP], use * 16 + 16)
                    nc.scalar.copy(ys[k % DEEP], YB[k % 2][:, 0:SEQ].rearrange("p (t d) -> p t d", t=2)).then_inc(x_yc, 1)

                def store(b, k):
                    act.wait_ge(x_yc, done(b))
                    act.dma_start(expert_rows[bass.ds(b * BLK, BLK), :].rearrange("(t q) d -> q t d", q=P),
                                  ys[k % DEEP]).then_inc(x_st[k % DEEP], 16)

                for k in range(DEEP):
                    act.sem_inc(x_st[k], 16)
                gelu(0, 0)
                gelu(1, 1)
                gelu(2, 2)
                with act.Fori(0, WMAIN) as i:
                    for k in range(WDEEP):
                        copy_out(i * WDEEP + k, k, i * 2 + k // DEEP)
                        gelu(i * WDEEP + (k + 3), (k + 3) % WDEEP)
                        store(i * WDEEP + k, k)
                for b in range(WMAIN * WDEEP, BLOCKS):
                    copy_out(b, b % WDEEP, b // DEEP)
                    if b + 3 < BLOCKS:
                        gelu(b + 3, (b + 3) % WDEEP)
                    store(b, b % WDEEP)
                for k in range(DEEP):
                    act.wait_ge(x_st[k], 16 * len(range(k, BLOCKS, DEEP)) + 16)

        Yg = [AT[:, 1024 + NK * D * k:1024 + NK * D * (k + 1)].rearrange("p (c d) -> p c d", d=D) for k in range(2)]
        mh = [Gs[k][:, :, 0:HEADS] for k in range(2)]
        pTs = AT_s
        idx1 = sb("idx1", [1, B * K1], I32)
        idx1f = sb("idx1f", [1, B * K1])
        diff = [tiles(AT[:, 256 * k:256 * k + 256]) for k in range(2)]
        prob = [tiles(AT[:, 512 + 256 * k:768 + 256 * k]) for k in range(2)]
        ln2 = [tiles(KmT[:, QTOK * k:QTOK * (k + 1)]) for k in range(2)]
        hf = [AT[:, 512 * k:512 * k + 512] for k in range(2)]
        hs = [KmT[:, 512 * k:512 * k + 512].bitcast(F16).rearrange("p (h t) -> p h t", h=2) for k in range(2)]
        MDEEP = 6
        wm = [hcT[:, K1 * MEW * k:K1 * MEW * (k + 1)].rearrange("p (k w) -> p k w", k=K1) for k in range(MDEEP)]
        wm16 = [w.rearrange("p k w -> p (k w)").bitcast(F16).rearrange("p (k w) -> p k w", k=K1) for w in wm]
        onehot = sb("onehot", [E1, B, K1])
        sel = sb("sel", [E1, B])
        selw = MT[0:E1, :].bitcast(F16)

        with nc.Block() as block:
            (scales_ready, v_ready, vT_psum, vT_ready, sc_psum, sc_ready, ex_ready, pr_ready, pT_psum, pT_ready, o_psum,
             x_ready, got_in, ln_chain, max_chain, sum_chain) = (sem("a1_" + s) for s in (
                "row_scales", "v_ready", "vT_psum", "vT_ready", "sc_psum", "sc_ready", "exp_ready", "prob_ready", "pT_psum",
                "pT_ready", "o_psum", "x_ready", "combined", "ln_chain", "max_chain", "sum_chain"))
            (mv_set, scale_chain, ln_ready, hi_ready, w_ready, wt_psum, wt_saved, s_psum, s_read, ln2_chain, top_chain) = (
                sem("r1_" + s) for s in ("mv_set", "scale_chain", "ln_ready", "hi_ready", "w_ready", "wT_psum", "wT_saved", "s_psum",
                                         "s_read", "ln_chain", "top_chain"))
            gat = [sem(f"a1_gathered{i}") for i in range(2)]
            T, S, A, O, TU, LG = banks[0], banks[1:3], banks[3], banks[4], banks[5], banks[6:8]
            LA, LC = K0 + MV_LINKS, 2

            @block.tensor
            def _(pe):
                for c in range(4):
                    shared_hidden(EARLY, c, pe)
                shared_outputs(EARLY, 0, pe, late_mix, first=True)
                shared_outputs(EARLY + 1, 1, pe, late_mix, last=True)
                shared_back(EARLY + 1, 1, pe, late_mix)

            @block.scalar
            def _(act):
                for g in range(EARLY, NQ):
                    for c in range(4):
                        shared_gelu(g, c, act, late_mix)
                shared_copy(EARLY, 0, act, late_mix)
                shared_copy(EARLY + 1, 1, act, late_mix)

            @block.vector
            def _(dve):
                link = Chain(dve, s_lk)
                for g in range(EARLY, NQ):
                    shared_split(g, g % 2, dve, link, late_mix)
                for g in range(EARLY, NQ):
                    shared_add(g, g % 2, dve)

            @block.gpsimd
            def _(pool):
                def gather(n):
                    if n >= 2:
                        pool.wait_ge(got_in, free(n))
                    hold(pool, "pool")
                    for c in range(NK):
                        nc.gpsimd.indirect_dma_start(
                            out=Yg[n % 2][:, c, :], out_offset=None, in_=expert_rows,
                            in_offset=bass.IndirectOffsetOnAxis(ap=places[:, n * NK + c:n * NK + c + 1], axis=0)
                        ).then_inc(gat[n % 2], 16)

                for n in range(NQ):
                    gather(n)

            @block.vector
            def _(dve):
                for s in (scales_ready, sc_ready, pr_ready, x_ready, got_in, w_ready, s_read):
                    dve.sem_inc(s, CREDIT)
                ln_link, max_link, sum_link = Chain(dve, ln_chain), Chain(dve, max_chain), Chain(dve, sum_chain)
                ln2_link, scale_link, top_link = Chain(dve, ln2_chain), Chain(dve, scale_chain), Chain(dve, top_chain)
                for par in range(2):
                    ins = nc.vector.memset(mv[par][:], 1.0)
                ins.then_inc(mv_set, 1)
                dve.wait_ge(mv_set, 1)

                def by_head(ap):
                    return ap.rearrange("p t (s h) -> p t h s", h=HEADS)

                def per_head(ap):
                    return ap.rearrange("p t (o h) -> p t o h", o=1).broadcast_to([P, TQ, L // HEADS, HEADS])

                def split_heads(ap):
                    return ap.rearrange("p t (s h) -> p t s h", h=HEADS)

                def combine(n, par, use):
                    ln_link.start(n * LA)
                    dve.wait_ge(gat[par], (use + 1) * 16 * NK)
                    for k in range(K0):
                        for j in range(TQ):
                            xj = X[:, bass.ds(n * TQ + j, 1), :].rearrange("p o d -> p (o d)")
                            ins = nc.vector.scalar_tensor_tensor(
                                xj, Yg[par][:, j * K0 + k, :], gk[:, bass.ds(n * NK + (j * K0 + k), 1)], xj, ALU.mult, ALU.add)
                        ln_link(ins)
                    dve.sem_inc(got_in, 1)
                    mean_variance(dve, ln_link, xq(n), par)

                def less_maximum(n, par, use):
                    max_link.start(n)
                    s = tiles(S[par][:, 0:TQ * L])
                    dve.wait_ge(sc_psum, done(n))
                    max_link(nc.vector.tensor_reduce(mh[par], by_head(s), AX, ALU.max))
                    nc.vector.tensor_tensor(split_heads(diff[par]), split_heads(s), per_head(mh[par]),
                                            ALU.subtract).then_inc(sc_ready, 1)

                def probabilities(n, par, use):
                    sum_link.start(n * LC)
                    dve.wait_ge(ex_ready, done(n))
                    sum_link(nc.vector.tensor_reduce(mh[par], by_head(diff[par]), AX, ALU.add))
                    sum_link(nc.vector.reciprocal(mh[par], mh[par]))
                    dve.wait_ge(pT_psum, free(n))
                    nc.vector.tensor_tensor(split_heads(prob[par]), split_heads(diff[par]), per_head(mh[par]),
                                            ALU.mult).then_inc(pr_ready, 1)

                def add_attention(n, par, use):
                    dve.wait_ge(o_psum, done(n))
                    nc.vector.scalar_tensor_tensor(xq(n), tiles(O[:]), tg[:, 1:2], xq(n), ALU.mult, ALU.add
                                                   ).then_inc(x_ready, 1)

                def second_norm(n, par, use):
                    ln2_link.start(n * MV_LINKS)
                    dve.wait_ge(x_ready, done(n))
                    mean_variance(dve, ln2_link, xq(n), par, second=1)

                def scales(n, par, use):
                    scale_link.start(n * (LN_LINKS - MV_LINKS))
                    dve.wait_ge(v_ready, free(n))
                    if not isinstance(n, int) or n >= 4:
                        dve.wait_ge(ln_ready, done(n - 4))
                    scales_of(dve, scale_link, par, scales_ready, norms=2)

                def split_low(n, par, use):
                    hi, lo = (u16[:, bass.ds(n * TQ, TQ), h * D:(h + 1) * D] for h in range(2))
                    dve.wait_ge(hi_ready, done(n))
                    nc.vector.scalar_tensor_tensor(lo, ln2[par][:], SU, hi, ALU.mult, ALU.subtract).then_inc(w_ready, 1)

                def choose(n, par, use):
                    top_link.start(2 * n)
                    dve.wait_ge(s_psum, done(n))
                    hold(dve, "dve")
                    for k in range(2):
                        ins = nc.vector.max(v8[par][0:1, k, :], LG[par][0:1, k * 16:k * 16 + E1])
                    top_link(ins)
                    hold(dve, "dve")
                    for k in range(2):
                        ins = nc.vector.max_index(i8[par][0:1, k, :], v8[par][0:1, k, :], LG[par][0:1, k * 16:k * 16 + E1])
                    top_link(ins)
                    for to in (idx1, idx1f):
                        ins = nc.vector.tensor_copy(to[0:1, bass.ds(n * 2 * K1, 2 * K1)].rearrange("p (b k) -> p b k", k=K1),
                                                    i8[par][0:1, 0:2, 0:K1])
                    ins.then_inc(s_read, 1)

                pipelined(dve, (2, probabilities), (0, combine), (4, choose), (2, add_attention), (2, second_norm),
                          (3, split_low), (1, less_maximum), (0, scales, NQ + 2))

            @block.scalar
            def _(act):
                for s in (v_ready, vT_ready, ex_ready, pT_ready, ln_ready, hi_ready, wt_saved):
                    act.sem_inc(s, CREDIT)

                def normalise(n, par, use):
                    act.wait_ge(scales_ready, done(n))
                    act.wait_ge(vT_psum, free(n))
                    normalise_rows(xq(n), ln_out[par], par).then_inc(v_ready, 1)

                def stage_tokens(n, par, use):
                    act.wait_ge(vT_psum, done(n))
                    act.wait_ge(sc_psum, free(n))
                    nc.scalar.copy(xT_s[par][:], T[:]).then_inc(vT_ready, 1)

                def exponentials(n, par, use):
                    act.wait_ge(sc_ready, done(n))
                    nc.scalar.activation(diff[par], diff[par], ACT.Exp).then_inc(ex_ready, 1)

                def stage_probabilities(n, par, use):
                    act.wait_ge(pT_psum, done(n))
                    act.wait_ge(o_psum, free(n))
                    nc.scalar.copy(pTs[par], A[0:L, :]).then_inc(pT_ready, 1)

                def split_high(n, par, use):
                    act.wait_ge(scales_ready, done(n + 2))
                    act.wait_ge(w_ready, free(n))
                    normalise_rows(xq(n), ln2[par], par, second=1).then_inc(ln_ready, 1)
                    act.wait_ge(ln_ready, done(n))
                    nc.scalar.activation(u16[:, bass.ds(n * TQ, TQ), 0:D], ln2[par][:], ACT.Copy, scale=SU
                                         ).then_inc(hi_ready, 1)

                def save_rows(n, par, use):
                    act.wait_ge(wt_psum, done(n))
                    nc.scalar.copy(uT[:, :, bass.ds(n * QTOK, QTOK)],
                                   TU[:].bitcast(F16).rearrange("p (h t) -> p h t", h=2)).then_inc(wt_saved, 1)

                pipelined(act, (0, normalise), (1, stage_probabilities), (0, stage_tokens), (2, split_high), (0, exponentials),
                          (2, save_rows))

            @block.tensor
            def _(pe):
                mm = nc.tensor.matmul
                for s in (vT_psum, sc_psum, pT_psum, o_psum, wt_psum, s_psum):
                    pe.sem_inc(s, CREDIT)

                def transpose_tokens(n, par, use):
                    pe.wait_ge(v_ready, done(n))
                    pe.wait_ge(vT_ready, done(n - 1))
                    for j in range(TQ):
                        ins = nc.tensor.transpose(T[:, j * P:(j + 1) * P], ln_out[par][:, j, :], ident)
                    ins.then_inc(vT_psum, 1)

                def scores(n, par, use):
                    pe.wait_ge(vT_ready, done(n))
                    pe.wait_ge(sc_ready, free(n))
                    for j in range(TQ):
                        keys = bass.ds((n * 2 + j // TPB) * L, L)
                        o = S[par][:, j * L:(j + 1) * L]
                        mm(o, xT_s[par][:, j * P:(j + 1) * P], QK[:, keys], start=True, stop=False)
                        ins = mm(o, ones[0:1, :], srow[0:1, 1, keys], start=False, stop=True)
                    ins.then_inc(sc_psum, 1)

                def transpose_probabilities(n, par, use):
                    pe.wait_ge(pr_ready, done(n))
                    pe.wait_ge(pT_ready, done(n - 1))
                    hold(pe, "pe")
                    for j in range(TQ):
                        ins = nc.tensor.transpose(A[0:L, j * P:(j + 1) * P], prob[par][:, j, :], ident)
                    ins.then_inc(pT_psum, 1)

                def attention_output(n, par, use):
                    pe.wait_ge(pT_ready, done(n))
                    pe.wait_ge(x_ready, done(n - 1))
                    for j in range(TQ):
                        ins = mm(O[:, j * D:(j + 1) * D], pTs[par][:, j * P:(j + 1) * P],
                                 VO[:, bass.ds(n * 2 + j // TPB, 1), :].rearrange("p o d -> p (o d)"), start=True, stop=True)
                    ins.then_inc(o_psum, 1)

                def transpose_rows(n, par, use):
                    pe.wait_ge(w_ready, done(n))
                    pe.wait_ge(wt_saved, done(n - 1))
                    t16 = TU[:].bitcast(F16)
                    for j in range(TQ):
                        for h in range(2):
                            ins = nc.tensor.transpose(
                                t16[:, h * QTOK + j * P:h * QTOK + (j + 1) * P],
                                u16[:, bass.ds(n * TQ + j, 1), h * D:(h + 1) * D].rearrange("p o d -> p (o d)"), ident16[:])
                    ins.then_inc(wt_psum, 1)

                def router_scores(n, par, use):
                    pe.wait_ge(wt_saved, done(n))
                    pe.wait_ge(s_read, free(n))
                    for k in range(2):
                        o = LG[par][:, k * 16:k * 16 + E1]
                        uh, ul = (uT[:, h, bass.ds(n * QTOK + k * SEQ, P)] for h in range(2))
                        mm(o, uh, wr16[:, 0, :], start=True, stop=False)
                        mm(o, uh, wr16[:, 1, :], start=False, stop=False)
                        mm(o, ul, wr16[:, 0, :], start=False, stop=False)
                        ins = mm(o, ones[0:1, :], rows[0:1, 1, 0:E1], start=False, stop=True)
                    ins.then_inc(s_psum, 1)

                pipelined(pe, (1, transpose_probabilities), (0, transpose_tokens), (1, attention_output), (0, scores),
                          (2, transpose_rows), (2, router_scores))

            m_h, m_hf, m_lo, m_y, m_x, m_lk, m_sel, m_selp = (sem("m1_" + s) for s in (
                "h_psum", "gelu", "split", "y_psum", "x", "chain", "chosen", "chosen_psum"))
            m_ld = [sem(f"m1_weights_loaded{i}") for i in range(MDEEP)]
            m_st = sem("m1_stored")
            HB, YB = banks[0:2], banks[2:4]
            ROUNDS = 2

            @block.sync
            def _(sp):
                def load_weights(n, k):
                    sp.wait_ge(s_read, done(n // 2))
                    for j in range(K1):
                        e = sp.value_load(idx1[0:1, bass.ds(n * K1 + j, 1)], min_val=0, max_val=E1 - 1)
                        sp.dma_start(wm[k][:, j, :], ME[:, bass.ds(e, 1), :].rearrange("p o w -> p (o w)")).then_inc(m_ld[k], 16)

                for n in range(B):
                    if n >= MDEEP:
                        sp.wait_ge(m_y, done(n - MDEEP))
                    load_weights(n, n % MDEEP)

            @block.gpsimd
            def _(pool):
                out_v = out.rearrange("b (t p) d -> p (b t) d", p=P)
                with pool.Fori(0, B) as n:
                    pool.wait_ge(m_x, done(n))
                    pool.dma_start(out_v[:, bass.ds(n * TPB, TPB), :], xt(n)).then_inc(m_st, 16)
                pool.wait_ge(m_st, 16 * B)

            @block.tensor
            def _(pe):
                mm = nc.tensor.matmul
                for s in (m_h, m_y):
                    pe.sem_inc(s, CREDIT)

                def hidden(n, k, use):
                    par = k % 2
                    pe.wait_ge(m_ld[k], use)
                    pe.wait_ge(m_hf, free(n))
                    uh, ul = (uT[:, h, bass.ds(n * SEQ, SEQ)] for h in range(2))
                    for j in range(K1):
                        wh, wl = (wm16[k][:, j, h * D:(h + 1) * D] for h in range(2))
                        o = HB[par][:, j * SEQ:(j + 1) * SEQ]
                        mm(o, wh, uh, start=True, stop=False)
                        mm(o, wh, ul, start=False, stop=False)
                        ins = mm(o, wl, uh, start=False, stop=True)
                    ins.then_inc(m_h, 1)

                def outputs(n, k):
                    par = k % 2
                    pe.wait_ge(m_lo, done(n))
                    pe.wait_ge(m_x, free(n))
                    for t in range(TPB):
                        o = YB[par][:, t * D:(t + 1) * D]
                        chosen = selw[:, bass.ds(n * P, P)]
                        for h in range(2):
                            mm(o, chosen, b2m16[:, h, :], start=(h == 0), stop=False)
                        for j in range(K1):
                            hh, hl = (hs[par][:, h, j * SEQ + t * P:j * SEQ + (t + 1) * P] for h in range(2))
                            wh, wl = (wm16[k][:, j, (2 + h) * D:(3 + h) * D] for h in range(2))
                            mm(o, hh, wh, start=False, stop=False)
                            mm(o, hh, wl, start=False, stop=False)
                            ins = mm(o, hl, wh, start=False, stop=(j == K1 - 1))
                    ins.then_inc(m_y, 1)

                pe.wait_ge(s_read, done(NQ - 1))
                pe.wait_ge(x_ready, done(NQ - 1))
                pe.wait_ge(sc_ready, done(NQ - 1))
                mm(banks[4][0:E1, 0:B * K1], ones[0:1, 0:E1], idx1f[:], start=True, stop=True).then_inc(m_selp, 1)
                hidden(0, 0, 32)
                hidden(1, 1, 32)
                pe.wait_ge(m_sel, 3)
                with pe.Fori(0, ROUNDS) as i:
                    for k in range(MDEEP):
                        hidden(i * MDEEP + (k + 2), (k + 2) % MDEEP, (i + (k + 2) // MDEEP) * 32 + 32)
                        outputs(i * MDEEP + k, k)
                for n in range(ROUNDS * MDEEP, B):
                    if n + 2 < B:
                        hidden(n + 2, (n + 2) % MDEEP, (n + 2) // MDEEP * 32 + 32)
                    outputs(n, n % MDEEP)

            @block.scalar
            def _(act):
                act.sem_inc(m_hf, CREDIT)

                def gelu(n, k):
                    par = k % 2
                    act.wait_ge(m_h, done(n))
                    act.wait_ge(m_lo, free(n))
                    for j in range(K1):
                        js = slice(j * SEQ, (j + 1) * SEQ)
                        ins = nc.scalar.activation(hf[par][:, js], HB[par][:, js], ACT.Gelu,
                                                   bias=wm[k][:, j, 2 * D:2 * D + 1], scale=UN1)
                    ins.then_inc(m_hf, 1)

                with act.Fori(0, ROUNDS) as i:
                    for k in range(MDEEP):
                        gelu(i * MDEEP + k, k)
                for n in range(ROUNDS * MDEEP, B):
                    gelu(n, n % MDEEP)

            @block.vector
            def _(dve):
                for s in (m_lo, m_x):
                    dve.sem_inc(s, CREDIT)
                lnk, sel_link = Chain(dve, m_lk), Chain(dve, m_sel)

                def split(n, par):
                    lnk.start(n)
                    dve.wait_ge(m_hf, done(n))
                    dve.wait_ge(m_y, free(n))
                    lnk(nc.vector.tensor_scalar(hs[par][:, 0, :], hf[par], SH, None, ALU.mult))
                    nc.vector.scalar_tensor_tensor(hs[par][:, 1, :], hf[par], SH, hs[par][:, 0, :],
                                                   ALU.mult, ALU.subtract).then_inc(m_lo, 1)

                def add(n, par):
                    dve.wait_ge(m_y, done(n))
                    nc.vector.scalar_tensor_tensor(xt(n), YB[par][:, 0:SEQ].rearrange("p (t d) -> p t d", t=2),
                                                   tgs[:, 1:2], xt(n), ALU.mult, ALU.add).then_inc(m_x, 1)

                dve.wait_ge(m_selp, 1)
                sel_link(nc.vector.tensor_scalar(onehot[:].rearrange("p b k -> p (b k)"), banks[4][0:E1, 0:B * K1],
                                                 cst[0:E1, C_PART:C_PART + 1], SH, ALU.is_equal, ALU.mult))
                sel_link(nc.vector.tensor_reduce(sel[:], onehot[:], AX, ALU.add))
                sel_link(nc.vector.tensor_copy(selw.rearrange("p (b q) -> p b q", q=P),
                                               sel[:].rearrange("p (b o) -> p b o", o=1).broadcast_to([E1, B, P])))
                split(0, 0)
                with dve.Fori(0, B // 2 - 1) as i:
                    for par in range(2):
                        split(i * 2 + 1 + par, 1 - par)
                        add(i * 2 + par, par)
                split(B - 1, 1)
                add(B - 2, 0)
                add(B - 1, 1)


_INS = ['x', 'ctx_1024', 'g_xattn', 'g_ffn', 'L0_xattn_w_sim', 'L0_xattn_b_sim', 'L0_xattn_W_qv', 'L0_xattn_b_qv',
        'L0_ffn_sW1', 'L0_ffn_sb1', 'L0_ffn_sW2', 'L0_ffn_sb2', 'L0_ffn_rW1', 'L0_ffn_rb1', 'L0_ffn_rW2',
        'L0_ffn_rb2', 'L0_ffn_gW', 'L0_ffn_gb', 'L1_xattn_Wq', 'L1_xattn_bq', 'L1_xattn_Wk', 'L1_xattn_bk',
        'L1_xattn_Wv', 'L1_xattn_bv', 'L1_xattn_Wo', 'L1_xattn_bo', 'L1_ffn_Wr', 'L1_ffn_br', 'L1_ffn_W1',
        'L1_ffn_b1', 'L1_ffn_W2', 'L1_ffn_b2']


def constants():
    import numpy as np
    c = np.zeros((P, NCONST), np.float32)
    c[:, C_ID:C_ID + P] = np.eye(P)
    c[:, C_TRI:C_TRI + P] = np.triu(np.ones((P, P)), 1)
    c[:, C_MASK:C_MASK + L] = np.arange(P)[:, None] // HD == np.arange(L)[None, :] % HEADS
    c[:, C_IOTA:C_IOTA + 6 * E0] = np.tile(np.arange(E0), 6)
    c[:, C_BASE:C_BASE + E0] = np.arange(E0) * REGION
    c[:, C_LE:C_LE + E0 * E0] = np.tril(np.ones((E0, E0))).reshape(-1)
    c[:, C_PART] = np.arange(P)
    return c


def kernel(**inputs):
    import numpy as np
    import concourse.bacc as bacc
    from concourse.bass_utils import run_bass_kernel_spmd as run

    nc = bacc.Bacc("TRN2", target_bir_lowering=False, num_devices=1)
    arrays, aps = {}, {}
    for name in _INS:
        arr = np.ascontiguousarray(inputs[name])
        arrays["in_" + name] = arr
        aps[name] = nc.dram_tensor("in_" + name, arr.shape, mybir.dt.from_np(arr.dtype), kind="ExternalInput").ap()
    arrays["in_const"] = constants()
    const = nc.dram_tensor("in_const", (P, NCONST), F32, kind="ExternalInput").ap()
    out = nc.dram_tensor("out", (B, SEQ, D), F32, kind="ExternalOutput").ap()
    build(nc, aps, const, out)
    return run(nc, [arrays], core_ids=[0]).results[0]["out"]
```
